# Optimizing a Trainium2 kernel written in Bass

```python
import numpy as np
import jax
import jax.numpy as jnp

def _softmax(x, axis=-1):
    return jax.nn.softmax(x, axis=axis)

def _gelu(x):
    return jax.nn.gelu(x, approximate=True)

def _silu(x):
    return jax.nn.silu(x)

def _sigmoid(x):
    return jax.nn.sigmoid(x)

def _layernorm(x, axis=-1, eps=1e-05):
    m = jnp.mean(x, axis=axis, keepdims=True)
    v = jnp.var(x, axis=axis, keepdims=True)
    return (x - m) / jnp.sqrt(v + eps)

def _scatter_add(tgt, idx, src, axis=0):
    return tgt.at[idx].add(src)

def _segment_sum(src, seg, n):
    return jax.ops.segment_sum(src, seg, n)
kernel_name = 'mk_adaln_d4_jaxref_r8_15a42c'

def setup_inputs(seed: int=0):
    np.random.seed(seed)
    _w = jnp.asarray

    def _L0_attn_setup():
        import jax, jax.numpy as jnp
        import numpy as np
        EPS = 1e-05
        CHUNK = 128

        def lightning_attn(q, k, v, ld, chunk=CHUNK):
            b, n, h, d = q.shape
            nc = n // chunk
            idx = jnp.arange(chunk)
            diff = idx[:, None] - idx[None, :]
            mask = diff >= 0
            D = jnp.exp(ld[:, None, None] * jnp.where(mask, diff, 0)) * mask
            q_decay = jnp.exp(ld[None, :] * (idx + 1)[:, None])
            k_decay = jnp.exp(ld[None, :] * (chunk - 1 - idx)[:, None])
            chunk_decay = jnp.exp(ld * chunk)
            qc = jnp.moveaxis(q.reshape(b, nc, chunk, h, d), 1, 0)
            kc = jnp.moveaxis(k.reshape(b, nc, chunk, h, d), 1, 0)
            vc = jnp.moveaxis(v.reshape(b, nc, chunk, h, d), 1, 0)

            def step(S, inp):
                qb, kb, vb = inp
                scores = jnp.einsum('bchd,bshd->bhcs', qb, kb) * D[None]
                o_intra = jnp.einsum('bhcs,bshd->bchd', scores, vb)
                o_inter = jnp.einsum('bchd,bhde->bche', qb, S) * q_decay[None, :, :, None]
                S_new = chunk_decay[None, :, None, None] * S + jnp.einsum('bshd,bshe->bhde', kb * k_decay[None, :, :, None], vb)
                return (S_new, o_intra + o_inter)
            S0 = jnp.zeros((b, h, d, d), dtype=q.dtype)
            S_final, oc = jax.lax.scan(step, S0, (qc, kc, vc))
            out = jnp.moveaxis(oc, 0, 1).reshape(b, n, h, d)
            return (out, S_final)

        def group_rmsnorm_fused_gate(o, gate, w, num_heads):
            b, n, d = o.shape
            hd = d // num_heads
            o = o * jax.nn.sigmoid(gate)
            og = o.reshape(b, n, num_heads, hd)
            og = og * jax.lax.rsqrt(jnp.mean(og * og, axis=-1, keepdims=True) + EPS)
            return og.reshape(b, n, d) * w
        key = jax.random.key(seed)
        ks = jax.random.split(key, 10)
        B, N, D, H = (2, 512, 256, 16)
        HD = D // H
        s = 1.0 / np.sqrt(D)
        x = jax.random.normal(ks[0], (B, N, D), dtype=jnp.float32)
        log_decay = -jax.random.uniform(ks[1], (H,), dtype=jnp.float32, minval=0.01, maxval=1.0)
        Wq = jax.random.normal(ks[2], (D, D), dtype=jnp.float32) * s
        Wk = jax.random.normal(ks[3], (D, D), dtype=jnp.float32) * s
        Wv = jax.random.normal(ks[4], (D, D), dtype=jnp.float32) * s
        Wo = jax.random.normal(ks[5], (D, D), dtype=jnp.float32) * s
        Wg1 = jax.random.normal(ks[6], (D, HD), dtype=jnp.float32) * s
        Wg2 = jax.random.normal(ks[7], (HD, D), dtype=jnp.float32) / np.sqrt(HD)
        norm_w = jnp.ones((D,), dtype=jnp.float32)
        return {'x': x, 'log_decay': log_decay, 'Wq': Wq, 'Wk': Wk, 'Wv': Wv, 'Wo': Wo, 'Wg1': Wg1, 'Wg2': Wg2, 'norm_w': norm_w}
    _L0_attn_in = _L0_attn_setup()

    def _L0_ffn_setup():
        import jax, jax.numpy as jnp
        import numpy as np
        HIDDEN = 256
        INTER = 688
        LUT_SIZE = 16

        def _ghost_linear(x, idx, lut):
            w = lut[idx]
            return jnp.einsum('bsh,oh->bso', x, w)
        key = jax.random.key(seed)
        k_x, k_lut, k_g, k_u, k_d = jax.random.split(key, 5)
        x = jax.random.normal(k_x, (2, 512, HIDDEN), dtype=jnp.float32)
        lut = jax.random.normal(k_lut, (LUT_SIZE,), dtype=jnp.float32) * 0.02
        gate_idx = jax.random.randint(k_g, (INTER, HIDDEN), 0, LUT_SIZE, dtype=jnp.int32)
        up_idx = jax.random.randint(k_u, (INTER, HIDDEN), 0, LUT_SIZE, dtype=jnp.int32)
        down_idx = jax.random.randint(k_d, (HIDDEN, INTER), 0, LUT_SIZE, dtype=jnp.int32)
        return {'x': x, 'lut': lut, 'gate_idx': gate_idx, 'up_idx': up_idx, 'down_idx': down_idx}
    _L0_ffn_in = _L0_ffn_setup()
    _L0_c = _w((lambda *s: np.random.randn(*s).astype(np.float32) * 0.05)(16, 256))
    _L0_wmod = _w((lambda *s: np.random.randn(*s).astype(np.float32) * 0.05)(256, 6 * 256) * 256 ** (-0.5))

    def _L1_attn_setup():
        import jax, jax.numpy as jnp
        import numpy as np
        import math
        E = 256
        H = 16
        HD = E // H // 2
        DEPTH = 12
        LAMBDA_INIT = 0.8 - 0.6 * math.exp(-0.3 * DEPTH)
        key = jax.random.key(seed)
        ks = jax.random.split(key, 9)
        s = 0.02
        return {'x': jax.random.normal(ks[0], (2, 256, E), jnp.float32), 'Wq': jax.random.normal(ks[1], (E, E), jnp.float32) * s, 'Wk': jax.random.normal(ks[2], (E, E), jnp.float32) * s, 'Wv': jax.random.normal(ks[3], (E, E), jnp.float32) * s, 'Wo': jax.random.normal(ks[4], (E, E), jnp.float32) * s, 'lq1': jax.random.normal(ks[5], (HD,), jnp.float32) * 0.1, 'lk1': jax.random.normal(ks[6], (HD,), jnp.float32) * 0.1, 'lq2': jax.random.normal(ks[7], (HD,), jnp.float32) * 0.1, 'lk2': jax.random.normal(ks[8], (HD,), jnp.float32) * 0.1}
    _L1_attn_in = _L1_attn_setup()

    def _L1_ffn_setup():
        import jax, jax.numpy as jnp
        import numpy as np
        B, S, D, E, TOPK = (4, 256, 256, 8, 2)
        key = jax.random.key(seed)
        k1, k2, k3 = jax.random.split(key, 3)
        x = jax.random.normal(k1, (B, S, D), dtype=jnp.float32)
        gate_w = jax.random.normal(k2, (E, D), dtype=jnp.float32) * 0.02
        expert_w = jax.random.normal(k3, (E, D, D), dtype=jnp.float32) / np.sqrt(D)
        expert_b = jnp.zeros((E, D), dtype=jnp.float32)
        return {'x': x, 'gate_w': gate_w, 'expert_w': expert_w, 'expert_b': expert_b}
    _L1_ffn_in = _L1_ffn_setup()
    _L1_c = _w((lambda *s: np.random.randn(*s).astype(np.float32) * 0.05)(16, 256))
    _L1_wmod = _w((lambda *s: np.random.randn(*s).astype(np.float32) * 0.05)(256, 6 * 256) * 256 ** (-0.5))

    def _L2_attn_setup():
        import jax, jax.numpy as jnp
        import numpy as np
        BATCH, SEQ, D_MODEL, D_STATE = (4, 512, 256, 128)
        key = jax.random.key(seed)
        kx, kb, kc = jax.random.split(key, 3)
        x = jax.random.normal(kx, (BATCH, SEQ, D_MODEL), dtype=jnp.float32)
        B = jax.random.normal(kb, (D_STATE, D_MODEL), dtype=jnp.float32) * 0.01
        C = jax.random.normal(kc, (D_MODEL, D_STATE), dtype=jnp.float32) * 0.01
        D = jnp.zeros((D_MODEL,), dtype=jnp.float32)
        return {'x': x, 'B': B, 'C': C, 'D': D}
    _L2_attn_in = _L2_attn_setup()

    def _L2_ffn_setup():
        import jax, jax.numpy as jnp
        import numpy as np
        NUM_EXPERTS = 8
        RANK = 16
        TOP_K = 2
        SCALING = 32.0 / RANK
        IN_F = 256
        OUT_F = 256
        key = jax.random.key(seed)
        k1, k2, k3, k4, k5 = jax.random.split(key, 5)
        B, T = (4, 256)
        x = jax.random.normal(k1, (B, T, IN_F), dtype=jnp.float32)
        bound_w = 1.0 / np.sqrt(IN_F)
        weight = jax.random.uniform(k2, (OUT_F, IN_F), jnp.float32, -bound_w, bound_w)
        lora_A = jax.random.uniform(k3, (NUM_EXPERTS, RANK, IN_F), jnp.float32, -bound_w, bound_w)
        lora_B = 0.02 * jax.random.normal(k4, (NUM_EXPERTS, OUT_F, RANK), dtype=jnp.float32)
        router_w = jax.random.uniform(k5, (NUM_EXPERTS, IN_F), jnp.float32, -bound_w, bound_w)
        return {'x': x, 'weight': weight, 'lora_A': lora_A, 'lora_B': lora_B, 'router_w': router_w}
    _L2_ffn_in = _L2_ffn_setup()
    _L2_c = _w((lambda *s: np.random.randn(*s).astype(np.float32) * 0.05)(16, 256))
    _L2_wmod = _w((lambda *s: np.random.randn(*s).astype(np.float32) * 0.05)(256, 6 * 256) * 256 ** (-0.5))

    def _L3_attn_setup():
        import jax, jax.numpy as jnp
        import numpy as np
        H = 16
        EPS_DEN = 1e-06

        def _decay_scan(x, decay, init):
            xT = jnp.moveaxis(x, 2, 0)

            def step(s, xt):
                s = decay * s + xt
                return (s, s)
            _, ys = jax.lax.scan(step, init, xT)
            return jnp.moveaxis(ys, 0, 2)

        def _phi(z):
            return jax.nn.elu(z) + 1.0

        def _reference_tuple_inner(x, w_qkv, w_out, decay_param):
            B, T, Hid = x.shape
            D = Hid // H
            qkv = x @ w_qkv
            q, k, v = jnp.split(qkv, 3, axis=-1)

            def to_bhtd(t):
                return t.reshape(B, T, H, D).transpose(0, 2, 1, 3)
            q = _phi(to_bhtd(q))
            k = _phi(to_bhtd(k))
            v = to_bhtd(v)
            decay = jax.nn.sigmoid(decay_param).reshape(1, H, 1)
            init = jnp.zeros((B, H, D), dtype=x.dtype)
            running_kv = _decay_scan(k * v, decay, init)
            running_ksum = _decay_scan(k, decay, init)
            den = jnp.clip(jnp.sum(q * running_ksum, axis=-1, keepdims=True), EPS_DEN, None)
            out = q * running_kv / den
            out = out.transpose(0, 2, 1, 3).reshape(B, T, Hid) @ w_out
            new_kv = running_kv[:, :, -1, :]
            new_ksum = running_ksum[:, :, -1, :]
            return (out, new_kv, new_ksum)
        key = jax.random.key(seed)
        k1, k2, k3 = jax.random.split(key, 3)
        x = jax.random.normal(k1, (2, 512, 256), dtype=jnp.float32)
        w_qkv = jax.random.normal(k2, (256, 768), dtype=jnp.float32) * 0.02
        w_out = jax.random.normal(k3, (256, 256), dtype=jnp.float32) * 0.02
        decay_param = jnp.full((H,), 0.95, dtype=jnp.float32)
        return {'x': x, 'w_qkv': w_qkv, 'w_out': w_out, 'decay_param': decay_param}
    _L3_attn_in = _L3_attn_setup()

    def _L3_ffn_setup():
        import jax, jax.numpy as jnp
        import numpy as np
        B, T, D = (4, 128, 256)
        N, S, H = (8, 8, 8)
        ETA = 1.0
        key = jax.random.key(seed)
        ks = jax.random.split(key, 9)
        return {'x': jax.random.normal(ks[0], (B, T, D), jnp.float32), 'select_weight': jax.random.normal(ks[1], (N, D, S), jnp.float32) / D, 'select_mean_diff': jax.random.normal(ks[2], (N, D), jnp.float32) / D, 'imp_center': jax.random.normal(ks[3], (N,), jnp.float32), 'imp_slope': jax.random.normal(ks[4], (N,), jnp.float32) * 5.0, 'lora_update': jax.random.normal(ks[5], (N, D, H), jnp.float32) * 0.02, 'lora_degen': jax.random.normal(ks[6], (N, D, H), jnp.float32) * 0.02, 'bias_w': jax.random.normal(ks[7], (N, D), jnp.float32) * 0.02, 'debias_w': jax.random.normal(ks[8], (N, D), jnp.float32) * 0.02}
    _L3_ffn_in = _L3_ffn_setup()
    _L3_c = _w((lambda *s: np.random.randn(*s).astype(np.float32) * 0.05)(16, 256))
    _L3_wmod = _w((lambda *s: np.random.randn(*s).astype(np.float32) * 0.05)(256, 6 * 256) * 256 ** (-0.5))
    _d = {'L0_attn_x': _L0_attn_in['x'], 'L0_attn_log_decay': _L0_attn_in['log_decay'], 'L0_attn_Wq': _L0_attn_in['Wq'], 'L0_attn_Wk': _L0_attn_in['Wk'], 'L0_attn_Wv': _L0_attn_in['Wv'], 'L0_attn_Wo': _L0_attn_in['Wo'], 'L0_attn_Wg1': _L0_attn_in['Wg1'], 'L0_attn_Wg2': _L0_attn_in['Wg2'], 'L0_attn_norm_w': _L0_attn_in['norm_w'], 'L0_ffn_lut': _L0_ffn_in['lut'], 'L0_ffn_gate_idx': _L0_ffn_in['gate_idx'], 'L0_ffn_up_idx': _L0_ffn_in['up_idx'], 'L0_ffn_down_idx': _L0_ffn_in['down_idx'], 'L0_c': _L0_c, 'L0_wmod': _L0_wmod, 'L1_attn_Wq': _L1_attn_in['Wq'], 'L1_attn_Wk': _L1_attn_in['Wk'], 'L1_attn_Wv': _L1_attn_in['Wv'], 'L1_attn_Wo': _L1_attn_in['Wo'], 'L1_attn_lq1': _L1_attn_in['lq1'], 'L1_attn_lk1': _L1_attn_in['lk1'], 'L1_attn_lq2': _L1_attn_in['lq2'], 'L1_attn_lk2': _L1_attn_in['lk2'], 'L1_ffn_gate_w': _L1_ffn_in['gate_w'], 'L1_ffn_expert_w': _L1_ffn_in['expert_w'], 'L1_ffn_expert_b': _L1_ffn_in['expert_b'], 'L1_c': _L1_c, 'L1_wmod': _L1_wmod, 'L2_attn_B': _L2_attn_in['B'], 'L2_attn_C': _L2_attn_in['C'], 'L2_attn_D': _L2_attn_in['D'], 'L2_ffn_weight': _L2_ffn_in['weight'], 'L2_ffn_lora_A': _L2_ffn_in['lora_A'], 'L2_ffn_lora_B': _L2_ffn_in['lora_B'], 'L2_ffn_router_w': _L2_ffn_in['router_w'], 'L2_c': _L2_c, 'L2_wmod': _L2_wmod, 'L3_attn_w_qkv': _L3_attn_in['w_qkv'], 'L3_attn_w_out': _L3_attn_in['w_out'], 'L3_attn_decay_param': _L3_attn_in['decay_param'], 'L3_ffn_select_weight': _L3_ffn_in['select_weight'], 'L3_ffn_select_mean_diff': _L3_ffn_in['select_mean_diff'], 'L3_ffn_imp_center': _L3_ffn_in['imp_center'], 'L3_ffn_imp_slope': _L3_ffn_in['imp_slope'], 'L3_ffn_lora_update': _L3_ffn_in['lora_update'], 'L3_ffn_lora_degen': _L3_ffn_in['lora_degen'], 'L3_ffn_bias_w': _L3_ffn_in['bias_w'], 'L3_ffn_debias_w': _L3_ffn_in['debias_w'], 'L3_c': _L3_c, 'L3_wmod': _L3_wmod}
    _x0 = _d['L0_attn_x']
    _d['L0_attn_x'] = jax.random.normal(jax.random.fold_in(jax.random.key(seed), 1), (16, 256, 256), dtype=_x0.dtype)
    del _x0
    return _d

def reference(L0_attn_x, L0_attn_log_decay, L0_attn_Wq, L0_attn_Wk, L0_attn_Wv, L0_attn_Wo, L0_attn_Wg1, L0_attn_Wg2, L0_attn_norm_w, L0_ffn_lut, L0_ffn_gate_idx, L0_ffn_up_idx, L0_ffn_down_idx, L0_c, L0_wmod, L1_attn_Wq, L1_attn_Wk, L1_attn_Wv, L1_attn_Wo, L1_attn_lq1, L1_attn_lk1, L1_attn_lq2, L1_attn_lk2, L1_ffn_gate_w, L1_ffn_expert_w, L1_ffn_expert_b, L1_c, L1_wmod, L2_attn_B, L2_attn_C, L2_attn_D, L2_ffn_weight, L2_ffn_lora_A, L2_ffn_lora_B, L2_ffn_router_w, L2_c, L2_wmod, L3_attn_w_qkv, L3_attn_w_out, L3_attn_decay_param, L3_ffn_select_weight, L3_ffn_select_mean_diff, L3_ffn_imp_center, L3_ffn_imp_slope, L3_ffn_lora_update, L3_ffn_lora_degen, L3_ffn_bias_w, L3_ffn_debias_w, L3_c, L3_wmod):

    def _L0_attn_ref(x, log_decay, Wq, Wk, Wv, Wo, Wg1, Wg2, norm_w):
        import jax, jax.numpy as jnp
        import numpy as np
        EPS = 1e-05
        CHUNK = 128

        def lightning_attn(q, k, v, ld, chunk=CHUNK):
            b, n, h, d = q.shape
            nc = n // chunk
            idx = jnp.arange(chunk)
            diff = idx[:, None] - idx[None, :]
            mask = diff >= 0
            D = jnp.exp(ld[:, None, None] * jnp.where(mask, diff, 0)) * mask
            q_decay = jnp.exp(ld[None, :] * (idx + 1)[:, None])
            k_decay = jnp.exp(ld[None, :] * (chunk - 1 - idx)[:, None])
            chunk_decay = jnp.exp(ld * chunk)
            qc = jnp.moveaxis(q.reshape(b, nc, chunk, h, d), 1, 0)
            kc = jnp.moveaxis(k.reshape(b, nc, chunk, h, d), 1, 0)
            vc = jnp.moveaxis(v.reshape(b, nc, chunk, h, d), 1, 0)

            def step(S, inp):
                qb, kb, vb = inp
                scores = jnp.einsum('bchd,bshd->bhcs', qb, kb) * D[None]
                o_intra = jnp.einsum('bhcs,bshd->bchd', scores, vb)
                o_inter = jnp.einsum('bchd,bhde->bche', qb, S) * q_decay[None, :, :, None]
                S_new = chunk_decay[None, :, None, None] * S + jnp.einsum('bshd,bshe->bhde', kb * k_decay[None, :, :, None], vb)
                return (S_new, o_intra + o_inter)
            S0 = jnp.zeros((b, h, d, d), dtype=q.dtype)
            S_final, oc = jax.lax.scan(step, S0, (qc, kc, vc))
            out = jnp.moveaxis(oc, 0, 1).reshape(b, n, h, d)
            return (out, S_final)

        def group_rmsnorm_fused_gate(o, gate, w, num_heads):
            b, n, d = o.shape
            hd = d // num_heads
            o = o * jax.nn.sigmoid(gate)
            og = o.reshape(b, n, num_heads, hd)
            og = og * jax.lax.rsqrt(jnp.mean(og * og, axis=-1, keepdims=True) + EPS)
            return og.reshape(b, n, d) * w
        b, n, d = x.shape
        H = log_decay.shape[0]
        hd = d // H
        q = jax.nn.silu(jnp.einsum('bnd,de->bne', x, Wq).reshape(b, n, H, hd))
        k = jax.nn.silu(jnp.einsum('bnd,de->bne', x, Wk).reshape(b, n, H, hd))
        v = jax.nn.silu(jnp.einsum('bnd,de->bne', x, Wv).reshape(b, n, H, hd))
        o, _ = lightning_attn(q, k, v, log_decay)
        o = o.reshape(b, n, d)
        gate = jnp.einsum('bnk,kd->bnd', jnp.einsum('bnd,dk->bnk', x, Wg1), Wg2)
        o = group_rmsnorm_fused_gate(o, gate, norm_w, H)
        return jnp.einsum('bnd,de->bne', o, Wo)

    def _L0_ffn_ref(x, lut, gate_idx, up_idx, down_idx):
        import jax, jax.numpy as jnp
        import numpy as np
        HIDDEN = 256
        INTER = 688
        LUT_SIZE = 16

        def _ghost_linear(x, idx, lut):
            w = lut[idx]
            return jnp.einsum('bsh,oh->bso', x, w)
        gate = _ghost_linear(x, gate_idx, lut)
        up = _ghost_linear(x, up_idx, lut)
        h = jax.nn.silu(gate) * up
        return _ghost_linear(h, down_idx, lut)

    def _L1_attn_ref(x, Wq, Wk, Wv, Wo, lq1, lk1, lq2, lk2):
        import jax, jax.numpy as jnp
        import numpy as np
        import math
        E = 256
        H = 16
        HD = E // H // 2
        DEPTH = 12
        LAMBDA_INIT = 0.8 - 0.6 * math.exp(-0.3 * DEPTH)
        b, t, e = x.shape
        scaling = HD ** (-0.5)
        q = (x @ Wq).reshape(b, t, 2 * H, HD).transpose(0, 2, 1, 3) * scaling
        k = (x @ Wk).reshape(b, t, 2 * H, HD).transpose(0, 2, 1, 3)
        v = (x @ Wv).reshape(b, t, H, 2 * HD).transpose(0, 2, 1, 3)
        scores = jnp.einsum('bhqd,bhkd->bhqk', q, k)
        causal = jnp.triu(jnp.full((t, t), -jnp.inf, dtype=jnp.float32), 1)
        aw = jax.nn.softmax((scores + causal).astype(jnp.float32), axis=-1)
        lam = jnp.exp(jnp.sum(lq1 * lk1)) - jnp.exp(jnp.sum(lq2 * lk2)) + LAMBDA_INIT
        aw = aw.reshape(b, H, 2, t, t)
        aw = aw[:, :, 0] - lam * aw[:, :, 1]
        attn = jnp.einsum('bhqk,bhkd->bhqd', aw, v)
        attn = attn * jax.lax.rsqrt(jnp.mean(attn * attn, axis=-1, keepdims=True) + 1e-05)
        attn = attn * (1.0 - LAMBDA_INIT)
        attn = attn.transpose(0, 2, 1, 3).reshape(b, t, H * 2 * HD)
        return attn @ Wo

    def _L1_ffn_ref(x, gate_w, expert_w, expert_b):
        import jax, jax.numpy as jnp
        import numpy as np
        B, S, D, E, TOPK = (4, 256, 256, 8, 2)
        batch_shape = x.shape[:-1]
        xf = x.reshape(-1, x.shape[-1])
        T = xf.shape[0]
        logits = jnp.einsum('td,ed->te', xf, gate_w)
        top_w, top_i = jax.lax.top_k(logits, TOPK)
        top_w = jax.nn.softmax(top_w.astype(jnp.float32), axis=-1).astype(x.dtype)
        gates = jnp.zeros((T, logits.shape[-1]), dtype=x.dtype)
        gates = gates.at[jnp.arange(T)[:, None], top_i].set(top_w)
        y = jnp.einsum('td,edo->eto', xf, expert_w) + expert_b[:, None, :]
        out = jnp.einsum('te,eto->to', gates, y)
        return out.reshape(*batch_shape, -1)

    def _L2_attn_ref(x, B, C, D):
        import jax, jax.numpy as jnp
        import numpy as np
        BATCH, SEQ, D_MODEL, D_STATE = (4, 512, 256, 128)
        state = jnp.tanh(jnp.einsum('bsd,nd->bsn', x, B))
        return jnp.einsum('bsn,dn->bsd', state, C) + D * x

    def _L2_ffn_ref(x, weight, lora_A, lora_B, router_w):
        import jax, jax.numpy as jnp
        import numpy as np
        NUM_EXPERTS = 8
        RANK = 16
        TOP_K = 2
        SCALING = 32.0 / RANK
        IN_F = 256
        OUT_F = 256
        B, T, D = x.shape
        N = B * T
        base = jnp.einsum('btd,od->bto', x, weight)
        logits = jnp.einsum('btd,ed->bte', x, router_w)
        probs = jax.nn.softmax(logits, axis=-1)
        topk_vals, topk_idx = jax.lax.top_k(probs, TOP_K)
        topk_vals = topk_vals / topk_vals.sum(axis=-1, keepdims=True)
        w_dense = jnp.zeros((N, NUM_EXPERTS), dtype=x.dtype).at[jnp.arange(N)[:, None], topk_idx.reshape(N, TOP_K)].set(topk_vals.reshape(N, TOP_K))
        x_flat = x.reshape(N, D)
        Ax = jnp.einsum('nd,erd->ner', x_flat, lora_A)
        expert_out = jnp.einsum('ner,ne,eor->no', Ax, w_dense, lora_B) * SCALING
        return base + expert_out.reshape(B, T, OUT_F)

    def _L3_attn_ref(x, w_qkv, w_out, decay_param):
        import jax, jax.numpy as jnp
        import numpy as np
        H = 16
        EPS_DEN = 1e-06

        def _decay_scan(x, decay, init):
            xT = jnp.moveaxis(x, 2, 0)

            def step(s, xt):
                s = decay * s + xt
                return (s, s)
            _, ys = jax.lax.scan(step, init, xT)
            return jnp.moveaxis(ys, 0, 2)

        def _phi(z):
            return jax.nn.elu(z) + 1.0

        def _reference_tuple_inner(x, w_qkv, w_out, decay_param):
            B, T, Hid = x.shape
            D = Hid // H
            qkv = x @ w_qkv
            q, k, v = jnp.split(qkv, 3, axis=-1)

            def to_bhtd(t):
                return t.reshape(B, T, H, D).transpose(0, 2, 1, 3)
            q = _phi(to_bhtd(q))
            k = _phi(to_bhtd(k))
            v = to_bhtd(v)
            decay = jax.nn.sigmoid(decay_param).reshape(1, H, 1)
            init = jnp.zeros((B, H, D), dtype=x.dtype)
            running_kv = _decay_scan(k * v, decay, init)
            running_ksum = _decay_scan(k, decay, init)
            den = jnp.clip(jnp.sum(q * running_ksum, axis=-1, keepdims=True), EPS_DEN, None)
            out = q * running_kv / den
            out = out.transpose(0, 2, 1, 3).reshape(B, T, Hid) @ w_out
            new_kv = running_kv[:, :, -1, :]
            new_ksum = running_ksum[:, :, -1, :]
            return (out, new_kv, new_ksum)
        return _reference_tuple_inner(x, w_qkv, w_out, decay_param)[0]

    def _L3_ffn_ref(x, select_weight, select_mean_diff, imp_center, imp_slope, lora_update, lora_degen, bias_w, debias_w):
        import jax, jax.numpy as jnp
        import numpy as np
        B, T, D = (4, 128, 256)
        N, S, H = (8, 8, 8)
        ETA = 1.0
        x_diff = x[:, None, :, :] - select_mean_diff[None, :, None, :]
        x_diff = x_diff / jnp.linalg.norm(x_diff, axis=3, keepdims=True)
        cont = jnp.einsum('nds,bntd->bnts', select_weight, x_diff) ** 2
        score = cont.sum(axis=-1)
        gate = jax.nn.sigmoid(imp_slope[None, :, None] * (score - imp_center[None, :, None]))
        sel_scale = gate.max(axis=1)[..., None]
        sel_idx = gate.argmax(axis=1)
        debias = jnp.take(debias_w, sel_idx, axis=0)
        bias = jnp.take(bias_w, sel_idx, axis=0)
        upd = jnp.take(lora_update, sel_idx, axis=0)
        dgn = jnp.take(lora_degen, sel_idx, axis=0)
        x_debias = x - debias
        mod_x = jnp.einsum('btdh,btd->bth', upd, x_debias)
        degen_up = jnp.einsum('btdh,bth->btd', dgn, mod_x)
        mod_x_bias = ETA * (bias + degen_up)
        return (1.0 - sel_scale) * x + sel_scale * mod_x_bias
    x = L0_attn_x
    mod = (_silu(L0_c) @ L0_wmod).reshape(L0_c.shape[0], 6, 1, -1)
    sa, ca, ga, sb, cb, gb = (mod[:, 0], mod[:, 1], mod[:, 2], mod[:, 3], mod[:, 4], mod[:, 5])
    ga = (2 * (ga >= 0) - 1) * jnp.maximum(jnp.abs(ga), 0.25)
    gb = (2 * (gb >= 0) - 1) * jnp.maximum(jnp.abs(gb), 0.25)
    h = _layernorm(x, axis=-1) * (1 + ca) + sa
    x = x + ga * _L0_attn_ref(h, L0_attn_log_decay, L0_attn_Wq, L0_attn_Wk, L0_attn_Wv, L0_attn_Wo, L0_attn_Wg1, L0_attn_Wg2, L0_attn_norm_w)
    h = _layernorm(x, axis=-1) * (1 + cb) + sb
    x = x + gb * _L0_ffn_ref(h, L0_ffn_lut, L0_ffn_gate_idx, L0_ffn_up_idx, L0_ffn_down_idx)
    mod = (_silu(L1_c) @ L1_wmod).reshape(L1_c.shape[0], 6, 1, -1)
    sa, ca, ga, sb, cb, gb = (mod[:, 0], mod[:, 1], mod[:, 2], mod[:, 3], mod[:, 4], mod[:, 5])
    ga = (2 * (ga >= 0) - 1) * jnp.maximum(jnp.abs(ga), 0.25)
    gb = (2 * (gb >= 0) - 1) * jnp.maximum(jnp.abs(gb), 0.25)
    h = _layernorm(x, axis=-1) * (1 + ca) + sa
    x = x + ga * _L1_attn_ref(h, L1_attn_Wq, L1_attn_Wk, L1_attn_Wv, L1_attn_Wo, L1_attn_lq1, L1_attn_lk1, L1_attn_lq2, L1_attn_lk2)
    h = _layernorm(x, axis=-1) * (1 + cb) + sb
    x = x + gb * _L1_ffn_ref(h, L1_ffn_gate_w, L1_ffn_expert_w, L1_ffn_expert_b)
    mod = (_silu(L2_c) @ L2_wmod).reshape(L2_c.shape[0], 6, 1, -1)
    sa, ca, ga, sb, cb, gb = (mod[:, 0], mod[:, 1], mod[:, 2], mod[:, 3], mod[:, 4], mod[:, 5])
    ga = (2 * (ga >= 0) - 1) * jnp.maximum(jnp.abs(ga), 0.25)
    gb = (2 * (gb >= 0) - 1) * jnp.maximum(jnp.abs(gb), 0.25)
    h = _layernorm(x, axis=-1) * (1 + ca) + sa
    x = x + ga * _L2_attn_ref(h, L2_attn_B, L2_attn_C, L2_attn_D)
    h = _layernorm(x, axis=-1) * (1 + cb) + sb
    x = x + gb * _L2_ffn_ref(h, L2_ffn_weight, L2_ffn_lora_A, L2_ffn_lora_B, L2_ffn_router_w)
    mod = (_silu(L3_c) @ L3_wmod).reshape(L3_c.shape[0], 6, 1, -1)
    sa, ca, ga, sb, cb, gb = (mod[:, 0], mod[:, 1], mod[:, 2], mod[:, 3], mod[:, 4], mod[:, 5])
    ga = (2 * (ga >= 0) - 1) * jnp.maximum(jnp.abs(ga), 0.25)
    gb = (2 * (gb >= 0) - 1) * jnp.maximum(jnp.abs(gb), 0.25)
    h = _layernorm(x, axis=-1) * (1 + ca) + sa
    x = x + ga * _L3_attn_ref(h, L3_attn_w_qkv, L3_attn_w_out, L3_attn_decay_param)
    h = _layernorm(x, axis=-1) * (1 + cb) + sb
    x = x + gb * _L3_ffn_ref(h, L3_ffn_select_weight, L3_ffn_select_mean_diff, L3_ffn_imp_center, L3_ffn_imp_slope, L3_ffn_lora_update, L3_ffn_lora_degen, L3_ffn_bias_w, L3_ffn_debias_w)
    return x

_drawn_inputs = setup_inputs


def setup_inputs(seed=0):
    import zlib

    import numpy as np

    out = dict(_drawn_inputs(seed))
    spreads = {'L0_attn_norm_w': (1.0, 0.2),
     'L1_ffn_expert_b': (0.0, 0.467),
     'L2_attn_D': (0.0, 0.346),
     'L3_attn_decay_param': (0.949999988079071, 0.6)}
    factors = {'L0_ffn_lut': 3.051,
     'L1_attn_Wq': 4.002,
     'L1_attn_Wk': 3.811,
     'L1_attn_lq1': 36.191,
     'L1_attn_lk1': 23.052,
     'L1_attn_lq2': 8.0,
     'L1_attn_lk2': 8.0,
     'L2_attn_B': 8.0,
     'L2_attn_C': 8.0,
     'L2_ffn_lora_A': 3.618,
     'L2_ffn_lora_B': 3.606,
     'L2_ffn_router_w': 4.164,
     'L3_attn_w_qkv': 8.0,
     'L3_attn_w_out': 8.0,
     'L3_ffn_select_weight': 8.0,
     'L3_ffn_select_mean_diff': 8.0,
     'L3_ffn_imp_center': 8.0,
     'L3_ffn_imp_slope': 8.0,
     'L3_ffn_lora_update': 8.0,
     'L3_ffn_lora_degen': 8.0,
     'L3_ffn_bias_w': 8.0,
     'L3_ffn_debias_w': 8.0,
     'L3_c': 8.0,
     'L3_wmod': 8.0}
    for name, (base, spread) in spreads.items():
        noise = np.random.default_rng([zlib.crc32(name.encode()), seed]).standard_normal(out[name].shape)
        drawn = base * np.exp(spread * noise) if base else spread * noise
        out[name] = jnp.asarray(drawn.astype(out[name].dtype))
    for name, factor in factors.items():
        out[name] = (out[name] * factor).astype(out[name].dtype)
    return out
```

```python
import math
from contextlib import ExitStack

import numpy as np

import concourse.bass as bass
from concourse import mybir

F32 = mybir.dt.float32
BF16 = mybir.dt.bfloat16
I32 = mybir.dt.int32
ALU = mybir.AluOpType
ACT = mybir.ActivationFunctionType
AX = mybir.AxisListType

P = 128
B = 16
T = 256
TT = T // P
D = 256
KH = D // P
LAYERS = 4
SECTIONS = 6
LN_EPS = 1e-5
HEADS = 16
HD = D // HEADS
INTER = 688
FT = -(-INTER // P)
LUT = 16
EPS_DEN = 1e-6
LAMBDA_INIT = 0.8 - 0.6 * math.exp(-0.3 * 12)
QK_SCALE = (HD // 2) ** -0.5
LOW = -1e30
E = 8
NS = 64
LORA_SCALE = 2.0
PHASES = ["L0_attn", "L0_ffn", "L1_attn", "L1_ffn", "L2_attn", "L2_ffn", "L3_attn", "L3_ffn"]


class Idx:

    def __init__(self, reg, off):
        self.reg, self.off = reg, off

    def __add__(self, k):
        return Idx(self.reg, self.off + k)

    def __sub__(self, k):
        return Idx(self.reg, self.off - k)

    @property
    def n(self):
        return self.off if self.reg is None else self.reg + self.off

    @property
    def par(self):
        return self.off % 2

    @property
    def ok(self):
        return self.reg is not None or 0 <= self.off < B


class Sig:

    def __init__(self, sem, base, per):
        self.sem, self.base, self.per = sem, base, per

    def __call__(self, b, k=None):
        k = self.per if k is None else k
        if b.reg is None:
            v = self.base + self.per * b.off + k
            assert v > 0
            return self.sem, v
        return self.sem, b.reg * self.per + (self.base + self.per * b.off + k)


class Signals:

    def __init__(self, sig):
        self.stat_raw, self.stat, self.rstd_raw, self.rstd, self.xn = \
            sig("stat_raw"), sig("stat"), sig("rstd_raw"), sig("rstd"), sig("xn")
        self.xT, self.h, self.hfree, self.y, self.x = \
            sig("xT"), sig("h"), sig("hfree"), sig("y"), sig("x")
        self.acc, self.acc0, self.att, self.ax, self.ax_ps = \
            sig("acc"), sig("acc0"), sig("att"), sig("ax"), sig("ax_ps")
        self.bias_ps, self.clip, self.den_ps, self.e, self.ed = \
            sig("bias_ps"), sig("clip"), sig("den_ps"), sig("e"), sig("ed")
        self.ek, self.eq, self.g, self.gT, self.gT_ps = \
            sig("ek"), sig("eq"), sig("g"), sig("gT"), sig("gT_ps")
        self.gate, self.gate_ps, self.hid, self.hsq, self.ht = \
            sig("gate"), sig("gate_ps"), sig("hid"), sig("hsq"), sig("ht")
        self.htok_ps, self.k, self.k_ps, self.kdec, self.kg = \
            sig("htok_ps"), sig("k"), sig("k_ps"), sig("kdec"), sig("kg")
        self.lcopy, self.logit_ps, self.mT, self.mT_ps, self.max = \
            sig("lcopy"), sig("logit_ps"), sig("mT"), sig("mT_ps"), sig("max")
        self.max_ps, self.mparts, self.ms, self.msplit, self.mx = \
            sig("max_ps"), sig("mparts"), sig("ms"), sig("msplit"), sig("mx")
        self.n_ps, self.num, self.o, self.oT, self.og = \
            sig("n_ps"), sig("num"), sig("o"), sig("oT"), sig("og")
        self.ogT, self.ogT_ps, self.oms, self.otok_ps, self.p_ps = \
            sig("ogT"), sig("ogT_ps"), sig("oms"), sig("otok_ps"), sig("p_ps")
        self.parts, self.pick, self.picked, self.prob, self.pv = \
            sig("parts"), sig("pick"), sig("picked"), sig("prob"), sig("pv")
        self.q, self.q_ps, self.qdec, self.qs, self.rden = \
            sig("q"), sig("q_ps"), sig("qdec"), sig("qs"), sig("rden")
        self.rl, self.rn, self.rn_raw, self.rt, self.scan = \
            sig("rl"), sig("rn"), sig("rn_raw"), sig("rt"), sig("scan")
        self.score, self.se_ps, self.split, self.sq, self.state = \
            sig("score"), sig("se_ps"), sig("split"), sig("sq"), sig("state")
        self.state_ps, self.sumk, self.tk, self.u, self.unit_ps = \
            sig("state_ps"), sig("sumk"), sig("tk"), sig("u"), sig("unit_ps")
        self.v, self.v_ps, self.wx, self.wx_ps, self.y1 = \
            sig("v"), sig("v_ps"), sig("wx"), sig("wx_ps"), sig("y1")
        self.y_ps, self.z, self.zT_ps, self.zr, self.zz = \
            sig("y_ps"), sig("z"), sig("zT_ps"), sig("zr"), sig("zz")


def slots(eng, slot, first, steady, last):
    lo, hi = steady
    assert lo % 2 == 0 and hi % 2 == 0 and hi > lo
    for i in range(first, lo):
        slot(Idx(None, i))
    with eng.Fori(lo // 2, hi // 2) as r:
        slot(Idx(r * 2, 0))
        slot(Idx(r * 2, 1))
    for i in range(hi, last + 1):
        slot(Idx(None, i))


def layout(**inputs):
    a = {k: np.asarray(v) for k, v in inputs.items()}
    f = np.float32
    k = np.arange(P)
    two = lambda w: np.ascontiguousarray(w.reshape(KH, P, -1).transpose(1, 0, 2))
    out = {"x": a["L0_attn_x"].reshape(B, TT, P, D)}
    out["c"] = np.ascontiguousarray(np.stack([two(a[f"L{i}_c"].T) for i in range(LAYERS)], 1))
    out["wmod"] = np.stack([a[f"L{i}_wmod"] for i in range(LAYERS)])
    ident = np.eye(P, dtype=f)
    out["ident"] = ident
    for n in "qkvo":
        out[f"l0_w{n}"] = two(a[f"L0_attn_W{n}"])
    out["l0_wg1"], out["l0_wg2"] = two(a["L0_attn_Wg1"]), a["L0_attn_Wg2"]
    ld = a["L0_attn_log_decay"]
    out["l0_ld"] = ld
    out["l0_ld_col"] = np.ascontiguousarray(np.repeat(ld, HD).reshape(KH, P).T)
    out["l0_ld_row"] = np.repeat(ld, HD)
    out["l0_nw"] = np.ascontiguousarray(a["L0_attn_norm_w"].reshape(KH, P).T)
    age = k[None, :] - k[:, None]
    out["l0_age"] = np.maximum(age, 0).astype(f)
    out["causal"] = (age >= 0).astype(f)
    out["count"] = np.broadcast_to((k + 1).astype(f), (P, P)).copy()
    out["left"] = (P - 1 - k).astype(f)[:, None]
    own = np.zeros((P, KH, D), f)
    for h in range(HEADS):
        own[h % 8 * HD:h % 8 * HD + HD, h // 8, h % 8 * 32:h % 8 * 32 + HD] = 1
    out["l0_own"] = own
    pad = np.zeros((FT * P - INTER, D), np.int32)
    down = np.concatenate([a["L0_ffn_down_idx"].T, pad]).reshape(FT, P, D).transpose(1, 0, 2)
    out["l0_idx"] = np.concatenate([two(a["L0_ffn_gate_idx"].T).reshape(P, -1), two(a["L0_ffn_up_idx"].T).reshape(P, -1),
                                    down.reshape(P, -1)], 1)
    out["l0_lut"] = a["L0_ffn_lut"]
    out["iota"] = np.arange(16, dtype=f)
    out["l2_b"] = two(a["L2_attn_B"].T)
    out["l2_c"] = np.ascontiguousarray(a["L2_attn_C"].T)
    out["l2_d"] = np.ascontiguousarray(a["L2_attn_D"].reshape(KH, P).T)
    out["l3_wqkv"], out["l3_wo"] = two(a["L3_attn_w_qkv"]), two(a["L3_attn_w_out"])
    out["l3_dec"] = np.ascontiguousarray(np.repeat(a["L3_attn_decay_param"], HD).reshape(KH, P).T)
    out["l3_same"] = (k[:, None] // HD == k[None, :] // HD).astype(f)
    for n in "qkvo":
        out[f"l1_w{n}"] = two(a[f"L1_attn_W{n}"])
    out["lam_v"] = np.stack([np.stack([a[f"L1_attn_lq{i}"], a[f"L1_attn_lk{i}"]]) for i in (1, 2)])
    bf = mybir.dt.np(BF16)
    low = np.where(age < 0, np.float32(LOW), np.float32(0))
    out["ident_b"] = ident.astype(bf)
    out["later4"] = np.ascontiguousarray(np.broadcast_to(low.T[:, None], (P, 4, P))).astype(bf)
    out["earlier4"] = np.ascontiguousarray(np.broadcast_to(low[:, None], (P, 4, P))).astype(bf)
    pick = np.zeros((P, 16, P), f)
    for part in range(3):
        for h in range(16):
            pick[16 * part + h, h] = 1
    out["pick16"] = pick.astype(bf)
    out["l1_we"] = np.ascontiguousarray(a["L1_ffn_expert_w"].reshape(E, KH, P, D).transpose(2, 1, 0, 3))
    out["l1_gw"], out["l1_eb"] = two(a["L1_ffn_gate_w"].T), a["L1_ffn_expert_b"]
    out["l2_la"], out["l2_w"] = two(a["L2_ffn_lora_A"].reshape(P, D).T), two(a["L2_ffn_weight"].T)
    out["l2_rw"] = two(a["L2_ffn_router_w"].T)
    out["l2_lb"] = np.ascontiguousarray(a["L2_ffn_lora_B"].transpose(0, 2, 1)).reshape(P, D)
    out["l2_sel"] = (np.arange(E)[:, None] == k[None, :] // (P // E)).astype(f)
    rows = lambda w: w.transpose(1, 0, 2).reshape(D, NS)
    out["l3_sw"] = two(rows(a["L3_ffn_select_weight"]))
    out["l3_up"] = two(np.concatenate([rows(a["L3_ffn_lora_update"]), np.zeros((D, E), f)], 1))
    out["l3_md"], out["l3_db"], out["l3_mdr"] = two(a["L3_ffn_select_mean_diff"].T), two(a["L3_ffn_debias_w"].T), a["L3_ffn_select_mean_diff"]
    out["l3_cs"] = np.stack([a["L3_ffn_imp_center"], a["L3_ffn_imp_slope"]], 1)
    out["l3_dg"] = np.concatenate([a["L3_ffn_lora_degen"].transpose(0, 2, 1).reshape(NS, D), a["L3_ffn_bias_w"]])
    blk = (np.arange(NS)[:, None] // (NS // E) == np.arange(E)[None, :]).astype(f)
    out["l3_blk"] = np.concatenate([blk, np.zeros((P - NS, E), f)])
    out["l3_own"] = np.concatenate([blk, np.zeros((E, E), f)])
    out["l3_e72"] = np.ascontiguousarray(np.concatenate([blk, np.eye(E, dtype=f)]).T)
    out["l3_tail"] = (np.arange(NS + E) >= NS).astype(f)[:, None]
    out["l3_one"] = np.ones((P, E), f)
    out["rank"] = np.broadcast_to(np.arange(E, 0, -1).astype(f), (P, TT, E)).copy()
    return {"in_" + k: v for k, v in out.items()}


def build(nc, ins, y_out, first=0, last=8):
    ctx = ExitStack()
    with ctx:
        def sem(name):
            return ctx.enter_context(nc.semaphore(name))

        taken = {}

        def sb(name, shape, dt=F32, stack=ctx):
            taken[stack] = taken.get(stack, 0) + math.prod(shape[1:]) * (2 if dt == BF16 else 4)
            return stack.enter_context(nc.sbuf_tensor(name, shape, dt))

        common = ["stat_raw", "stat", "rstd_raw", "rstd", "xn", "xT", "h", "hfree", "y", "x"]
        per_phase = {
            "L0_attn": {"q_ps": 1, "k_ps": 1, "v_ps": 1, "q": 1, "k": 1, "v": 1, "kg": 1, "qdec": 1, "kdec": 1,
                        "gate_ps": 1, "state_ps": 1, "gate": 1, "state": 1, "score": 8, "prob": 8, "pv": 8, "oT": 1,
                        "otok_ps": 2, "u": 2, "sq": 1, "ms": 1, "rn_raw": 1, "rn": 1, "og": 1, "ogT_ps": 1, "ogT": 1,
                        "y_ps": 1, "pick": 1, "picked": 1},
            "L0_ffn": {"gate_ps": FT - 1, "gate": FT, "hid": FT, "y_ps": 1},
            "L1_ffn": {"logit_ps": 1, "lcopy": 1, "rt": 16, "ed": 1, "e": 1, "g": 1, "gT_ps": 1, "gT": 1,
                       "bias_ps": 1, "acc0": 1, "unit_ps": 7, "acc": 16},
            "L2_ffn": {"logit_ps": 1, "lcopy": 1, "rt": 16, "ed": 1, "e": 1, "g": 1, "gT_ps": 1, "gT": 1,
                       "ax_ps": 1, "wx_ps": 1, "wx": 1, "ax": 1},
            "L1_attn": {"q_ps": 1, "k_ps": 1, "q": 1, "k": 1, "v": 1, "split": 2, "parts": 1, "max_ps": 24, "max": 24,
                        "msplit": 6, "mparts": 2, "mT_ps": 2, "mT": 2, "score": 24, "prob": 24, "pv": 8, "oT": 8,
                        "otok_ps": 4, "rl": 4, "u": 4, "att": 1, "sq": 1, "ms": 1, "rn_raw": 1, "rn": 1, "og": 1,
                        "ogT_ps": 1, "ogT": 1, "y_ps": 1},
            "L3_attn": {"q_ps": 1, "k_ps": 1, "q": 1, "k": 1, "eq": 1, "ek": 1, "v": 1, "scan": 1, "sumk": 1,
                        "num": 1, "qs": 1, "den_ps": 1, "clip": 1, "rden": 1, "o": 1, "y_ps": 1},
            "L3_ffn": {"p_ps": 1, "htok_ps": 1, "hsq": 1, "sq": 1, "mx": 1, "ht": 1, "n_ps": 1, "zr": 3, "z": 1, "zT_ps": 1,
                       "tk": 7, "ed": 1, "e": 1, "g": 1, "oms": 1, "gT_ps": 1, "gT": 1, "se_ps": 1, "zz": 1, "y_ps": 1, "y1": 2},
            "L2_attn": {"state_ps": 1, "state": 1},
        }
        names = common + sorted({n for d in per_phase.values() for n in d})
        sems = {n: sem(n) for n in names}
        ga_in = [sem("ga_in0"), sem("ga_in1")]
        base = {n: 0 for n in names}
        sigs = []
        for p in range(first, last):
            per = {n: 1 for n in common} | per_phase.get(PHASES[p], {})
            sigs.append(Signals(lambda n: Sig(sems[n], base[n], per.get(n, 0))))
            for n, k in per.items():
                base[n] += B * k

        def ga_loaded(pl, b):
            v = 16 * (B // 2) * pl + 16 * (b.off // 2 + 1)
            return ga_in[b.par], v if b.reg is None else b.reg * 8 + v

        x_in = [sem("x_in_first"), sem("x_in_rest")]
        const_in = sem("const_in")
        idx_in = sem("idx_in")
        wmod_in = [sem("wmod_in0"), sem("wmod_in1")]
        ga_scr = sem("ga_scratch")
        w_in = [sem(f"w_in_{p}") for p in range(8)]
        out_done = sem("out_done")
        mod_sems = {n: sem("mod_" + n) for n in ("silu", "rows_ps", "rows", "col_ps", "col", "sign", "clip", "both", "ga")}

        X = sb("X", [P, B, TT, D])
        ident = sb("ident", [P, P])
        cT = sb("cT", [P, LAYERS, KH, B])
        scT = sb("scT", [P, LAYERS, KH, B])
        modT = sb("modT", [P, 2 * LAYERS, 2, KH, B])
        hT = [sb(f"hT{i}", [P, KH, T]) for i in range(2)]
        xn = [sb(f"xn{i}", [P, TT, D]) for i in range(2)]
        st6 = [sb(f"st6_{i}", [P, TT, 6]) for i in range(2)]
        mv = [sb(f"mv{i}", [P, TT, 2]) for i in range(2)]
        rs = [sb(f"rs{i}", [P, TT]) for i in range(2)]
        half = sb("half", [P, 32])
        eps = sb("eps", [P, TT])
        zero = sb("zero", [P, 1])
        eps_sum = sb("eps_sum", [P, 32])
        eps_sum1 = sb("eps_sum1", [P, 32])
        spare = sb("spare", [P, 1])
        rank = sb("rank", [P, TT, E])
        rt_l, rt_eq = sb("rt_l", [P, TT, E]), sb("rt_eq", [P, TT, E])
        rt_o = sb("rt_o", [P, 2, TT, E])
        rt_m, rt_w = sb("rt_m", [P, 2, TT]), sb("rt_w", [P, 2, TT])
        rt_r, rt_d, rt_e = sb("rt_r", [P, TT]), sb("rt_d", [P, TT]), sb("rt_e", [P, TT])
        rt_g = [sb(f"rt_g{i}", [P, TT, E]) for i in range(2)]
        rt_gT = sb("rt_gT", [E, T])
        ga_sb = [sb(f"ga_sb{i}", [P, D]) for i in range(2)]
        y_sb = [sb(f"y_sb{i}", [P, TT, D]) for i in range(2)]
        ga_dram = nc.dram_tensor("ga_dram", (2 * LAYERS, B, D), F32, kind="Internal").ap()
        PS = ctx.enter_context(nc.psum_tensor("PS", [P, 8, 512], F32))
        half_set = sem("half_set")

        kmask_in = [sem("kmask_in0"), sem("kmask_in1")]
        setup = {n: sem("set_" + n) for n in ("exp", "wo", "zero", "decay", "pads", "dexp", "dsum", "ddec",
                                                    "f_ps", "f_step", "f_set", "a_zero", "a_wo", "a_dot", "a_exp", "a_lam",
                                                    "a_pad", "a_one")}

        wbuf = lambda n, shape, k=2, dt=F32: [sb(f"{n}{i}", shape, dt, work) for i in range(k)]
        work = ExitStack()
        l1_we = sb("l1_we", [P, KH, E, D], F32, work)
        l1_gw = sb("l1_gw", [P, KH, E], F32, work)
        l1_eb = sb("l1_eb", [E, D], F32, work)
        l1_acc = wbuf("l1_acc", [P, TT, D])
        work.close()
        work = ExitStack()
        l2_la, l2_w = sb("l2_la", [P, KH, P], F32, work), sb("l2_w", [P, KH, D], F32, work)
        l2_rw, l2_lb = sb("l2_rw", [P, KH, E], F32, work), sb("l2_lb", [P, D], F32, work)
        l2_sel = sb("l2_sel", [E, P], F32, work)
        l2_ax = wbuf("l2_ax", [P, T])
        l2_wx = sb("l2_wx", [P, T], F32, work)
        work.close()
        work = ExitStack()
        l3_sw, l3_up = sb("l3_sw", [P, KH, NS], F32, work), sb("l3_up", [P, KH, NS + E], F32, work)
        l3_md, l3_db, l3_m2 = (sb("l3_" + n, [P, KH, E], F32, work) for n in ("md", "db", "m2"))
        l3_mdr, l3_mdsq = sb("l3_mdr", [E, D], F32, work), sb("l3_mdsq", [E, D], F32, work)
        l3_cs, l3_md2 = sb("l3_cs", [E, 2], F32, work), sb("l3_md2", [E, 1], F32, work)
        l3_dg = sb("l3_dg", [NS + E, D], F32, work)
        l3_e72 = sb("l3_e72", [E, NS + E], F32, work)
        l3_blk, l3_own = sb("l3_blk", [P, E], F32, work), sb("l3_own", [NS + E, E], F32, work)
        l3_tail, l3_one = sb("l3_tail", [NS + E, 1], F32, work), sb("l3_one", [P, E], F32, work)
        l3_g1, l3_g0 = sb("l3_g1", [NS, E], F32, work), sb("l3_g0", [NS + E, E], F32, work)
        l3_c1, l3_c0 = sb("l3_c1", [NS, 1], F32, work), sb("l3_c0", [NS + E, 1], F32, work)
        l3_hsq, l3_sq = sb("l3_hsq", [P, KH, T], F32, work), sb("l3_sq", [P, T], F32, work)
        l3_mx, l3_ht, l3_oms = wbuf("l3_mx", [NS + E, T]), wbuf("l3_ht", [P, TT, D]), wbuf("l3_oms", [P, TT])
        l3_n, l3_z, l3_zz = sb("l3_n", [E, T], F32, work), sb("l3_z", [E, T], F32, work), sb("l3_zz", [NS + E, T], F32, work)
        l3_ez, l3_ee, l3_y1 = sb("l3_ez", [P, TT, E], F32, work), sb("l3_ee", [P, TT, E], F32, work), sb("l3_y1", [P, TT, D], F32, work)
        work.close()

        lut_w = sb("lut_w", [P, 2 * KH * INTER + FT * D])
        l2_dd_set = sem("l2_dd_set")
        ffn_size = max(taken[w] for w in taken if w is not ctx)
        beyond = ffn_size - 4 * (2 * KH * INTER + FT * D)

        work = ExitStack()
        wmod = [sb(f"wmod{i}", [P, KH, SECTIONS * D], F32, work) for i in range(2)]
        mrow = [sb(f"mrow{i}", [B, SECTIONS, D], F32, work) for i in range(2)]
        gtmp = sb("gtmp", [B, 3, 2, D], F32, work)
        work.close()
        work = ExitStack()
        sb(f"beyond{len(taken)}", [P, beyond // 4], F32, work)
        l2_b = sb("l2_b", [P, KH, P], F32, work)
        l2_c = sb("l2_c", [P, D], F32, work)
        l2_d = sb("l2_d", [P, KH], F32, work)
        l2_dd = sb("l2_dd", [P, KH, P], F32, work)
        l2_st = [sb(f"l2_st{i}", [P, T], F32, work) for i in range(2)]
        work.close()
        work = ExitStack()
        l0_pick = sb("l0_pick", [P, 2 * KH * INTER + FT * D], F32, work)
        l0_idx = sb("l0_idx", [P, 2 * KH * INTER + FT * D], I32, work)
        kmask = wbuf("l0_kmask", [P, 8, KH, T])
        l0_w = {n: sb("l0_w" + n, [P, KH, D], F32, work) for n in "qkvo"}
        l0_wo_n = l0_w["o"]
        l0_wg1 = sb("l0_wg1", [P, KH, HD], F32, work)
        l0_wg2 = sb("l0_wg2", [HD, D], F32, work)
        l0_ld = sb("l0_ld", [P, HEADS], F32, work)
        l0_ld_col = sb("l0_ld_col", [P, KH], F32, work)
        l0_ld_row = sb("l0_ld_row", [P, D], F32, work)
        l0_nw = sb("l0_nw", [P, KH], F32, work)
        l0_age = sb("l0_age", [P, P], F32, work)
        causal = sb("causal", [P, P], F32, work)
        count = sb("count", [P, P], F32, work)
        left = sb("left", [P, 1], F32, work)
        l0_own = sb("l0_own", [P, KH * D], F32, work)
        l0_decay = sb("l0_decay", [P, HEADS, P], F32, work)
        l0_qdec = sb("l0_qdec", [P, KH, P], F32, work)
        l0_kdec = l0_ld_row
        l0_lut = sb("l0_lut", [P, LUT], F32, work)
        iota = sb("iota", [P, LUT], F32, work)
        qT, kT = wbuf("l0_qT", [P, KH, T]), wbuf("l0_kT", [P, KH, T], 1)
        vpad = wbuf("l0_vpad", [P, TT, HEADS, 32])
        kraw, kdec, g1T, qdec = wbuf("l0_kraw", [P, D], 1), wbuf("l0_kdec_", [P, D]), wbuf("l0_g1T", [HD, T]), wbuf("l0_qdec_", [P, KH, P])
        gate = wbuf("l0_gate", [P, TT, D])
        state = wbuf("l0_state", [P, KH * D])
        prob = wbuf("l0_prob", [P, 4, P], 4)
        oT = sb("l0_oT", [P, 4, TT, P], F32, work)
        u_sb, sq_sb, og_sb, ogT_sb = (sb("l0_" + n, [P, TT, D], F32, work) for n in ("u", "sq", "og", "ogT"))
        ms_sb = sb("l0_ms", [P, TT * HEADS], F32, work)
        work.close()

        work = ExitStack()
        sb(f"beyond{len(taken)}", [P, beyond // 4], F32, work)
        l1_w = {n: sb("l1_w" + n, [P, KH, D], F32, work) for n in "qkvo"}
        lam_v, lam_p, lam = sb("lam_v", [P, 2, 2, 8], F32, work), sb("lam_p", [P, 2, 8], F32, work), sb("lam", [P, 3], F32, work)
        ident_b = sb("ident_b", [P, P], BF16, work)
        later4 = sb("later4", [P, 4, P], BF16, work)
        earlier4 = sb("earlier4", [P, 4, P], BF16, work)
        pick16 = sb("pick16", [P, 16, P], BF16, work)
        qk32, qk_rest = sb("qk32", [P, 2, KH * T], F32, work), sb("qk_rest", [P, 2, KH * T], F32, work)
        qk_parts = wbuf("qk_parts", [P, 3, 2, KH * T], 2, BF16)
        QS, KS = wbuf("QS", [P, 16, 2, T], 2, BF16), wbuf("KS", [P, 16, T], 2, BF16)
        negmax = wbuf("negmax", [P, TT, 32])
        m_rest = sb("m_rest", [P, TT, 16], F32, work)
        mparts, maxT = wbuf("mparts", [P, TT, P], 2, BF16), wbuf("maxT", [P, T], 2, BF16)
        pw = [wbuf(f"pw{i}_", [P, 2, T]) for i in range(2)]
        pz = wbuf("pz", [P, 4, P])
        l1_vpad = wbuf("l1_vpad", [P, TT, HEADS, 32])
        l1_oT = sb("l1_oT", [P, 8, T], F32, work)
        l1_rl, l1_t = sb("l1_rl", [P, TT, 32], F32, work), sb("l1_t", [P, TT, 32, HD], F32, work)
        l1_att, l1_sq = sb("l1_att", [P, TT * HEADS, HD], F32, work), sb("l1_sq", [P, TT * HEADS, HD], F32, work)
        l1_ms = sb("l1_ms", [P, TT * HEADS], F32, work)
        l1_og, l1_ogT = sb("l1_og", [P, TT, D], F32, work), sb("l1_ogT", [P, KH, T], F32, work)
        work.close()
        before = taken[work] - 4 * (3 * T + 2 * FT * T) + 9 * 1024
        work = ExitStack()
        sb("before", [P, before // 4], F32, work)
        act_sb = wbuf("l0f_act", [P, T], 3)
        hid = wbuf("l0f_hid", [P, FT, T])
        work.close()
        work = ExitStack()
        sb(f"beyond{len(taken)}", [P, beyond // 4], F32, work)
        l3_wqkv = sb("l3_wqkv", [P, KH, 3 * D], F32, work)
        l3_wo = sb("l3_wo", [P, KH, D], F32, work)
        l3_same = sb("l3_same", [P, P], F32, work)
        l3_dec = sb("l3_dec", [P, KH], F32, work)
        l3_r, l3_e = wbuf("l3_r", [P, KH * T]), wbuf("l3_e", [P, KH * T])
        l3_qk = wbuf("l3_qk", [P, KH, T])
        l3_sk, l3_kv, l3_skv, l3_qs = (sb("l3_" + n, [P, KH, T], F32, work) for n in ("sk", "kv", "skv", "qs"))
        l3_num = wbuf("l3_num", [P, KH, T])
        l3_den = sb("l3_den", [P, KH * T], F32, work)
        work.close()

        qk_dram = nc.dram_tensor("qk_dram", (2, 3, 2, KH, P, T), BF16, kind="Internal").ap()
        stack_in, scratch_in = [sem("stack_in0"), sem("stack_in1")], [sem("scratch_in0"), sem("scratch_in1")]

        block = ctx.enter_context(nc.Block())

        def xb(b):
            return X[:, bass.ds(b.n, 1), :, :].rearrange("p a t d -> p (a t) d")

        def has(pl, b):
            return pl > 0 or b.ok

        def ln_stats(dve, pl, s, b):
            if pl == 0:
                if b.reg is None and b.off < 4:
                    dve.wait_ge(x_in[0], 16)
                else:
                    dve.wait_ge(x_in[1], 16)
            else:
                dve.wait_ge(*sigs[pl - 1].x(b))
            for t in range(TT):
                last_ = dve.bn_stats(st6[b.par][:, t, :], xb(b)[:, t, :])
            last_.then_inc(s.stat_raw.sem, 1)
            dve.wait_ge(*s.stat_raw(b))
            dve.memset(spare[:, :], 0.0)
            for t in range(TT):
                last_ = dve.bn_aggr(mv[b.par][:, t, :], st6[b.par][:, t, :])
            last_.then_inc(s.stat.sem, 1)

        def ln_rstd(pool, pl, s, b):
            pool.wait_ge(*s.stat(b))
            if has(pl, b - 2):
                pool.wait_ge(*s.xn(b - 2))
            pool.tensor_tensor(rs[b.par][:, :], mv[b.par][:, :, 1], eps[:, 0:TT], ALU.add).then_inc(s.rstd_raw.sem, 1)
            pool.wait_ge(*s.rstd_raw(b))
            pool.tensor_tensor(rs[b.par][:, :], rs[b.par][:, :], half[:, 0:TT], ALU.pow).then_inc(s.rstd.sem, 1)

        def ln_apply(dve, pl, s, b):
            dve.wait_ge(*s.rstd(b))
            if has(pl, b - 2):
                dve.wait_ge(*s.xT(b - 2))
            for t in range(TT):
                last_ = dve.tensor_scalar(xn[b.par][:, t, :], xb(b)[:, t, :], mv[b.par][:, t, 0:1],
                                          rs[b.par][:, t:t + 1], ALU.subtract, ALU.mult)
            last_.then_inc(s.xn.sem, 1)

        def ln_transpose(pe, pl, s, b):
            pe.wait_ge(*s.xn(b))
            if has(pl, b - 1):
                pe.wait_ge(*s.h(b - 1))
            for kh in range(KH):
                for t in range(TT):
                    last_ = pe.transpose(PS[:, 0, kh * T + t * P:kh * T + (t + 1) * P],
                                         xn[b.par][:, t, kh * P:(kh + 1) * P], ident[:, :])
            last_.then_inc(s.xT.sem, 1)

        def modulate(act, pl, s, b):
            sub = first + pl
            act.wait_ge(*s.xT(b))
            if has(pl, b - 2):
                act.wait_ge(*s.hfree(b - 2))
            for kh in range(KH):
                last_ = act.activation(hT[b.par][:, kh, :], PS[:, 0, kh * T:(kh + 1) * T], ACT.Identity,
                                       bias=modT[:, sub, 0, kh, bass.ds(b.n, 1)],
                                       scale=modT[:, sub, 1, kh, bass.ds(b.n, 1)])
            last_.then_inc(s.h.sem, 1)

        def gate_load(sp, pl, s, b):
            if has(pl, b - 2):
                sp.wait_ge(*s.y(b - 2))
            sp.dma_start(ga_sb[b.par][:, :], ga_dram[first + pl, bass.ds(b.n, 1), :].rearrange("a d -> (a d)")
                         .partition_broadcast(P)).then_inc(ga_in[b.par], 16)

        def gated(dve, pl, s, b, out_ps):
            dve.wait_ge(*ga_loaded(pl, b))
            if has(pl, b - 2):
                dve.wait_ge(*s.x(b - 2))
            dve.tensor_tensor(y_sb[b.par][:, :, :], out_ps, ga_sb[b.par][:, :].unsqueeze(1).broadcast_to([P, TT, D]),
                              ALU.mult).then_inc(s.y.sem, 1)

        def add_to_x(pool, pl, s, b):
            pool.wait_ge(*s.y(b))
            pool.tensor_tensor(xb(b), xb(b), y_sb[b.par][:, :, :], ALU.add).then_inc(s.x.sem, 1)

        def psum_free(pe, pl):
            if pl > 0:
                pe.wait_ge(*sigs[pl - 1].y(Idx(None, B - 1)))
            elif first > 0:
                mod_done(pe)

        def memory_free(eng, pl):
            if pl > 0:
                if first + pl == 1:
                    eng.wait_ge(*sigs[pl - 1].x(Idx(None, B - 1)))
            elif first > 0:
                mod_done(eng)

        def mod_done(eng):
            eng.wait_ge(ga_scr, 16 * LAYERS)
            eng.wait_ge(mod_sems["col"], LAYERS)

        begun = {}
        depth = lambda step, pl: (2 if step in (ln_stats, ln_rstd) else 1) + (1 if first + pl == 2 else 0)

        def ahead(step, eng, pl, i, k):
            b = i + k
            if b.reg is not None or b.off < B:
                if b.ok and (b.reg is not None or b.off >= begun.get((step, pl), 0)):
                    step(eng, pl, sigs[pl], b)
            elif i.off < B and pl + 1 < len(sigs) and b.off - B < depth(step, pl + 1):
                step(eng, pl + 1, sigs[pl + 1], Idx(None, b.off - B))
                begun[step, pl + 1] = b.off - B + 1

        M = mod_sems

        def mod_tensor(pe):
            pe.wait_ge(const_in, 16 * n_const)
            pe.wait_ge(M["silu"], 1)
            for i in range(LAYERS):
                pe.wait_ge(wmod_in[i % 2], 16 * (i // 2 + 1))
                if i:
                    pe.wait_ge(M["rows"], i)
                for n in range(3):
                    for kh in range(KH):
                        last_ = pe.matmul(PS[0:B, 1 + n, :], scT[:, i, kh, :], wmod[i % 2][:, kh, n * 512:(n + 1) * 512],
                                          start=kh == 0, stop=kh == KH - 1)
                last_.then_inc(M["rows_ps"], 1)
                pe.wait_ge(M["rows"], i + 1)
                if i:
                    pe.wait_ge(M["col"], i)
                for sub in range(2):
                    for c in range(2):
                        for kh in range(KH):
                            at = ((sub * 2 + c) * KH + kh) * B
                            last_ = pe.transpose(PS[:, 4, at:at + B],
                                                 mrow[i % 2][:, 3 * sub + c, kh * P:(kh + 1) * P], ident[0:B, 0:B])
                last_.then_inc(M["col_ps"], 1)

        def mod_scalar(act):
            act.wait_ge(const_in, 16 * n_const)
            act.activation(scT[:, :, :, :], cT[:, :, :, :], ACT.Silu).then_inc(M["silu"], 1)
            for i in range(LAYERS):
                act.wait_ge(M["rows_ps"], i + 1)
                if i >= 2:
                    act.wait_ge(M["col_ps"], i - 1)
                    act.wait_ge(M["both"], i - 1)
                act.activation(mrow[i % 2][:, :, :].rearrange("p s d -> p (s d)"), PS[0:B, 1:4, :].rearrange("p a n -> p (a n)"),
                               ACT.Copy).then_inc(M["rows"], 1)

        def mod_vector(dve):
            for i in range(LAYERS):
                dve.wait_ge(M["col_ps"], i + 1)
                cols = PS[:, 4, 0:8 * B].rearrange("p (s c k) -> p s c k", s=2, c=2)
                to = modT[:, 2 * i:2 * i + 2, :, :, :].rearrange("p s c k b -> p s c (k b)")
                dve.tensor_copy(to[:, :, 0, :], cols[:, :, 0, :])
                dve.tensor_scalar(to[:, :, 1, :], cols[:, :, 1, :], 1.0, None, ALU.add).then_inc(M["col"], 1)
                g = mrow[i % 2][:, 2:SECTIONS:3, :]
                if i:
                    dve.wait_ge(ga_scr, 16 * i)
                dve.scalar_tensor_tensor(gtmp[:, 0], g, -1.0, g, ALU.mult, ALU.max).then_inc(M["sign"], 1)
                dve.tensor_scalar(gtmp[:, 1], g, 0.0, 2.0, ALU.is_ge, ALU.mult).then_inc(M["both"], 1)
                dve.wait_ge(M["sign"], i + 1)
                dve.tensor_scalar(gtmp[:, 0], gtmp[:, 0], 0.25, None, ALU.max).then_inc(M["clip"], 1)
                dve.wait_ge(M["clip"], i + 1)
                dve.wait_ge(M["both"], i + 1)
                dve.scalar_tensor_tensor(gtmp[:, 2], gtmp[:, 1], -1.0, gtmp[:, 0], ALU.add, ALU.mult).then_inc(M["ga"], 1)

        def mod_sync(sp):
            for i in range(LAYERS):
                if i >= 2:
                    sp.wait_ge(M["rows_ps"], i - 1)
                    sp.dma_start(wmod[i % 2][:, :, :], ins["wmod"][i].rearrange("(k p) n -> p k n", p=P)).then_inc(wmod_in[i % 2], 16)
                sp.wait_ge(M["ga"], i + 1)
                sp.dma_start(ga_dram[2 * i:2 * i + 2].rearrange("s b d -> b s d"), gtmp[:, 2]).then_inc(ga_scr, 16)
            sp.wait_ge(ga_scr, 16 * LAYERS)

        LOOP0 = (4, 14)

        def bank(i, rows=P):
            return PS[0:rows, i, :]

        def kmask_ready(b):
            v = 16 * 8 * (b.off // 2 + 1)
            return kmask_in[b.par], v if b.reg is None else b.reg * 64 + v

        def l0a_tensor(pe, pl, s):
            psum_free(pe, pl)
            pe.wait_ge(w_in[0], 16 * len(weights[0]))
            pe.wait_ge(setup["wo"], 1)
            pe.wait_ge(setup["pads"], 1)

            def project(b):
                h = hT[b.par]
                pe.wait_ge(*s.h(b))
                if b.reg is not None or b.off >= 1:
                    pe.wait_ge(*s.gate(b - 1))
                    pe.wait_ge(*s.state(b - 1))
                for n, bk, done in (("q", 1, s.q_ps), ("k", 2, s.k_ps)):
                    for m in range(KH):
                        for kh in range(KH):
                            last_ = pe.matmul(bank(bk)[:, m * T:(m + 1) * T], l0_w[n][:, kh, m * P:(m + 1) * P],
                                              h[:, kh, :], start=kh == 0, stop=kh == 1)
                    last_.then_inc(done.sem, 1)
                pe.wait_ge(*s.q(b))
                for t in range(TT):
                    for kh in range(KH):
                        last_ = pe.matmul(bank(1)[:, t * D:(t + 1) * D], h[:, kh, t * P:(t + 1) * P],
                                          l0_w["v"][:, kh, :], start=kh == 0, stop=kh == 1)
                last_.then_inc(s.v_ps.sem, 1)
                pe.wait_ge(*s.k(b))
                for kh in range(KH):
                    pe.matmul(bank(2)[:, 0:D], h[:, kh, 0:P], l0_w["k"][:, kh, :], start=kh == 0, stop=kh == 1)
                for kh in range(KH):
                    last_ = pe.matmul(PS[0:HD, 2, D:D + T], l0_wg1[:, kh, :], h[:, kh, :], start=kh == 0, stop=kh == 1)
                last_.then_inc(s.hfree.sem, 1)

            def gate_state(b):
                pe.wait_ge(*s.kg(b))
                pe.wait_ge(*s.v(b))
                for t in range(TT):
                    last_ = pe.matmul(bank(1)[:, t * D:(t + 1) * D], g1T[b.par][:, t * P:(t + 1) * P], l0_wg2[:, :],
                                      start=True, stop=True)
                last_.then_inc(s.gate_ps.sem, 1)
                pe.wait_ge(*s.kdec(b))
                for m in range(KH):
                    last_ = pe.matmul(bank(2)[:, m * D:(m + 1) * D], kdec[b.par][:, m * P:(m + 1) * P],
                                      vpad[b.par][:, 0, 8 * m:8 * m + 8, :], start=True, stop=True)
                last_.then_inc(s.state_ps.sem, 1)

            def values(b, u):
                t, g = u // 4, u % 4
                pe.wait_ge(*s.prob(b, u + 1))
                if u == 0 and (b - 1).ok:
                    pe.wait_ge(*s.oT(b - 1))
                o = PS[:, 6 + g // 2, (g % 2 * 2 + t) * P:(g % 2 * 2 + t + 1) * P]
                if t == 1:
                    pe.wait_ge(*s.state(b))
                    pe.wait_ge(*s.qdec(b))
                    pe.matmul(o, state[b.par][:, g * P:(g + 1) * P], qdec[b.par][:, g // 2, :], start=True, stop=False)
                for j in range(4):
                    last_ = pe.matmul(o[32 * j:32 * j + 32], vpad[b.par][:, t, 4 * g + j, :], prob[u % 4][:, j, :],
                                      start=t == 0, stop=True)
                last_.then_inc(s.pv.sem, 1)

            def by_token(b):
                pe.wait_ge(*s.oT(b))
                for t in range(TT):
                    for g in range(4):
                        last_ = pe.transpose(bank(3 + t)[:, g * P:(g + 1) * P], oT[:, g, t, :], ident[:, :])
                    last_.then_inc(s.otok_ps.sem, 1)

            def normed_T(b):
                pe.wait_ge(*s.og(b))
                for kh in range(KH):
                    for t in range(TT):
                        last_ = pe.transpose(bank(3)[:, kh * T + t * P:kh * T + (t + 1) * P],
                                             og_sb[:, t, kh * P:(kh + 1) * P], ident[:, :])
                last_.then_inc(s.ogT_ps.sem, 1)

            def out(b):
                pe.wait_ge(*s.ogT(b))
                for t in range(TT):
                    for kh in range(KH):
                        last_ = pe.matmul(bank(4)[:, t * D:(t + 1) * D], ogT_sb[:, kh, t * P:(t + 1) * P],
                                          l0_wo_n[:, kh, :], start=kh == 0, stop=kh == 1)
                last_.then_inc(s.y_ps.sem, 1)

            def slot(i):
                if i.ok:
                    project(i)
                if (i - 2).ok:
                    pe.wait_ge(*s.prob(i - 2))
                    if (i - 3).ok:
                        pe.wait_ge(*s.y(i - 3))
                    by_token(i - 2)
                if (i - 1).ok:
                    c = i - 1
                    for u in range(8):
                        if u == 0 and (i - 2).ok:
                            pe.wait_ge(*s.u(i - 2))
                        t_scores(c, u)
                        if u >= 2:
                            values(c, u - 2)
                    values(c, 6)
                    values(c, 7)
                if (i - 2).ok:
                    if (i - 1).ok:
                        pe.wait_ge(*s.prob(i - 1))
                    normed_T(i - 2)
                if i.ok:
                    gate_state(i)
                ahead(ln_transpose, pe, pl, i, 1)
                if (i - 2).ok:
                    out(i - 2)

            def t_scores(b, u):
                t, g = u // 4, u % 4
                if u == 0:
                    pe.wait_ge(*kmask_ready(b))
                    pe.wait_ge(*s.q(b))
                if u < 3:
                    if (b - 1).ok:
                        pe.wait_ge(*s.prob(b - 1))
                else:
                    pe.wait_ge(*s.prob(b, u - 2))
                for j in range(4):
                    h = 4 * g + j
                    last_ = pe.matmul(bank(3 + u % 3)[:, j * P:(j + 1) * P], kmask[b.par][:, h % 8, h // 8, t * P:(t + 1) * P],
                                      qT[b.par][:, h // 8, t * P:(t + 1) * P], start=True, stop=True)
                last_.then_inc(s.score.sem, 1)

            slots(pe, slot, -1, LOOP0, B + 1)

        def l0a_scalar(act, pl, s):
            memory_free(act, pl)
            act.wait_ge(w_in[0], 16 * len(weights[0]))
            for h in range(HEADS):
                act.activation(l0_decay[:, h, :], l0_age[:, :], ACT.Exp, scale=l0_ld[:, h:h + 1])
            for m in range(KH):
                act.activation(l0_qdec[:, m, :], count[:, :], ACT.Exp, scale=l0_ld_col[:, m:m + 1])
            act.activation(l0_kdec[:, :], l0_ld_row[:, :], ACT.Exp, scale=left[:, 0:1]).then_inc(setup["exp"], 1)

            def slot(i):
                b = i
                if b.ok:
                    act.wait_ge(*s.q_ps(b))
                    if (b - 2).ok:
                        act.wait_ge(*s.score(b - 2))
                        act.wait_ge(*s.qdec(b - 2))
                    act.activation(qT[b.par][:, :, :].rearrange("p k t -> p (k t)"), bank(1), ACT.Silu).then_inc(s.q.sem, 1)
                    act.wait_ge(*s.k_ps(b))
                    if (b - 1).ok:
                        act.wait_ge(*kmask_ready(b - 1))
                    act.activation(kT[0][:, :, :].rearrange("p k t -> p (k t)"), bank(2), ACT.Silu).then_inc(s.k.sem, 1)
                    act.wait_ge(*s.v_ps(b))
                    if (b - 2).ok:
                        act.wait_ge(*s.pv(b - 2))
                    act.activation(vpad[b.par][:, :, :, 0:HD].rearrange("p t h e -> p (t h) e"),
                                   bank(1).rearrange("p (t e) -> p t e", e=HD), ACT.Silu).then_inc(s.v.sem, 1)
                    act.wait_ge(*s.hfree(b))
                    if (b - 1).ok:
                        act.wait_ge(*s.kdec(b - 1))
                    if (b - 2).ok:
                        act.wait_ge(*s.gate_ps(b - 2))
                    act.activation(kraw[0][:, :], bank(2)[:, 0:D], ACT.Silu)
                    act.activation(g1T[b.par][:, :], PS[0:HD, 2, D:D + T], ACT.Copy).then_inc(s.kg.sem, 1)
                if (i - 1).ok:
                    act.wait_ge(*s.pv(i - 1))
                    if (i - 2).ok:
                        act.wait_ge(*s.otok_ps(i - 2))
                    act.activation(oT[:, :, :, :].rearrange("p g t c -> p (g t c)"), PS[:, 6:8, :].rearrange("p a n -> p (a n)"),
                                   ACT.Copy).then_inc(s.oT.sem, 1)
                if (i - 2).ok:
                    act.wait_ge(*s.ogT_ps(i - 2))
                    if (i - 3).ok:
                        act.wait_ge(*s.y_ps(i - 3))
                    act.activation(ogT_sb[:, :, :].rearrange("p k t -> p (k t)"), bank(3), ACT.Copy).then_inc(s.ogT.sem, 1)
                if b.ok:
                    act.wait_ge(*s.gate_ps(b))
                    act.activation(gate[b.par][:, :, :].rearrange("p t d -> p (t d)"), bank(1), ACT.Tanh, scale=0.5)\
                       .then_inc(s.gate.sem, 1)
                ahead(modulate, act, pl, i, 1)

            slots(act, slot, -1, LOOP0, B + 1)

        def l0a_vector(dve, pl, s):
            memory_free(dve, pl)
            dve.wait_ge(ga_scr, 16 * LAYERS)
            for i in range(2):
                dve.memset(kmask[i][:, :, :, :], 0.0)
                last_ = dve.memset(vpad[i][:, :, :, :], 0.0)
            last_.then_inc(setup["pads"], 1)
            dve.wait_ge(w_in[0], 16 * len(weights[0]))
            for m in range(KH):
                last_ = dve.tensor_scalar(l0_wo_n[:, m, :], l0_w["o"][:, m, :], l0_nw[:, m:m + 1], HD ** 0.5, ALU.mult, ALU.mult)
            last_.then_inc(setup["wo"], 1)
            dve.wait_ge(setup["exp"], 1)
            dve.tensor_tensor(l0_decay[:, :, :], l0_decay[:, :, :], causal[:, :].unsqueeze(1).broadcast_to([P, HEADS, P]),
                              ALU.mult).then_inc(setup["decay"], 1)

            dve.wait_ge(idx_in, 16)

            def slot(i):
                ahead(ln_stats, dve, pl, i, 2)
                if i.ok:
                    if (i - 1).ok:
                        dve.wait_ge(*s.picked(i - 1))
                    dve.tensor_scalar(l0_pick[:, :], l0_idx[:, :], iota[:, bass.ds(i.n, 1)], l0_lut[:, bass.ds(i.n, 1)],
                                      ALU.is_equal, ALU.mult).then_inc(s.pick.sem, 1)
                if (i - 2).ok:
                    b = i - 2
                    for t in range(TT):
                        dve.wait_ge(*s.otok_ps(b, t + 1))
                        if t == 0:
                            dve.wait_ge(*s.gate(b))
                            if (b - 1).ok:
                                dve.wait_ge(*s.sq(b - 1))
                        dve.scalar_tensor_tensor(u_sb[:, t, :].rearrange("p (h e) -> p h e", e=HD),
                                                 gate[b.par][:, t, :].rearrange("p (h e) -> p h e", e=HD), 1.0,
                                                 bank(3 + t).rearrange("p (h e) -> p h e", e=32)[:, :, 0:HD],
                                                 ALU.add, ALU.mult).then_inc(s.u.sem, 1)
                if (i - 1).ok:
                    b = i - 1
                    for u in range(8):
                        dve.wait_ge(*s.score(b, u + 1))
                        if u == 0:
                            dve.wait_ge(setup["decay"], 1)
                        if u < 4:
                            if (b - 1).ok:
                                dve.wait_ge(*s.pv(b - 1, u + 5))
                        else:
                            dve.wait_ge(*s.pv(b, u - 3))
                        g = u % 4
                        dve.tensor_tensor(prob[u % 4][:, :, :], bank(3 + u % 3).rearrange("p (j c) -> p j c", j=4),
                                          l0_decay[:, 4 * g:4 * g + 4, :], ALU.mult).then_inc(s.prob.sem, 1)
                        if u == 2 and (i - 2).ok:
                            mean_square(i - 2)
                        if u == 6 and (i - 2).ok:
                            norm(i - 2)
                if not (i - 1).ok and (i - 2).ok:
                    mean_square(i - 2)
                    norm(i - 2)
                ahead(ln_apply, dve, pl, i, 1)
                if i.ok:
                    dve.wait_ge(*s.state_ps(i))
                    if (i - 2).ok:
                        dve.wait_ge(*s.pv(i - 2))
                    dve.tensor_tensor(state[i.par][:, :], bank(2), l0_own[:, :], ALU.mult).then_inc(s.state.sem, 1)
                if (i - 2).ok:
                    dve.wait_ge(*s.y_ps(i - 2))
                    gated(dve, pl, s, i - 2, bank(4).rearrange("p (t d) -> p t d", t=TT))

            def mean_square(b):
                dve.wait_ge(*s.sq(b))
                if (b - 1).ok:
                    dve.wait_ge(*s.rn(b - 1))
                dve.tensor_reduce(ms_sb[:, :], sq_sb[:, :, :].rearrange("p t (h e) -> p (t h) e", e=HD), AX.X, ALU.add)\
                   .then_inc(s.ms.sem, 1)

            def norm(b):
                dve.wait_ge(*s.rn(b))
                if (b - 1).ok:
                    dve.wait_ge(*s.ogT_ps(b - 1))
                dve.tensor_tensor(og_sb[:, :, :].rearrange("p t (h e) -> p (t h) e", e=HD),
                                  u_sb[:, :, :].rearrange("p t (h e) -> p (t h) e", e=HD),
                                  ms_sb[:, :].unsqueeze(2).broadcast_to([P, TT * HEADS, HD]), ALU.mult).then_inc(s.og.sem, 1)

            slots(dve, slot, -2, LOOP0, B + 1)

        def l0a_pool(pool, pl, s):
            memory_free(pool, pl)
            pool.memset(lut_w[:, :], 0.0).then_inc(setup["zero"], 1)
            pool.wait_ge(setup["zero"], 1)
            pool.wait_ge(setup["exp"], 1)

            def slot(i):
                ahead(ln_rstd, pool, pl, i, 2)
                if (i - 2).ok:
                    b = i - 2
                    pool.wait_ge(*s.u(b))
                    pool.tensor_tensor(sq_sb[:, :, :], u_sb[:, :, :], u_sb[:, :, :], ALU.mult).then_inc(s.sq.sem, 1)
                    pool.wait_ge(*s.ms(b))
                    pool.tensor_tensor(ms_sb[:, :], ms_sb[:, :], eps_sum[:, 0:TT * HEADS], ALU.add).then_inc(s.rn_raw.sem, 1)
                    pool.wait_ge(*s.rn_raw(b))
                    pool.tensor_tensor(ms_sb[:, :], ms_sb[:, :], half[:, 0:TT * HEADS], ALU.pow).then_inc(s.rn.sem, 1)
                if i.ok:
                    pool.wait_ge(*s.q(i))
                    if (i - 2).ok:
                        pool.wait_ge(*s.pv(i - 2))
                    pool.tensor_tensor(qdec[i.par][:, :, :], qT[i.par][:, :, P:T], l0_qdec[:, :, :], ALU.mult)\
                        .then_inc(s.qdec.sem, 1)
                    pool.wait_ge(*s.kg(i))
                    pool.tensor_tensor(kdec[i.par][:, :], kraw[0][:, :], l0_kdec[:, :], ALU.mult).then_inc(s.kdec.sem, 1)
                if i.ok:
                    pool.wait_ge(*s.pick(i))
                    pool.tensor_tensor(lut_w[:, :], lut_w[:, :], l0_pick[:, :], ALU.add).then_inc(s.picked.sem, 1)
                if (i - 2).ok:
                    add_to_x(pool, pl, s, i - 2)

            slots(pool, slot, -2, LOOP0, B + 1)

        def l0a_sync(sp, pl, s, i):
            if i.ok:
                sp.wait_ge(*s.k(i))
                for r in range(8):
                    sp.dma_start(kmask[i.par][16 * r:16 * r + 16, r, :, :], kT[0][16 * r:16 * r + 16, :, :])\
                      .then_inc(kmask_in[i.par], 16)

        gate_w = lut_w[:, 0:KH * INTER].rearrange("p (k n) -> p k n", k=KH)
        up_w = lut_w[:, KH * INTER:2 * KH * INTER].rearrange("p (k n) -> p k n", k=KH)
        down_w = lut_w[:, 2 * KH * INTER:].rearrange("p (m d) -> p m d", m=FT)
        rows_of = lambda m: min(P, INTER - m * P)

        def l0f_tensor(pe, pl, s):
            psum_free(pe, pl)

            def slot(i):
                if i.ok:
                    pe.wait_ge(*s.h(i))
                    for m in range(FT):
                        r = rows_of(m)
                        if m >= 3:
                            pe.wait_ge(*s.hid(i, m - 2))
                        elif (i - 1).ok:
                            pe.wait_ge(*s.hid(i - 1))
                        for n, w in enumerate((gate_w, up_w)):
                            for kh in range(KH):
                                last_ = pe.matmul(PS[0:r, 1 + m % 3, n * T:(n + 1) * T], w[:, kh, m * P:m * P + r],
                                                  hT[i.par][:, kh, :], start=kh == 0, stop=kh == 1)
                        if m == FT - 1:
                            last_.then_inc(s.hfree.sem, 1)
                        else:
                            last_.then_inc(s.gate_ps.sem, 1)
                ahead(ln_transpose, pe, pl, i, 1)
                if (i - 1).ok:
                    b = i - 1
                    pe.wait_ge(*s.hid(b))
                    if (b - 1).ok:
                        pe.wait_ge(*s.y(b - 1))
                    for t in range(TT):
                        for m in range(FT):
                            r = rows_of(m)
                            last_ = pe.matmul(bank(4)[:, t * D:(t + 1) * D], hid[b.par][0:r, m, t * P:(t + 1) * P],
                                              down_w[0:r, m, :], start=m == 0, stop=m == FT - 1)
                    last_.then_inc(s.y_ps.sem, 1)

            slots(pe, slot, -1, (4, 14), B)

        def l0f_wait_gu(eng, s, b, m):
            if m == FT - 1:
                eng.wait_ge(*s.hfree(b))
            else:
                eng.wait_ge(*s.gate_ps(b, m + 1))

        def l0f_scalar(act, pl, s):
            memory_free(act, pl)

            def slot(i):
                if i.ok:
                    for m in range(FT):
                        r = rows_of(m)
                        l0f_wait_gu(act, s, i, m)
                        if m >= 3:
                            act.wait_ge(*s.hid(i, m - 2))
                        elif (i - 1).ok:
                            act.wait_ge(*s.hid(i - 1))
                        act.activation(act_sb[m % 3][0:r, :], PS[0:r, 1 + m % 3, 0:T], ACT.Silu).then_inc(s.gate.sem, 1)
                        if m == 2:
                            ahead(modulate, act, pl, i, 1)
                else:
                    ahead(modulate, act, pl, i, 1)

            slots(act, slot, -1, (4, 14), B - 1)

        def l0f_vector(dve, pl, s):
            memory_free(dve, pl)

            def slot(i):
                ahead(ln_stats, dve, pl, i, 2)
                if not i.ok:
                    ahead(ln_apply, dve, pl, i, 1)
                if i.ok:
                    for m in range(FT):
                        r = rows_of(m)
                        dve.wait_ge(*s.gate(i, m + 1))
                        if m == 0 and (i - 2).ok:
                            dve.wait_ge(*s.y_ps(i - 2))
                        dve.tensor_tensor(hid[i.par][0:r, m, :], act_sb[m % 3][0:r, :], PS[0:r, 1 + m % 3, T:2 * T],
                                          ALU.mult).then_inc(s.hid.sem, 1)
                        if m == 0:
                            ahead(ln_apply, dve, pl, i, 1)
                if (i - 1).ok:
                    dve.wait_ge(*s.y_ps(i - 1))
                    gated(dve, pl, s, i - 1, bank(4).rearrange("p (t d) -> p t d", t=TT))

            slots(dve, slot, -2, (4, 14), B)

        def l3a_tensor(pe, pl, s):
            psum_free(pe, pl)
            pe.wait_ge(w_in[6], 16 * len(weights[6]))

            def slot(i):
                if i.ok:
                    pe.wait_ge(*s.h(i))
                    for n, done, free in ((0, s.q_ps, s.q), (1, s.k_ps, s.k), (2, s.hfree, s.v)):
                        if (i - 1).ok:
                            pe.wait_ge(*free(i - 1))
                        for m in range(KH):
                            for kh in range(KH):
                                last_ = pe.matmul(bank(1 + n)[:, m * T:(m + 1) * T],
                                                  l3_wqkv[:, kh, n * D + m * P:n * D + (m + 1) * P],
                                                  hT[i.par][:, kh, :], start=kh == 0, stop=kh == 1)
                        last_.then_inc(done.sem, 1)
                ahead(ln_transpose, pe, pl, i, 1)
                if (i - 1).ok:
                    b = i - 1
                    pe.wait_ge(*s.qs(b))
                    if (b - 1).ok:
                        pe.wait_ge(*s.clip(b - 1))
                    for m in range(KH):
                        last_ = pe.matmul(bank(4)[:, m * T:(m + 1) * T], l3_same[:, :], l3_qs[:, m, :], start=True, stop=True)
                    last_.then_inc(s.den_ps.sem, 1)
                if (i - 2).ok:
                    b = i - 2
                    pe.wait_ge(*s.o(b))
                    if (b - 1).ok:
                        pe.wait_ge(*s.y(b - 1))
                    for t in range(TT):
                        for kh in range(KH):
                            last_ = pe.matmul(bank(5)[:, t * D:(t + 1) * D], l3_num[b.par][:, kh, t * P:(t + 1) * P],
                                              l3_wo[:, kh, :], start=kh == 0, stop=kh == 1)
                    last_.then_inc(s.y_ps.sem, 1)

            slots(pe, slot, -1, (6, 14), B + 1)

        def l3a_scalar(act, pl, s):
            memory_free(act, pl)
            act.wait_ge(w_in[6], 16 * len(weights[6]))
            act.activation(l3_dec[:, :], l3_dec[:, :], ACT.Exp, scale=-1.0).then_inc(setup["dexp"], 1)

            def slot(i):
                if i.ok:
                    for n, ps, done, r, e in ((0, s.q_ps, s.eq, l3_r[0], l3_e[0]), (1, s.k_ps, s.ek, l3_r[1], l3_e[1])):
                        act.wait_ge(*ps(i))
                        if (i - 1).ok:
                            act.wait_ge(*(s.q, s.k)[n](i - 1))
                        act.activation(r[:, :], bank(1 + n), ACT.Relu)
                        act.activation(e[:, :], bank(1 + n), ACT.Exp).then_inc(done.sem, 1)
                ahead(modulate, act, pl, i, 1)

            slots(act, slot, -1, (6, 14), B - 1)

        def l3a_vector(dve, pl, s):
            memory_free(dve, pl)

            def slot(i):
                ahead(ln_stats, dve, pl, i, 2)
                ahead(ln_apply, dve, pl, i, 1)
                if i.ok:
                    for n, done, ready in ((0, s.q, s.eq), (1, s.k, s.ek)):
                        dve.wait_ge(*ready(i))
                        if n == 0 and (i - 1).ok:
                            dve.wait_ge(*s.num(i - 1))
                            dve.wait_ge(*s.qs(i - 1))
                        dve.scalar_tensor_tensor(l3_qk[n][:, :, :].rearrange("p k t -> p (k t)"), l3_e[n][:, :], 1.0, l3_r[n][:, :],
                                                 ALU.min, ALU.add).then_inc(done.sem, 1)
                    dve.wait_ge(*s.k(i))
                    for m in range(KH):
                        last_ = dve.tensor_tensor_scan(l3_sk[:, m, :], l3_dec[:, m:m + 1].broadcast_to([P, T]), l3_qk[1][:, m, :],
                                                       0.0, ALU.mult, ALU.add)
                    last_.then_inc(s.sumk.sem, 1)
                    dve.wait_ge(*s.hfree(i))
                    dve.tensor_tensor(l3_kv[:, :, :].rearrange("p k t -> p (k t)"), l3_qk[1][:, :, :].rearrange("p k t -> p (k t)"),
                                      bank(3), ALU.mult).then_inc(s.v.sem, 1)
                    dve.wait_ge(*s.v(i))
                    for m in range(KH):
                        last_ = dve.tensor_tensor_scan(l3_skv[:, m, :], l3_dec[:, m:m + 1].broadcast_to([P, T]), l3_kv[:, m, :],
                                                       0.0, ALU.mult, ALU.add)
                    last_.then_inc(s.scan.sem, 1)
                if (i - 1).ok:
                    b = i - 1
                    dve.wait_ge(*s.den_ps(b))
                    if (b - 1).ok:
                        dve.wait_ge(*s.o(b - 1))
                    dve.tensor_scalar(l3_den[:, :], bank(4), EPS_DEN, None, ALU.max).then_inc(s.clip.sem, 1)
                    dve.wait_ge(*s.clip(b))
                    dve.reciprocal(l3_den[:, :], l3_den[:, :]).then_inc(s.rden.sem, 1)
                if (i - 2).ok:
                    dve.wait_ge(*s.y_ps(i - 2))
                    gated(dve, pl, s, i - 2, bank(5).rearrange("p (t d) -> p t d", t=TT))

            dve.wait_ge(w_in[6], 16 * len(weights[6]))
            dve.wait_ge(setup["dexp"], 1)
            dve.tensor_scalar(l3_dec[:, :], l3_dec[:, :], 1.0, None, ALU.add).then_inc(setup["dsum"], 1)
            dve.wait_ge(setup["dsum"], 1)
            dve.reciprocal(l3_dec[:, :], l3_dec[:, :]).then_inc(setup["ddec"], 1)
            dve.wait_ge(setup["ddec"], 1)
            slots(dve, slot, -2, (6, 14), B + 1)

        def l3a_pool(pool, pl, s):
            memory_free(pool, pl)

            def slot(i):
                ahead(ln_rstd, pool, pl, i, 2)
                if i.ok:
                    b = i
                    pool.wait_ge(*s.sumk(b))
                    if (b - 1).ok:
                        pool.wait_ge(*s.den_ps(b - 1))
                    pool.tensor_tensor(l3_qs[:, :, :], l3_qk[0][:, :, :], l3_sk[:, :, :], ALU.mult).then_inc(s.qs.sem, 1)
                    pool.wait_ge(*s.scan(b))
                    if (b - 2).ok:
                        pool.wait_ge(*s.y_ps(b - 2))
                    pool.tensor_tensor(l3_num[b.par][:, :, :], l3_qk[0][:, :, :], l3_skv[:, :, :], ALU.mult).then_inc(s.num.sem, 1)
                if (i - 1).ok:
                    b = i - 1
                    pool.wait_ge(*s.rden(b))
                    pool.wait_ge(*s.num(b))
                    o = l3_num[b.par][:, :, :].rearrange("p k t -> p (k t)")
                    pool.tensor_tensor(o, o, l3_den[:, :], ALU.mult).then_inc(s.o.sem, 1)
                if (i - 2).ok:
                    add_to_x(pool, pl, s, i - 2)

            slots(pool, slot, -2, (6, 14), B + 1)

        BIG = 3e38

        def logits(pe, pl, s, b, w):
            pe.wait_ge(*s.h(b))
            if (b - 1).ok:
                pe.wait_ge(*s.lcopy(b - 1))
            for t in range(TT):
                for kh in range(KH):
                    last_ = pe.matmul(bank(5)[:, t * E:(t + 1) * E], hT[b.par][:, kh, t * P:(t + 1) * P], w[:, kh, :],
                                      start=kh == 0, stop=kh == 1)
            last_.then_inc(s.logit_ps.sem, 1)

        def first_of(dve, link, vals, top, one):
            link(dve.tensor_reduce(top, vals, AX.X, ALU.max))
            link(dve.tensor_tensor(rt_eq[:, :, :], vals, top.unsqueeze(2).broadcast_to([P, TT, E]), ALU.is_equal))
            link(dve.tensor_tensor(rt_eq[:, :, :], rt_eq[:, :, :], rank[:, :, :], ALU.mult))
            link(dve.tensor_reduce(rt_r[:, :], rt_eq[:, :, :], AX.X, ALU.max))
            link(dve.tensor_tensor(one, rank[:, :, :], rt_r[:, :].unsqueeze(2).broadcast_to([P, TT, E]), ALU.is_equal))

        def route(dve, pl, s, b):
            n = [0]

            def link(ins):
                n[0] += 1
                ins.then_inc(s.rt.sem, 1)
                dve.wait_ge(*s.rt(b, n[0]))

            dve.wait_ge(*s.logit_ps(b))
            dve.tensor_copy(rt_l[:, :, :], bank(5)[:, 0:TT * E].rearrange("p (t e) -> p t e", t=TT)).then_inc(s.lcopy.sem, 1)
            dve.wait_ge(*s.lcopy(b))
            first_of(dve, link, rt_l[:, :, :], rt_m[:, 0, :], rt_o[:, 0])
            link(dve.scalar_tensor_tensor(rt_l[:, :, :], rt_o[:, 0], -BIG, rt_l[:, :, :], ALU.mult, ALU.add))
            first_of(dve, link, rt_l[:, :, :], rt_m[:, 1, :], rt_o[:, 1])
            if (b - 1).ok:
                dve.wait_ge(*s.e(b - 1))
            dve.tensor_tensor(rt_d[:, :], rt_m[:, 1, :], rt_m[:, 0, :], ALU.subtract).then_inc(s.ed.sem, 1)
            dve.wait_ge(*s.e(b))
            link(dve.tensor_scalar(rt_w[:, 0, :], rt_e[:, :], 1.0, None, ALU.add))
            link(dve.reciprocal(rt_w[:, 0, :], rt_w[:, 0, :]))
            link(dve.tensor_tensor(rt_w[:, 1, :], rt_e[:, :], rt_w[:, 0, :], ALU.mult))
            for m in range(2):
                link(dve.tensor_tensor(rt_o[:, m], rt_o[:, m], rt_w[:, m, :].unsqueeze(2).broadcast_to([P, TT, E]), ALU.mult))
            dve.tensor_tensor(rt_g[b.par][:, :, :], rt_o[:, 0], rt_o[:, 1], ALU.add).then_inc(s.g.sem, 1)

        def route_exp(act, pl, s, b):
            act.wait_ge(*s.ed(b))
            if PHASES[first + pl] == "L3_ffn":
                act.activation(l3_ee[:, :, :], l3_ez[:, :, :], ACT.Exp).then_inc(s.e.sem, 1)
            else:
                act.activation(rt_e[:, :], rt_d[:, :], ACT.Exp).then_inc(s.e.sem, 1)

        def gates_T(pe, pl, s, b, bk):
            pe.wait_ge(*s.g(b))
            if (b - 1).ok:
                pe.wait_ge(*s.gT(b - 1))
            for t in range(TT):
                last_ = pe.transpose(PS[0:E, bk, t * P:(t + 1) * P], rt_g[b.par][:, t, :], ident[:, :])
            last_.then_inc(s.gT_ps.sem, 1)

        def gates_T_copy(act, pl, s, b, bk):
            act.wait_ge(*s.gT_ps(b))
            act.activation(rt_gT[:, :], PS[0:E, bk, 0:T], ACT.Copy).then_inc(s.gT.sem, 1)

        def l1f_tensor(pe, pl, s):
            psum_free(pe, pl)
            pe.wait_ge(w_in[3], 16 * len(weights[3]))

            def slot(i):
                b = i
                if b.ok:
                    for u in range(8):
                        t, e2 = u % 2, u // 2
                        if u >= 4:
                            pe.wait_ge(*s.acc(b, 4 * (e2 - 2) + 3 + t))
                        elif (b - 1).ok:
                            pe.wait_ge(*s.acc(b - 1, 4 * (e2 + 2) + 3 + t))
                        for kh in range(KH):
                            last_ = pe.matmul(bank(1 + u % 4), hT[b.par][:, kh, t * P:(t + 1) * P],
                                              l1_we[:, kh, 2 * e2:2 * e2 + 2, :], start=kh == 0, stop=kh == 1)
                        last_.then_inc((s.hfree if u == 7 else s.unit_ps).sem, 1)
                        if u == 2:
                            gates_T(pe, pl, s, b, 6)
                        if u == 3:
                            pe.wait_ge(*s.gT(b))
                            if (b - 1).ok:
                                pe.wait_ge(*s.acc0(b - 1))
                            for tt in range(TT):
                                last_ = pe.matmul(bank(7)[:, tt * D:(tt + 1) * D], rt_gT[:, tt * P:(tt + 1) * P], l1_eb[:, :],
                                                  start=True, stop=True)
                            last_.then_inc(s.bias_ps.sem, 1)
                        if u == 5:
                            ahead(ln_transpose, pe, pl, i, 1)
                else:
                    ahead(ln_transpose, pe, pl, i, 1)
                if (i + 1).ok:
                    logits(pe, pl, s, i + 1, l1_gw)

            slots(pe, slot, -1, (4, 14), B - 1)

        def l1f_scalar(act, pl, s):
            memory_free(act, pl)

            def slot(i):
                b = i
                if b.ok:
                    gates_T_copy(act, pl, s, b, 6)
                    act.wait_ge(*s.bias_ps(b))
                    if (b - 2).ok:
                        act.wait_ge(*s.y(b - 2))
                    act.activation(l1_acc[b.par][:, :, :].rearrange("p t d -> p (t d)"), bank(7), ACT.Copy).then_inc(s.acc0.sem, 1)
                ahead(modulate, act, pl, i, 1)
                if (i + 1).ok:
                    route_exp(act, pl, s, i + 1)

            slots(act, slot, -1, (4, 14), B - 1)

        def l1f_vector(dve, pl, s):
            memory_free(dve, pl)
            dve.wait_ge(w_in[3], 16 * len(weights[3]))

            def slot(i):
                b = i
                ahead(ln_stats, dve, pl, i, 2)
                if b.ok:
                    n = 0
                    for q in range(4):
                        for e in range(2):
                            for t in range(TT):
                                if n == 0:
                                    dve.wait_ge(*s.acc0(b))
                                if e == 0:
                                    u = 2 * q + t
                                    if u == 7:
                                        dve.wait_ge(*s.hfree(b))
                                    else:
                                        dve.wait_ge(*s.unit_ps(b, u + 1))
                                if n >= 2:
                                    dve.wait_ge(*s.acc(b, n - 1))
                                x_ = 2 * q + e
                                dve.scalar_tensor_tensor(l1_acc[b.par][:, t, :], bank(1 + (2 * q + t) % 4)[:, e * D:(e + 1) * D],
                                                         rt_g[b.par][:, t, x_:x_ + 1], l1_acc[b.par][:, t, :],
                                                         ALU.mult, ALU.add).then_inc(s.acc.sem, 1)
                                n += 1
                        if q == 1:
                            ahead(ln_apply, dve, pl, i, 1)
                else:
                    ahead(ln_apply, dve, pl, i, 1)
                if (i + 1).ok:
                    route(dve, pl, s, i + 1)

            slots(dve, slot, -2, (4, 14), B - 1)

        def gate_on_pool(pool, pl, s, b, src, done):
            pool.wait_ge(*done)
            pool.wait_ge(*ga_loaded(pl, b))
            if has(pl, b - 1):
                pool.wait_ge(*s.x(b - 1))
            pool.tensor_tensor(y_sb[b.par][:, :, :], src, ga_sb[b.par][:, :].unsqueeze(1).broadcast_to([P, TT, D]),
                               ALU.mult).then_inc(s.y.sem, 1)
            add_to_x(pool, pl, s, b)

        def l1f_pool(pool, pl, s):
            memory_free(pool, pl)

            def slot(i):
                ahead(ln_rstd, pool, pl, i, 2)
                if i.ok:
                    gate_on_pool(pool, pl, s, i, l1_acc[i.par][:, :, :], s.acc(i))

            slots(pool, slot, -2, (4, 14), B - 1)

        def l2f_tensor(pe, pl, s):
            psum_free(pe, pl)
            pe.wait_ge(w_in[5], 16 * len(weights[5]))

            def slot(i):
                b = i
                if b.ok:
                    h = hT[b.par]
                    if (b - 1).ok:
                        pe.wait_ge(*s.ax(b - 1))
                    for kh in range(KH):
                        last_ = pe.matmul(bank(1)[:, 0:T], l2_la[:, kh, :], h[:, kh, :], start=kh == 0, stop=kh == 1)
                    last_.then_inc(s.ax_ps.sem, 1)
                    gates_T(pe, pl, s, b, 6)
                ahead(ln_transpose, pe, pl, i, 1)
                if b.ok:
                    pe.wait_ge(*s.gT(b))
                    pe.matmul(bank(2)[:, 0:T], l2_sel[:, :], rt_gT[:, :], start=True, stop=True).then_inc(s.wx_ps.sem, 1)
                    pe.wait_ge(*s.ax(b))
                    if (b - 2).ok:
                        pe.wait_ge(*s.y(b - 2))
                    for t in range(TT):
                        o = bank(3 + b.par)[:, t * D:(t + 1) * D]
                        for kh in range(KH):
                            pe.matmul(o, h[:, kh, t * P:(t + 1) * P], l2_w[:, kh, :], start=kh == 0, stop=False)
                        last_ = pe.matmul(o, l2_ax[b.par][:, t * P:(t + 1) * P], l2_lb[:, :], start=False, stop=True)
                    last_.then_inc(s.hfree.sem, 1)
                if (i + 1).ok:
                    logits(pe, pl, s, i + 1, l2_rw)

            slots(pe, slot, -1, (4, 14), B - 1)

        def l2f_scalar(act, pl, s):
            memory_free(act, pl)

            def slot(i):
                b = i
                if b.ok:
                    gates_T_copy(act, pl, s, b, 6)
                    act.wait_ge(*s.wx_ps(b))
                    if (b - 1).ok:
                        act.wait_ge(*s.ax(b - 1))
                    act.activation(l2_wx[:, :], bank(2)[:, 0:T], ACT.Copy, scale=LORA_SCALE).then_inc(s.wx.sem, 1)
                ahead(modulate, act, pl, i, 1)
                if (i + 1).ok:
                    route_exp(act, pl, s, i + 1)

            slots(act, slot, -1, (4, 14), B - 1)

        def l2f_vector(dve, pl, s):
            memory_free(dve, pl)
            dve.wait_ge(w_in[5], 16 * len(weights[5]))

            def slot(i):
                b = i
                ahead(ln_stats, dve, pl, i, 2)
                ahead(ln_apply, dve, pl, i, 1)
                if b.ok:
                    dve.wait_ge(*s.wx(b))
                    if (b - 2).ok:
                        dve.wait_ge(*s.hfree(b - 2))
                    dve.tensor_tensor(l2_ax[b.par][:, :], bank(1)[:, 0:T], l2_wx[:, :], ALU.mult).then_inc(s.ax.sem, 1)
                if (b - 1).ok:
                    dve.wait_ge(*s.hfree(b - 1))
                    gated(dve, pl, s, b - 1, bank(3 + (b - 1).par).rearrange("p (t d) -> p t d", t=TT))
                if (i + 1).ok:
                    route(dve, pl, s, i + 1)

            slots(dve, slot, -2, (4, 14), B)

        def l3f_tensor(pe, pl, s):
            psum_free(pe, pl)
            pe.wait_ge(w_in[7], 16 * len(weights[7]))
            for kh in range(KH):
                pe.matmul(PS[0:NS, 7, 0:E], l3_sw[:, kh, :], l3_md[:, kh, :], start=kh == 0, stop=kh == 1)
            for kh in range(KH):
                last_ = pe.matmul(PS[0:NS + E, 7, 8:8 + E], l3_up[:, kh, :], l3_db[:, kh, :], start=kh == 0, stop=kh == 1)
            last_.then_inc(setup["f_ps"], 1)
            pe.wait_ge(setup["f_set"], 1)

            def slot(i):
                if (i - 2).ok:
                    b = i - 2
                    gates_T(pe, pl, s, b, 6)
                    pe.wait_ge(*s.gT(b))
                    if (b - 1).ok:
                        pe.wait_ge(*s.zz(b - 1))
                    pe.matmul(PS[0:NS + E, 7, 0:T], l3_e72[:, :], rt_gT[:, :], start=True, stop=True).then_inc(s.se_ps.sem, 1)
                if (i - 1).ok:
                    b = i - 1
                    pe.wait_ge(*s.z(b))
                    if (b - 1).ok:
                        pe.wait_ge(*s.ed(b - 1))
                    for t in range(TT):
                        last_ = pe.matmul(bank(5)[:, t * E:(t + 1) * E], l3_z[:, t * P:(t + 1) * P], ident[0:E, 0:E],
                                          start=True, stop=True)
                    last_.then_inc(s.zT_ps.sem, 1)
                if i.ok:
                    b = i
                    h = hT[b.par]
                    pe.wait_ge(*s.h(b))
                    if (b - 1).ok:
                        pe.wait_ge(*s.mx(b - 1))
                        pe.wait_ge(*s.ht(b - 1))
                    for kh in range(KH):
                        pe.matmul(PS[0:NS, 1, 0:T], l3_sw[:, kh, :], h[:, kh, :], start=kh == 0, stop=kh == 1)
                    for kh in range(KH):
                        last_ = pe.matmul(PS[0:NS + E, 1, T:2 * T], l3_up[:, kh, :], h[:, kh, :], start=kh == 0, stop=kh == 1)
                    last_.then_inc(s.p_ps.sem, 1)
                    for t in range(TT):
                        for kh in range(KH):
                            last_ = pe.transpose(bank(2)[:, t * D + kh * P:t * D + (kh + 1) * P], h[:, kh, t * P:(t + 1) * P], ident[:, :])
                    last_.then_inc(s.htok_ps.sem, 1)
                if (i - 2).ok:
                    b = i - 2
                    pe.wait_ge(*s.zz(b))
                    if (b - 1).ok:
                        pe.wait_ge(*s.y1(b - 1))
                    for t in range(TT):
                        last_ = pe.matmul(bank(4)[:, t * D:(t + 1) * D], l3_zz[:, t * P:(t + 1) * P], l3_dg[:, :],
                                          start=True, stop=True)
                    last_.then_inc(s.y_ps.sem, 1)
                ahead(ln_transpose, pe, pl, i, 1)
                if i.ok:
                    b = i
                    h = hT[b.par]
                    pe.wait_ge(*s.sq(b))
                    if (b - 1).ok:
                        pe.wait_ge(*s.z(b - 1))
                    pe.matmul(PS[0:E, 3, 0:T], l3_blk[:, :], l3_sq[:, :], start=True, stop=True)
                    for kh in range(KH):
                        pe.matmul(PS[0:E, 3, T:2 * T], l3_one[:, :], l3_hsq[:, kh, :], start=kh == 0, stop=False)
                    for kh in range(KH):
                        last_ = pe.matmul(PS[0:E, 3, T:2 * T], l3_m2[:, kh, :], h[:, kh, :], start=False, stop=kh == 1)
                    last_.then_inc(s.hfree.sem, 1)

            slots(pe, slot, -1, (4, 14), B + 1)

        def l3f_scalar(act, pl, s):
            memory_free(act, pl)
            act.wait_ge(setup["f_set"], 1)

            def slot(i):
                if (i - 2).ok:
                    gates_T_copy(act, pl, s, i - 2, 6)
                if i.ok:
                    b = i
                    act.wait_ge(*s.h(b))
                    if (b - 1).ok:
                        act.wait_ge(*s.hfree(b - 1))
                    act.activation(l3_hsq[:, :, :], hT[b.par][:, :, :], ACT.Square)
                    act.wait_ge(*s.p_ps(b))
                    act.activation(l3_sq[0:NS, :], PS[0:NS, 1, 0:T], ACT.Square, bias=l3_c1[:, 0:1]).then_inc(s.sq.sem, 1)
                    if (b - 2).ok:
                        act.wait_ge(*s.zz(b - 2))
                        act.wait_ge(*s.y1(b - 2))
                    act.activation(l3_mx[b.par][:, :], PS[0:NS + E, 1, T:2 * T], ACT.Identity, bias=l3_c0[:, 0:1])\
                       .then_inc(s.mx.sem, 1)
                    act.wait_ge(*s.htok_ps(b))
                    act.activation(l3_ht[b.par][:, :, :].rearrange("p t d -> p (t d)"), bank(2), ACT.Copy).then_inc(s.ht.sem, 1)
                if (i - 1).ok:
                    route_exp(act, pl, s, i - 1)
                ahead(modulate, act, pl, i, 1)

            slots(act, slot, -1, (4, 14), B + 1)

        def l3f_vector(dve, pl, s):
            memory_free(dve, pl)
            dve.wait_ge(w_in[7], 16 * len(weights[7]))
            dve.wait_ge(setup["f_ps"], 1)
            f = setup["f_step"]
            dve.memset(l3_sq[NS:P, :], 0.0)
            dve.tensor_tensor(l3_g1[:, :], PS[0:NS, 7, 0:E], l3_blk[0:NS, :], ALU.mult)
            dve.tensor_tensor(l3_g0[:, :], PS[0:NS + E, 7, 8:8 + E], l3_own[:, :], ALU.mult)
            dve.tensor_tensor(l3_mdsq[:, :], l3_mdr[:, :], l3_mdr[:, :], ALU.mult)
            dve.tensor_scalar(l3_m2[:, :, :], l3_md[:, :, :], -2.0, None, ALU.mult).then_inc(f, 1)
            dve.wait_ge(f, 1)
            dve.tensor_reduce(l3_c1[:, :], l3_g1[:, :], AX.X, ALU.add, negate=True)
            dve.tensor_reduce(l3_c0[:, :], l3_g0[:, :], AX.X, ALU.add, negate=True)
            dve.tensor_reduce(l3_md2[:, :], l3_mdsq[:, :], AX.X, ALU.add).then_inc(f, 1)
            dve.wait_ge(f, 2)
            dve.tensor_tensor(l3_c0[:, :], l3_c0[:, :], l3_tail[:, :], ALU.add).then_inc(setup["f_set"], 1)
            dve.wait_ge(setup["f_set"], 1)

            def slot(i):
                ahead(ln_stats, dve, pl, i, 2)
                if (i - 2).ok:
                    b = i - 2
                    dve.wait_ge(*s.se_ps(b))
                    if (b - 1).ok:
                        dve.wait_ge(*s.y_ps(b - 1))
                    dve.tensor_tensor(l3_zz[:, :], PS[0:NS + E, 7, 0:T], l3_mx[b.par][:, :], ALU.mult).then_inc(s.zz.sem, 1)
                ahead(ln_apply, dve, pl, i, 1)
                if (i - 2).ok:
                    b = i - 2
                    dve.wait_ge(*s.y_ps(b))
                    if (b - 1).ok:
                        dve.wait_ge(*s.y(b - 1))
                    for t in range(TT):
                        dve.scalar_tensor_tensor(l3_y1[:, t, :], l3_ht[b.par][:, t, :], l3_oms[b.par][:, t:t + 1],
                                                 bank(4)[:, t * D:(t + 1) * D], ALU.mult, ALU.add).then_inc(s.y1.sem, 1)
                if (i - 1).ok:
                    b = i - 1
                    n = [0]

                    def link(ins):
                        n[0] += 1
                        ins.then_inc(s.tk.sem, 1)
                        dve.wait_ge(*s.tk(b, n[0]))

                    dve.wait_ge(*s.zT_ps(b))
                    if (b - 1).ok:
                        dve.wait_ge(*s.e(b - 1))
                    dve.tensor_scalar(l3_ez[:, :, :].rearrange("p t e -> p (t e)"), bank(5)[:, 0:TT * E], -1.0, 88.0,
                                      ALU.mult, ALU.min).then_inc(s.ed.sem, 1)
                    dve.wait_ge(*s.e(b))
                    link(dve.tensor_scalar(l3_ee[:, :, :], l3_ee[:, :, :], 1.0, None, ALU.add))
                    link(dve.reciprocal(rt_l[:, :, :], l3_ee[:, :, :]))
                    first_of(dve, link, rt_l[:, :, :], rt_m[:, 0, :], rt_o[:, 0])
                    dve.tensor_scalar(l3_oms[b.par][:, :], rt_m[:, 0, :], -1.0, 1.0, ALU.mult, ALU.add).then_inc(s.oms.sem, 1)
                    dve.tensor_tensor(rt_g[b.par][:, :, :], rt_o[:, 0], rt_m[:, 0, :].unsqueeze(2).broadcast_to([P, TT, E]),
                                      ALU.mult).then_inc(s.g.sem, 1)
                if i.ok:
                    b = i
                    dve.wait_ge(*s.hfree(b))
                    dve.tensor_scalar(l3_n[:, :], PS[0:E, 3, T:2 * T], l3_md2[:, 0:1], None, ALU.add).then_inc(s.zr.sem, 1)
                    dve.wait_ge(*s.zr(b, 1))
                    dve.reciprocal(l3_n[:, :], l3_n[:, :]).then_inc(s.zr.sem, 1)
                    dve.wait_ge(*s.zr(b, 2))
                    dve.tensor_tensor(l3_n[:, :], l3_n[:, :], PS[0:E, 3, 0:T], ALU.mult).then_inc(s.zr.sem, 1)
                    dve.wait_ge(*s.zr(b, 3))
                    if (b - 1).ok:
                        dve.wait_ge(*s.zT_ps(b - 1))
                    dve.tensor_scalar(l3_z[:, :], l3_n[:, :], l3_cs[:, 0:1], l3_cs[:, 1:2], ALU.subtract, ALU.mult).then_inc(s.z.sem, 1)

            slots(dve, slot, -2, (4, 14), B + 1)

        def l3f_pool(pool, pl, s):
            memory_free(pool, pl)

            def slot(i):
                ahead(ln_rstd, pool, pl, i, 2)
                if (i - 2).ok:
                    gate_on_pool(pool, pl, s, i - 2, l3_y1[:, :, :], s.y1(i - 2))

            slots(pool, slot, -2, (4, 14), B + 1)

        LOOP2 = (4, 12)

        def stack_ready(b):
            v = 16 * N_STACK * (b.off // 2 + 1)
            return stack_in[b.par], v if b.reg is None else b.reg * (8 * N_STACK) + v

        def scratch_ready(b):
            v = 16 * (b.off // 2 + 1)
            return scratch_in[b.par], v if b.reg is None else b.reg * 8 + v

        def l1a_tensor(pe, pl, s):
            psum_free(pe, pl)
            pe.wait_ge(w_in[2], 16 * len(weights[2]))
            pe.wait_ge(setup["a_wo"], 1)
            pe.wait_ge(setup["a_zero"], 1)

            def project(b):
                h = hT[b.par]
                pe.wait_ge(*s.h(b))
                if (b - 1).ok:
                    pe.wait_ge(*s.max(b - 1, 12))
                for n, done in (("q", s.q_ps), ("k", s.k_ps)):
                    for m in range(KH):
                        for kh in range(KH):
                            last_ = pe.matmul(bank(1 if n == "q" else 2)[:, m * T:(m + 1) * T], l1_w[n][:, kh, m * P:(m + 1) * P],
                                              h[:, kh, :], start=kh == 0, stop=kh == 1)
                    last_.then_inc(done.sem, 1)
                for t in range(TT):
                    for kh in range(KH):
                        last_ = pe.matmul(bank(3)[:, t * D:(t + 1) * D], h[:, kh, t * P:(t + 1) * P],
                                          l1_w["v"][:, kh, :], start=kh == 0, stop=kh == 1)
                last_.then_inc(s.hfree.sem, 1)

            def q_of(b, h, q0, q1):
                return QS[b.par][:, h // 2, h % 2, q0:q1]

            def k_of(b, h, k0, k1):
                return KS[b.par][:, h // 2, k0:k1]

            def max_scores(b, gg):
                if gg == 0:
                    pe.wait_ge(*stack_ready(b))
                for n in range(3):
                    if gg:
                        pe.wait_ge(*s.max(b, 3 * gg + n - 2))
                    elif (b - 1).ok:
                        pe.wait_ge(*s.max(b - 1, 22 + n))
                    else:
                        pe.wait_ge(*(s.q, s.k, s.v)[n](b))
                    if gg == 4 and (b + 1).ok:
                        pe.wait_ge(*(s.q, s.k, s.v)[n](b + 1))
                    if n == 0 and gg == 4:
                        pe.wait_ge(*s.mT(b, 1))
                    if n == 0 and gg == 1 and (b - 1).ok:
                        pe.wait_ge(*s.mT(b - 1, 2))
                    if n == 0:
                        pe.matmul(bank(1), ident_b[:, :], later4[:, :, :], start=True, stop=False)
                        for j in range(4):
                            h = 4 * gg + j
                            last_ = pe.matmul(bank(1)[:, j * P:(j + 1) * P], q_of(b, h, 0, P), k_of(b, h, 0, P), start=False, stop=j == 3)
                    else:
                        for j in range(2):
                            h = 4 * gg + 2 * (n - 1) + j
                            o = bank(1 + n)[:, j * T:(j + 1) * T]
                            pe.matmul(o, q_of(b, h, P, T), k_of(b, h, 0, T), start=True, stop=False)
                            last_ = pe.matmul(o[:, P:T], ident_b[:, :], later4[:, 0, :], start=False, stop=True)
                    last_.then_inc(s.max_ps.sem, 1)

            def max_T(b, half_):
                pe.wait_ge(*s.mparts(b, half_ + 1))
                if half_ == 0:
                    if (b + 1).ok:
                        pe.wait_ge(*s.q(b + 1))
                    else:
                        pe.wait_ge(*s.max(b, 10))
                elif (b + 1).ok:
                    pe.wait_ge(*s.max(b + 1, 1))
                to = PS[:, 1, :].bitcast(BF16)
                for qt in range(TT):
                    last_ = pe.transpose(to[:, qt * P:(qt + 1) * P], mparts[half_][:, qt, :], ident_b[:, :])
                last_.then_inc(s.mT_ps.sem, 1)

            def exp_scores(b, gg):
                half_ = gg // 4
                for n in range(3):
                    if gg:
                        pe.wait_ge(*s.prob(b, 3 * gg + n - 2))
                    elif (b - 1).ok:
                        pe.wait_ge(*s.prob(b - 1, 22 + n))
                    if n == 0 and gg == 1 and (b - 1).ok:
                        pe.wait_ge(*s.u(b - 1))
                    if n == 0 and gg == 4 and (b - 1).ok:
                        pe.wait_ge(*s.ogT(b - 1))
                        pe.wait_ge(*s.y(b - 1))
                    if n == 0 and gg % 4 == 0:
                        pe.wait_ge(*s.mT(b, half_ + 1))
                    if n < 2:
                        for j in range(2):
                            h = 4 * gg + 2 * n + j
                            o = bank(4 + n)[:, j * T:(j + 1) * T]
                            pe.matmul(o, k_of(b, h, 0, P), q_of(b, h, 0, T), start=True, stop=False)
                            pe.matmul(o, pick16[:, h % 16, :], maxT[half_][:, :], start=False, stop=False)
                            last_ = pe.matmul(o[:, 0:P], ident_b[:, :], earlier4[:, 0, :], start=False, stop=True)
                    else:
                        pe.matmul(bank(6), ident_b[:, :], earlier4[:, :, :], start=True, stop=False)
                        for j in range(4):
                            h = 4 * gg + j
                            o = bank(6)[:, j * P:(j + 1) * P]
                            pe.matmul(o, k_of(b, h, P, T), q_of(b, h, P, T), start=False, stop=False)
                            last_ = pe.matmul(o, pick16[:, h % 16, :], maxT[half_][:, P:T], start=False, stop=j == 3)
                    last_.then_inc(s.score.sem, 1)

            def values(b, gg):
                pe.wait_ge(*s.prob(b, 3 * gg + 3))
                if gg:
                    pe.wait_ge(*s.oT(b, gg))
                elif (b - 1).ok:
                    pe.wait_ge(*s.oT(b - 1))
                at = gg % 2 * T
                for j in range(4):
                    h = 4 * gg + j
                    o = PS[32 * j:32 * j + 32, 7, at:at + T]
                    pe.matmul(o, l1_vpad[b.par][:, 0, h // 2, :], pw[gg % 2][j // 2][:, j % 2, :], start=True, stop=False)
                    last_ = pe.matmul(o[:, P:T], l1_vpad[b.par][:, 1, h // 2, :], pz[gg % 2][:, j, :], start=False, stop=True)
                last_.then_inc(s.pv.sem, 1)

            def by_token(b):
                pe.wait_ge(*s.oT(b))
                if (b + 1).ok:
                    pe.wait_ge(*s.prob(b + 1, 3))
                for n in range(4):
                    if n == 3:
                        pe.wait_ge(*s.u(b, 1))
                    qt, gh = n // 2, n % 2
                    for g in range(4):
                        last_ = pe.transpose(bank(4 + n % 3)[:, g * P:(g + 1) * P], l1_oT[:, 4 * gh + g, qt * P:(qt + 1) * P], ident[:, :])
                    last_.then_inc(s.otok_ps.sem, 1)

            def normed_T(b):
                pe.wait_ge(*s.og(b))
                if (b + 1).ok:
                    pe.wait_ge(*s.prob(b + 1, 12))
                for kh in range(KH):
                    for t in range(TT):
                        last_ = pe.transpose(bank(4)[:, kh * T + t * P:kh * T + (t + 1) * P],
                                             l1_og[:, t, kh * P:(kh + 1) * P], ident[:, :])
                last_.then_inc(s.ogT_ps.sem, 1)

            def out(b):
                pe.wait_ge(*s.ogT(b))
                for t in range(TT):
                    for kh in range(KH):
                        last_ = pe.matmul(bank(5)[:, t * D:(t + 1) * D], l1_ogT[:, kh, t * P:(t + 1) * P],
                                          l1_w["o"][:, kh, :], start=kh == 0, stop=kh == 1)
                last_.then_inc(s.y_ps.sem, 1)

            def slot(i):
                for k in range(4):
                    if i.ok:
                        max_scores(i, k)
                    if (i - 1).ok:
                        if k == 0:
                            max_T(i - 1, 1)
                        exp_scores(i - 1, 4 + k)
                        if k:
                            values(i - 1, 3 + k)
                if (i + 1).ok:
                    project(i + 1)
                if (i - 1).ok:
                    values(i - 1, 7)
                if i.ok:
                    max_T(i, 0)
                for k in range(4):
                    if i.ok:
                        max_scores(i, 4 + k)
                        exp_scores(i, k)
                        if k:
                            values(i, k - 1)
                    if k == 0 and (i - 1).ok:
                        by_token(i - 1)
                if i.ok:
                    values(i, 3)
                if (i - 1).ok:
                    normed_T(i - 1)
                ahead(ln_transpose, pe, pl, i, 2)
                if (i - 1).ok:
                    out(i - 1)

            slots(pe, slot, -2, LOOP2, B)

        def l1a_scalar(act, pl, s):
            memory_free(act, pl)
            act.wait_ge(setup["a_dot"], 1)
            act.activation(lam[:, 0:2], lam[:, 0:2], ACT.Exp).then_inc(setup["a_exp"], 1)

            def copy_maxT(b, half_):
                act.wait_ge(*s.mT_ps(b, half_ + 1))
                if half_:
                    if (b - 1).ok:
                        act.wait_ge(*s.score(b - 1))
                elif (b - 1).ok:
                    act.wait_ge(*s.score(b - 1, 12))
                act.activation(maxT[half_][:, :], PS[:, 1, :].bitcast(BF16)[:, 0:T], ACT.Copy).then_inc(s.mT.sem, 1)

            def exps(b, gg):
                for n in range(3):
                    act.wait_ge(*s.score(b, 3 * gg + n + 1))
                    if n == 0:
                        if gg >= 2:
                            act.wait_ge(*s.pv(b, gg - 1))
                        elif (b - 1).ok:
                            act.wait_ge(*s.pv(b - 1, gg + 7))
                    to = pw[gg % 2][n][:, :, :] if n < 2 else pz[gg % 2][:, :, :]
                    act.activation(to.rearrange("p a n -> p (a n)"), bank(4 + n), ACT.Exp).then_inc(s.prob.sem, 1)

            def copy_oT(b, gg):
                act.wait_ge(*s.pv(b, gg + 1))
                if (b - 1).ok and gg == 0:
                    act.wait_ge(*s.otok_ps(b - 1))
                act.activation(l1_oT[:, gg, :], bank(7)[:, gg % 2 * T:(gg % 2 + 1) * T], ACT.Copy).then_inc(s.oT.sem, 1)

            def slot(i):
                for k in range(4):
                    if (i - 1).ok:
                        if k == 0:
                            copy_maxT(i - 1, 1)
                        exps(i - 1, 4 + k)
                        if k:
                            copy_oT(i - 1, 3 + k)
                if (i + 1).ok:
                    b = i + 1
                    for n, ps, done, scale in ((0, s.q_ps, s.q, QK_SCALE), (1, s.k_ps, s.k, 1.0)):
                        act.wait_ge(*ps(b))
                        if n == 0 and (b - 1).ok:
                            act.wait_ge(*s.split(b - 1, 1))
                        if n == 0 and (b - 2).ok:
                            act.wait_ge(*scratch_ready(b - 2))
                        act.activation(qk32[:, n, :], bank(1 + n), ACT.Copy, scale=scale)
                        act.activation(qk_parts[b.par][:, 0, n, :], bank(1 + n), ACT.Copy, scale=scale).then_inc(done.sem, 1)
                    act.wait_ge(*s.hfree(b))
                    if (b - 2).ok:
                        act.wait_ge(*s.pv(b - 2))
                    act.activation(l1_vpad[b.par][:, :, :, 0:HD].rearrange("p t h e -> p (t h) e"),
                                   bank(3).rearrange("p (t e) -> p t e", e=HD), ACT.Copy).then_inc(s.v.sem, 1)
                if (i - 1).ok:
                    copy_oT(i - 1, 7)
                if i.ok:
                    copy_maxT(i, 0)
                    for k in range(4):
                        exps(i, k)
                        if k:
                            copy_oT(i, k - 1)
                    copy_oT(i, 3)
                if (i - 1).ok:
                    act.wait_ge(*s.ogT_ps(i - 1))
                    act.activation(l1_ogT[:, :, :].rearrange("p k t -> p (k t)"), bank(4), ACT.Copy).then_inc(s.ogT.sem, 1)
                ahead(modulate, act, pl, i, 2)

            slots(act, slot, -2, LOOP2, B)

        def l1a_vector(dve, pl, s):
            memory_free(dve, pl)
            dve.wait_ge(w_in[2], 16 * len(weights[2]))
            dve.tensor_tensor(lam_p[:, :, :], lam_v[:, :, 0, :], lam_v[:, :, 1, :], ALU.mult)
            dve.tensor_scalar(l1_w["o"][:, :, :], l1_w["o"][:, :, :], (1 - LAMBDA_INIT) * HD ** 0.5, None, ALU.mult)\
               .then_inc(setup["a_wo"], 1)
            dve.wait_ge(setup["a_wo"], 1)
            dve.tensor_reduce(lam[:, 0:2], lam_p[:, :, :], AX.X, ALU.add).then_inc(setup["a_dot"], 1)
            dve.wait_ge(setup["a_exp"], 1)
            dve.scalar_tensor_tensor(lam[:, 2:3], lam[:, 1:2], LAMBDA_INIT, lam[:, 0:1], ALU.subtract, ALU.subtract)\
               .then_inc(setup["a_lam"], 1)
            dve.wait_ge(setup["a_lam"], 1)

            def maxima(b, gg):
                for n in range(3):
                    dve.wait_ge(*s.max_ps(b, 3 * gg + n + 1))
                    if n == 0:
                        to, src = negmax[b.par][:, 0, 4 * gg:4 * gg + 4], bank(1).rearrange("p (j k) -> p j k", j=4)
                    else:
                        h = 4 * gg + 2 * (n - 1)
                        to, src = negmax[b.par][:, 1, h:h + 2], bank(1 + n).rearrange("p (j k) -> p j k", j=2)
                    dve.tensor_reduce(to, src, AX.X, ALU.max, negate=True).then_inc(s.max.sem, 1)

            def by_token(b):
                for n in range(4):
                    qt, gh = n // 2, n % 2
                    dve.wait_ge(*s.otok_ps(b, n + 1))
                    o = bank(4 + n % 3).rearrange("p (h e) -> p h e", e=32)
                    rl_ = l1_rl[:, qt, 16 * gh:16 * gh + 16]
                    dve.reciprocal(rl_, o[:, :, HD]).then_inc(s.rl.sem, 1)
                    dve.wait_ge(*s.rl(b, n + 1))
                    dve.tensor_tensor(l1_t[:, qt, 16 * gh:16 * gh + 16, :], o[:, :, 0:HD],
                                      rl_.unsqueeze(2).broadcast_to([P, 16, HD]), ALU.mult).then_inc(s.u.sem, 1)
                dve.wait_ge(*s.u(b))
                pair = l1_t[:, :, :, :].rearrange("p q (h two) e -> p (q h) two e", two=2)
                dve.scalar_tensor_tensor(l1_att[:, :, :], pair[:, :, 1, :], lam[:, 2:3], pair[:, :, 0, :], ALU.mult, ALU.add)\
                   .then_inc(s.att.sem, 1)

            def slot(i):
                ahead(ln_stats, dve, pl, i, 3)
                for k in range(8):
                    if i.ok:
                        maxima(i, k)
                    if k == 3:
                        ahead(ln_apply, dve, pl, i, 2)
                    if (i - 1).ok:
                        b = i - 1
                        if k == 4:
                            by_token(b)
                        if k == 6:
                            dve.wait_ge(*s.sq(b))
                            dve.tensor_reduce(l1_ms[:, :], l1_sq[:, :, :], AX.X, ALU.add).then_inc(s.ms.sem, 1)
                        if k == 7:
                            dve.wait_ge(*s.rn(b))
                            dve.tensor_tensor(l1_og[:, :, :].rearrange("p t (h e) -> p (t h) e", e=HD), l1_att[:, :, :],
                                              l1_ms[:, :].unsqueeze(2).broadcast_to([P, TT * HEADS, HD]), ALU.mult)\
                               .then_inc(s.og.sem, 1)
                if (i - 1).ok:
                    dve.wait_ge(*s.y_ps(i - 1))
                    gated(dve, pl, s, i - 1, bank(5).rearrange("p (t d) -> p t d", t=TT))

            slots(dve, slot, -3, LOOP2, B)

        def l1a_pads(pool):
            for i in range(2):
                pool.memset(l1_vpad[i][:, :, :, :], 0.0)
                pool.memset(QS[i][:, :, :, :].bitcast(F32), 0.0)
                pool.memset(KS[i][:, :, :].bitcast(F32), 0.0)
                last_ = pool.memset(mparts[i][:, :, :].bitcast(F32), 0.0)
            last_.then_inc(setup["a_zero"], 1)
            pool.wait_ge(setup["a_zero"], 1)
            for i in range(2):
                last_ = pool.memset(l1_vpad[i][:, :, :, HD:HD + 1], 1.0)
            last_.then_inc(setup["a_one"], 1)

        def l1a_pool(pool, pl, s):
            memory_free(pool, pl)
            if pl == 0:
                l1a_pads(pool)

            def split_qk(b):
                pool.wait_ge(*s.q(b))
                pool.wait_ge(*s.k(b))
                if (b - 2).ok:
                    pool.wait_ge(*s.score(b - 2))
                pool.tensor_tensor(qk_rest[:, :, :], qk32[:, :, :], qk_parts[b.par][:, 0, :, :], ALU.subtract).then_inc(s.split.sem, 1)
                pool.wait_ge(*s.split(b, 1))
                pool.tensor_tensor(qk_parts[b.par][:, 1, :, :], qk_rest[:, :, :], zero[:, :].unsqueeze(1).broadcast_to([P, 2, KH * T]), ALU.add).then_inc(s.split.sem, 1)
                pool.wait_ge(*s.split(b, 2))
                pool.tensor_tensor(qk_parts[b.par][:, 2, :, :], qk_rest[:, :, :], qk_parts[b.par][:, 1, :, :], ALU.subtract)\
                    .then_inc(s.parts.sem, 1)

            def split_max(b, half_):
                m = negmax[b.par][:, :, 16 * half_:16 * half_ + 16]
                part = lambda n: mparts[half_][:, :, 16 * n:16 * n + 16]
                pool.wait_ge(*s.max(b, 12 * half_ + 12))
                if not (b - 1).ok and half_ == 0:
                    pool.wait_ge(setup["a_zero"], 1)
                if (b - 1).ok:
                    pool.wait_ge(*s.mT_ps(b - 1, half_ + 1))
                pool.tensor_tensor(part(0), m, zero[:, :].unsqueeze(1).broadcast_to([P, TT, 16]), ALU.add).then_inc(s.msplit.sem, 1)
                pool.wait_ge(*s.msplit(b, 3 * half_ + 1))
                pool.tensor_tensor(m_rest[:, :, :], m, part(0), ALU.subtract).then_inc(s.msplit.sem, 1)
                pool.wait_ge(*s.msplit(b, 3 * half_ + 2))
                pool.tensor_tensor(part(1), m_rest[:, :, :], zero[:, :].unsqueeze(1).broadcast_to([P, TT, 16]), ALU.add).then_inc(s.msplit.sem, 1)
                pool.wait_ge(*s.msplit(b, 3 * half_ + 3))
                pool.tensor_tensor(part(2), m_rest[:, :, :], part(1), ALU.subtract).then_inc(s.mparts.sem, 1)

            def slot(i):
                ahead(ln_rstd, pool, pl, i, 3)
                if i.ok:
                    split_max(i, 0)
                if (i + 1).ok:
                    split_qk(i + 1)
                if (i - 1).ok:
                    b = i - 1
                    pool.wait_ge(*s.att(b))
                    pool.tensor_tensor(l1_sq[:, :, :], l1_att[:, :, :], l1_att[:, :, :], ALU.mult).then_inc(s.sq.sem, 1)
                    pool.wait_ge(*s.ms(b))
                    pool.tensor_tensor(l1_ms[:, :], l1_ms[:, :], eps_sum1[:, 0:TT * HEADS], ALU.add).then_inc(s.rn_raw.sem, 1)
                    pool.wait_ge(*s.rn_raw(b))
                    pool.tensor_tensor(l1_ms[:, :], l1_ms[:, :], half[:, 0:TT * HEADS], ALU.pow).then_inc(s.rn.sem, 1)
                if i.ok:
                    split_max(i, 1)
                if (i - 1).ok:
                    add_to_x(pool, pl, s, i - 1)

            slots(pool, slot, -3, LOOP2, B)

        Q_TERMS, K_TERMS = (0, 0, 0, 1, 1, 2), (0, 1, 2, 0, 1, 0)
        N_STACK = 2 * 2 * len(Q_TERMS)

        def l1a_sync(sp, pl, s, i):
            if not i.ok:
                return
            if i.reg is None and i.off == 0:
                sp.wait_ge(setup["a_zero"], 1)
            sp.wait_ge(*s.parts(i))
            sp.dma_start(qk_dram[i.par].rearrange("a c m p t -> p a c m t"),
                         qk_parts[i.par][:, :, :, :].rearrange("p a c (m t) -> p a c m t", m=KH)).then_inc(scratch_in[i.par], 16)
            sp.wait_ge(*scratch_ready(i))
            for c, terms in ((0, Q_TERMS), (1, K_TERMS)):
                for pr in range(2):
                    for n, part in enumerate(terms):
                        src = qk_dram[i.par, part, c].rearrange("m (g r d) t -> r d (m g) t", g=8, r=2)[pr]
                        r0 = 64 * pr + 8 * n
                        to = QS[i.par][r0:r0 + 8, :, pr, :] if c == 0 else KS[i.par][r0:r0 + 8, :, :]
                        sp.dma_start(to, src).then_inc(stack_in[i.par], 16)

        def l2a_tensor(pe, pl, s):
            psum_free(pe, pl)
            pe.wait_ge(w_in[4], 48)
            pe.wait_ge(l2_dd_set, 1)

            def slot(i):
                b = i
                if b.ok:
                    pe.wait_ge(*s.h(b))
                    if has(0, b - 1):
                        pe.wait_ge(*s.state(b - 1))
                    for kh in range(KH):
                        last_ = pe.matmul(PS[:, 1, 0:T], l2_b[:, kh, :], hT[b.par][:, kh, :], start=kh == 0, stop=kh == 1)
                    last_.then_inc(s.state_ps.sem, 1)
                ahead(ln_transpose, pe, pl, i, 1)
                if b.ok:
                    pe.wait_ge(*s.state(b))
                    if has(0, b - 2):
                        pe.wait_ge(*s.y(b - 2))
                    for t in range(TT):
                        o = PS[:, 2 + b.par, t * D:(t + 1) * D]
                        pe.matmul(o, l2_st[b.par][:, t * P:(t + 1) * P], l2_c[:, :], start=True, stop=False)
                        for kh in range(KH):
                            last_ = pe.matmul(o[:, kh * P:(kh + 1) * P], hT[b.par][:, kh, t * P:(t + 1) * P],
                                              l2_dd[:, kh, :], start=False, stop=kh == 1)
                    last_.then_inc(s.hfree.sem, 1)

            slots(pe, slot, -1, (2, 14), B - 1)

        def l2a_scalar(act, pl, s):
            memory_free(act, pl)

            def slot(i):
                if i.ok:
                    act.wait_ge(*s.state_ps(i))
                    if has(0, i - 2):
                        act.wait_ge(*s.hfree(i - 2))
                    act.activation(l2_st[i.par][:, :], PS[:, 1, 0:T], ACT.Tanh).then_inc(s.state.sem, 1)
                ahead(modulate, act, pl, i, 1)

            slots(act, slot, -1, (2, 14), B - 1)

        def l2a_vector(dve, pl, s):
            memory_free(dve, pl)
            dve.wait_ge(w_in[4], 48)
            for kh in range(KH):
                last_ = dve.tensor_scalar(l2_dd[:, kh, :], ident[:, :], l2_d[:, kh:kh + 1], None, ALU.mult)
            last_.then_inc(l2_dd_set, 1)

            def slot(i):
                ahead(ln_stats, dve, pl, i, 2)
                ahead(ln_apply, dve, pl, i, 1)
                if i.ok:
                    dve.wait_ge(*s.hfree(i))
                    gated(dve, pl, s, i, PS[:, 2 + i.par, :].rearrange("p (t d) -> p t d", t=TT))

            slots(dve, slot, -2, (2, 14), B - 1)

        def plain_pool(pool, pl, s):
            memory_free(pool, pl)

            def slot(i):
                ahead(ln_rstd, pool, pl, i, 2)
                if (i - 1).ok:
                    add_to_x(pool, pl, s, i - 1)
                if first + pl == 1 and i.reg is None and i.off == 0 and pl + 1 < len(sigs):
                    l1a_pads(pool)

            slots(pool, slot, -2, (4, 14), B)

        tensor_of = {0: l0a_tensor, 1: l0f_tensor, 2: l1a_tensor, 3: l1f_tensor, 5: l2f_tensor, 7: l3f_tensor, 6: l3a_tensor, 4: l2a_tensor}
        scalar_of = {0: l0a_scalar, 1: l0f_scalar, 2: l1a_scalar, 3: l1f_scalar, 5: l2f_scalar, 7: l3f_scalar, 6: l3a_scalar, 4: l2a_scalar}
        vector_of = {0: l0a_vector, 1: l0f_vector, 2: l1a_vector, 3: l1f_vector, 5: l2f_vector, 7: l3f_vector, 6: l3a_vector, 4: l2a_vector}
        pool_of = {0: l0a_pool, 2: l1a_pool, 3: l1f_pool, 7: l3f_pool, 6: l3a_pool}
        consts = [(ident[:, :], ins["ident"]), (rank[:, :, :], ins["rank"]), (cT[:, :, :, :], ins["c"])]
        n_const = len(consts)
        rows = lambda x: x.partition_broadcast(P)
        weights = {0: [(l0_w[n][:, :, :], ins["l0_w" + n]) for n in "qkvo"] + [
            (l0_wg1[:, :, :], ins["l0_wg1"]), (l0_wg2[:, :], ins["l0_wg2"]), (l0_ld[:, :], rows(ins["l0_ld"])),
            (l0_ld_col[:, :], ins["l0_ld_col"]), (l0_ld_row[:, :], rows(ins["l0_ld_row"])), (l0_nw[:, :], ins["l0_nw"]),
            (l0_age[:, :], ins["l0_age"]), (causal[:, :], ins["causal"]), (count[:, :], ins["count"]), (left[:, :], ins["left"]),
            (l0_own[:, :], ins["l0_own"].rearrange("p k d -> p (k d)")),
            (l0_lut[:, :], rows(ins["l0_lut"])), (iota[:, :], rows(ins["iota"]))],
            1: [],
            2: [(l1_w[n][:, :, :], ins["l1_w" + n]) for n in "qkvo"] + [
                (lam_v[:, :, :, :], rows(ins["lam_v"])), (ident_b[:, :], ins["ident_b"]), (later4[:, :, :], ins["later4"]),
                (earlier4[:, :, :], ins["earlier4"]), (pick16[:, :, :], ins["pick16"])],
            3: [(l1_we[:, :, :, :], ins["l1_we"]), (l1_gw[:, :, :], ins["l1_gw"]), (l1_eb[:, :], ins["l1_eb"])],
            5: [(l2_la[:, :, :], ins["l2_la"]), (l2_w[:, :, :], ins["l2_w"]), (l2_rw[:, :, :], ins["l2_rw"]),
                (l2_lb[:, :], ins["l2_lb"]), (l2_sel[:, :], ins["l2_sel"])],
            7: [(l3_sw[:, :, :], ins["l3_sw"]), (l3_up[:, :, :], ins["l3_up"]), (l3_md[:, :, :], ins["l3_md"]),
                (l3_db[:, :, :], ins["l3_db"]), (l3_mdr[:, :], ins["l3_mdr"]), (l3_cs[:, :], ins["l3_cs"]), (l3_dg[:, :], ins["l3_dg"]),
                (l3_blk[:, :], ins["l3_blk"]), (l3_own[:, :], ins["l3_own"]), (l3_e72[:, :], ins["l3_e72"]),
                (l3_tail[:, :], ins["l3_tail"]), (l3_one[:, :], ins["l3_one"])],
            6: [(l3_wqkv[:, :, :], ins["l3_wqkv"]), (l3_wo[:, :, :], ins["l3_wo"]), (l3_same[:, :], ins["l3_same"]),
                (l3_dec[:, :], ins["l3_dec"])],
            4: [(l2_b[:, :, :], ins["l2_b"]), (l2_c[:, :], ins["l2_c"]), (l2_d[:, :], ins["l2_d"])]}

        @block.sync
        def _(sp):
            for to, src in consts:
                sp.dma_start(to, src).then_inc(const_in, 16)
            for i in range(2):
                sp.dma_start(wmod[i][:, :, :], ins["wmod"][i].rearrange("(k p) n -> p k n", p=P)).then_inc(wmod_in[i], 16)
            sp.dma_start(X[:, 0:4], ins["x"][0:4].rearrange("b t p d -> p b t d")).then_inc(x_in[0], 16)
            sp.dma_start(X[:, 4:B], ins["x"][4:B].rearrange("b t p d -> p b t d")).then_inc(x_in[1], 16)
            if first == 0:
                for to, src in weights[first]:
                    sp.dma_start(to, src).then_inc(w_in[first], 16)
            mod_sync(sp)
            if first:
                for to, src in weights[first]:
                    sp.dma_start(to, src).then_inc(w_in[first], 16)
            if first == 0:
                sp.dma_start(l0_idx[:, :], ins["l0_idx"]).then_inc(idx_in, 16)
            for p in range(first, last):
                pl = p - first
                if p == 0:
                    sp.wait_ge(setup["pads"], 1)

                def slot(i):
                    if p == 0:
                        l0a_sync(sp, pl, sigs[pl], i)
                    if i.ok:
                        gate_load(sp, pl, sigs[pl], i)
                    if i.reg is None and i.off == 1 and pl + 1 < len(sigs):
                        if pl:
                            sp.wait_ge(*sigs[pl - 1].x(Idx(None, B - 1)))
                        for to, src in weights[p + 1]:
                            sp.dma_start(to, src).then_inc(w_in[p + 1], 16)
                    if p == 2:
                        l1a_sync(sp, pl, sigs[pl], i + 1)
                    if p == last - 1 and (i - 2).ok:
                        o = i - 2
                        sp.wait_ge(*sigs[pl].x(o))
                        sp.dma_start(y_out[bass.ds(o.n, 1)].rearrange("a (t p) d -> p (a t) d", p=P), xb(o)).then_inc(out_done, 16)

                slots(sp, slot, -1 if p == 2 else 0, (4, 14), B - 1)
            for o in (Idx(None, B - 2), Idx(None, B - 1)):
                sp.wait_ge(*sigs[-1].x(o))
                sp.dma_start(y_out[bass.ds(o.n, 1)].rearrange("a (t p) d -> p (a t) d", p=P), xb(o)).then_inc(out_done, 16)
            sp.wait_ge(out_done, 16 * B)

        @block.gpsimd
        def _(pool):
            pool.memset(eps[:, :], LN_EPS)
            pool.memset(zero[:, :], 0.0)
            pool.memset(eps_sum[:, :], 4 * HD * LN_EPS)
            pool.memset(eps_sum1[:, :], HD * LN_EPS)
            pool.memset(half[:, :], -0.5).then_inc(half_set, 1)
            pool.wait_ge(half_set, 1)
            for p in range(first, last):
                pool_of.get(p, plain_pool)(pool, p - first, sigs[p - first])

        @block.scalar
        def _(act):
            mod_scalar(act)
            act.wait_ge(M["col"], LAYERS)
            for p in range(first, last):
                scalar_of[p](act, p - first, sigs[p - first])

        @block.vector
        def _(dve):
            mod_vector(dve)
            for p in range(first, last):
                vector_of[p](dve, p - first, sigs[p - first])

        @block.tensor
        def _(pe):
            mod_tensor(pe)
            for p in range(first, last):
                tensor_of[p](pe, p - first, sigs[p - first])


def declare_and_build(nc, arrays, first=0, last=8):
    ins = {k[3:]: nc.dram_tensor(k, v.shape, mybir.dt.from_np(v.dtype), kind="ExternalInput").ap() for k, v in arrays.items()}
    out = nc.dram_tensor("y_out", (B, T, D), F32, kind="ExternalOutput").ap()
    build(nc, ins, out, first, last)


def kernel(**inputs):
    import concourse.bacc as _bacc
    from concourse.bass_utils import run_bass_kernel_spmd as _run

    arrays = layout(**inputs)
    nc = _bacc.Bacc("TRN2", target_bir_lowering=False, num_devices=1)
    declare_and_build(nc, arrays)
    r = _run(nc, [arrays], core_ids=[0])
    return r.results[0]["y_out"]
```

```python
import math
from contextlib import ExitStack

import numpy as np

import concourse.bass as bass
from concourse import mybir

F32 = mybir.dt.float32
F32R = mybir.dt.float32r
BF16 = mybir.dt.bfloat16
I32 = mybir.dt.int32
ALU = mybir.AluOpType
ACT = mybir.ActivationFunctionType
AX = mybir.AxisListType

P = 128
B = 16
T = 256
TT = T // P
D = 256
KH = D // P
LAYERS = 4
SECTIONS = 6
LN_EPS = 1e-5
HEADS = 16
HD = D // HEADS
INTER = 688
FT = -(-INTER // P)
LUT = 16
EPS_DEN = 1e-6
LAMBDA_INIT = 0.8 - 0.6 * math.exp(-0.3 * 12)
QK_SCALE = (HD // 2) ** -0.5
LOW = -1e30
E = 8
NS = 64
LORA_SCALE = 2.0
PHASES = ["L0_attn", "L0_ffn", "L1_attn", "L1_ffn", "L2_attn", "L2_ffn", "L3_attn", "L3_ffn"]


class Idx:

    def __init__(self, reg, off):
        self.reg, self.off = reg, off

    def __add__(self, k):
        return Idx(self.reg, self.off + k)

    def __sub__(self, k):
        return Idx(self.reg, self.off - k)

    @property
    def n(self):
        return self.off if self.reg is None else self.reg + self.off

    @property
    def par(self):
        return self.off % 2

    @property
    def ok(self):
        return self.reg is not None or 0 <= self.off < B


class Sig:

    def __init__(self, sem, base, per):
        self.sem, self.base, self.per = sem, base, per

    def __call__(self, b, k=None):
        k = self.per if k is None else k
        if b.reg is None:
            v = self.base + self.per * b.off + k
            assert v > 0
            return self.sem, v
        return self.sem, b.reg * self.per + (self.base + self.per * b.off + k)


class Signals:

    def __init__(self, sig):
        self.stat_raw, self.stat, self.rstd_raw, self.rstd, self.xn = \
            sig("stat_raw"), sig("stat"), sig("rstd_raw"), sig("rstd"), sig("xn")
        self.xT, self.h, self.hfree, self.y, self.x = \
            sig("xT"), sig("h"), sig("hfree"), sig("y"), sig("x")
        self.acc, self.acc0, self.att, self.ax = \
            sig("acc"), sig("acc0"), sig("att"), sig("ax")
        self.bias_ps, self.clip, self.den_ps, self.e, self.ed = \
            sig("bias_ps"), sig("clip"), sig("den_ps"), sig("e"), sig("ed")
        self.ek, self.eq, self.g, self.gT, self.gT_ps = \
            sig("ek"), sig("eq"), sig("g"), sig("gT"), sig("gT_ps")
        self.gate, self.gate_ps, self.hid, self.hsq, self.ht = \
            sig("gate"), sig("gate_ps"), sig("hid"), sig("hsq"), sig("ht")
        self.htok_ps, self.k, self.k_ps, self.kdec, self.kg = \
            sig("htok_ps"), sig("k"), sig("k_ps"), sig("kdec"), sig("kg")
        self.lcopy, self.logit_ps, self.mT, self.mT_ps, self.max = \
            sig("lcopy"), sig("logit_ps"), sig("mT"), sig("mT_ps"), sig("max")
        self.max_ps, self.mparts, self.ms, self.msplit, self.mx = \
            sig("max_ps"), sig("mparts"), sig("ms"), sig("msplit"), sig("mx")
        self.n_ps, self.num, self.o, self.oT, self.og = \
            sig("n_ps"), sig("num"), sig("o"), sig("oT"), sig("og")
        self.ogT, self.ogT_ps, self.oms, self.otok_ps, self.p_ps = \
            sig("ogT"), sig("ogT_ps"), sig("oms"), sig("otok_ps"), sig("p_ps")
        self.parts, self.pick, self.picked, self.prob, self.pv = \
            sig("parts"), sig("pick"), sig("picked"), sig("prob"), sig("pv")
        self.q, self.q_ps, self.qdec, self.qs, self.rden = \
            sig("q"), sig("q_ps"), sig("qdec"), sig("qs"), sig("rden")
        self.rl, self.rn, self.rn_raw, self.rt, self.scan = \
            sig("rl"), sig("rn"), sig("rn_raw"), sig("rt"), sig("scan")
        self.score, self.se_ps, self.split, self.sq, self.state = \
            sig("score"), sig("se_ps"), sig("split"), sig("sq"), sig("state")
        self.state_ps, self.sumk, self.tk, self.u, self.unit_ps = \
            sig("state_ps"), sig("sumk"), sig("tk"), sig("u"), sig("unit_ps")
        self.v, self.v_ps, self.wx, self.wx_ps, self.y1 = \
            sig("v"), sig("v_ps"), sig("wx"), sig("wx_ps"), sig("y1")
        self.h_hi, self.h_lo, self.hid_hi, self.hid_lo = sig("h_hi"), sig("h_lo"), sig("hid_hi"), sig("hid_lo")
        self.y_ps, self.z, self.zT_ps, self.zr, self.zz = \
            sig("y_ps"), sig("z"), sig("zT_ps"), sig("zr"), sig("zz")


def slots(eng, slot, first, steady, last):
    lo, hi = steady
    assert lo % 2 == 0 and hi % 2 == 0 and hi > lo
    for i in range(first, lo):
        slot(Idx(None, i))
    with eng.Fori(lo // 2, hi // 2) as r:
        slot(Idx(r * 2, 0))
        slot(Idx(r * 2, 1))
    for i in range(hi, last + 1):
        slot(Idx(None, i))


def layout(**inputs):
    a = {k: np.asarray(v) for k, v in inputs.items()}
    f = np.float32
    k = np.arange(P)
    two = lambda w: np.ascontiguousarray(w.reshape(KH, P, -1).transpose(1, 0, 2))
    out = {"x": a["L0_attn_x"].reshape(B, TT, P, D)}
    out["c"] = np.ascontiguousarray(np.stack([two(a[f"L{i}_c"].T) for i in range(LAYERS)], 1))
    out["wmod"] = np.stack([a[f"L{i}_wmod"] for i in range(LAYERS)])
    ident = np.eye(P, dtype=f)
    out["ident"] = ident
    for n in "qkvo":
        out[f"l0_w{n}"] = two(a[f"L0_attn_W{n}"])
    out["l0_wg1"], out["l0_wg2"] = two(a["L0_attn_Wg1"]), a["L0_attn_Wg2"]
    ld = a["L0_attn_log_decay"]
    out["l0_ld"] = ld
    out["l0_ld_col"] = np.ascontiguousarray(np.repeat(ld, HD).reshape(KH, P).T)
    out["l0_ld_row"] = np.repeat(ld, HD)
    out["l0_nw"] = np.ascontiguousarray(a["L0_attn_norm_w"].reshape(KH, P).T)
    age = k[None, :] - k[:, None]
    out["l0_age"] = np.maximum(age, 0).astype(f)
    out["causal"] = (age >= 0).astype(f)
    out["count"] = np.broadcast_to((k + 1).astype(f), (P, P)).copy()
    out["left"] = (P - 1 - k).astype(f)[:, None]
    own = np.zeros((P, KH, D), f)
    for h in range(HEADS):
        own[h % 8 * HD:h % 8 * HD + HD, h // 8, h % 8 * 32:h % 8 * 32 + HD] = 1
    out["l0_own"] = own
    pad = np.zeros((FT * P - INTER, D), np.int32)
    down = np.concatenate([a["L0_ffn_down_idx"].T, pad]).reshape(FT, P, D).transpose(1, 0, 2)
    out["l0_idx"] = np.concatenate([two(a["L0_ffn_gate_idx"].T).reshape(P, -1), two(a["L0_ffn_up_idx"].T).reshape(P, -1),
                                    down.reshape(P, -1)], 1)
    out["l0_lut"] = a["L0_ffn_lut"]
    out["iota"] = np.arange(16, dtype=f)
    out["l2_b"] = two(a["L2_attn_B"].T)
    out["l2_c"] = np.ascontiguousarray(a["L2_attn_C"].T)
    out["l2_d"] = np.ascontiguousarray(a["L2_attn_D"].reshape(KH, P).T)
    out["l3_wqkv"], out["l3_wo"] = two(a["L3_attn_w_qkv"]), two(a["L3_attn_w_out"])
    out["l3_dec"] = np.ascontiguousarray(np.repeat(a["L3_attn_decay_param"], HD).reshape(KH, P).T)
    out["l3_same"] = (k[:, None] // HD == k[None, :] // HD).astype(f)
    for n in "qkvo":
        out[f"l1_w{n}"] = two(a[f"L1_attn_W{n}"])
    out["lam_v"] = np.stack([np.stack([a[f"L1_attn_lq{i}"], a[f"L1_attn_lk{i}"]]) for i in (1, 2)])
    bf = mybir.dt.np(BF16)
    low = np.where(age < 0, np.float32(LOW), np.float32(0))
    out["ident_b"] = ident.astype(bf)
    out["later4"] = np.ascontiguousarray(np.broadcast_to(low.T[:, None], (P, 4, P))).astype(bf)
    out["earlier4"] = np.ascontiguousarray(np.broadcast_to(low[:, None], (P, 4, P))).astype(bf)
    out["no_max"] = np.zeros((3, 16, T), bf)
    out["l1_we"] = np.ascontiguousarray(a["L1_ffn_expert_w"].reshape(E, KH, P, D).transpose(2, 1, 0, 3))
    out["l1_gw"], out["l1_eb"] = two(a["L1_ffn_gate_w"].T), a["L1_ffn_expert_b"]
    out["l2_la"], out["l2_w"] = two(a["L2_ffn_lora_A"].reshape(P, D).T), two(a["L2_ffn_weight"].T)
    out["l2_rw"] = two(a["L2_ffn_router_w"].T)
    out["l2_lb"] = np.ascontiguousarray(a["L2_ffn_lora_B"].transpose(0, 2, 1)).reshape(P, D)
    out["l2_sel"] = (np.arange(E)[:, None] == k[None, :] // (P // E)).astype(f)
    rows = lambda w: w.transpose(1, 0, 2).reshape(D, NS)
    out["l3_sw"] = two(rows(a["L3_ffn_select_weight"]))
    out["l3_up"] = two(np.concatenate([rows(a["L3_ffn_lora_update"]), np.zeros((D, E), f)], 1))
    out["l3_md"], out["l3_db"], out["l3_mdr"] = two(a["L3_ffn_select_mean_diff"].T), two(a["L3_ffn_debias_w"].T), a["L3_ffn_select_mean_diff"]
    out["l3_cs"] = np.stack([a["L3_ffn_imp_center"], a["L3_ffn_imp_slope"]], 1)
    out["l3_dg"] = np.concatenate([a["L3_ffn_lora_degen"].transpose(0, 2, 1).reshape(NS, D), a["L3_ffn_bias_w"]])
    blk = (np.arange(NS)[:, None] // (NS // E) == np.arange(E)[None, :]).astype(f)
    out["l3_blk"] = np.concatenate([blk, np.zeros((P - NS, E), f)])
    out["l3_own"] = np.concatenate([blk, np.zeros((E, E), f)])
    out["l3_e72"] = np.ascontiguousarray(np.concatenate([blk, np.eye(E, dtype=f)]).T)
    out["l3_tail"] = (np.arange(NS + E) >= NS).astype(f)[:, None]
    out["l3_one"] = np.ones((P, E), f)
    out["rank"] = np.broadcast_to(np.arange(E, 0, -1).astype(f), (P, TT, E)).copy()
    return {"in_" + k: v for k, v in out.items()}


def build(nc, ins, y_out, first=0, last=8):
    ctx = ExitStack()
    with ctx:
        def sem(name):
            return ctx.enter_context(nc.semaphore(name))

        taken = {}

        def sb(name, shape, dt=F32, stack=ctx):
            taken[stack] = taken.get(stack, 0) + math.prod(shape[1:]) * (2 if dt == BF16 else 4)
            return stack.enter_context(nc.sbuf_tensor(name, shape, dt))

        common = ["stat_raw", "stat", "rstd_raw", "rstd", "xn", "xT", "h", "hfree", "y", "x"]
        per_phase = {
            "L0_attn": {"q_ps": 1, "k_ps": 1, "v_ps": 1, "q": 1, "k": 1, "v": 1, "kg": 1, "qdec": 1, "kdec": 1,
                        "gate_ps": 1, "state_ps": 1, "gate": 1, "state": 1, "score": 8, "prob": 8, "pv": 8, "oT": 1,
                        "otok_ps": 2, "u": 2, "sq": 1, "ms": 1, "rn_raw": 1, "rn": 1, "og": 1, "ogT_ps": 1, "ogT": 1,
                        "y_ps": 1, "pick": 1, "picked": 1},
            "L0_ffn": {"gate_ps": FT - 1, "gate": FT, "hid": FT, "hid_hi": FT, "hid_lo": FT, "h_hi": 1, "h_lo": 1, "y_ps": 1},
            "L1_ffn": {"logit_ps": 1, "lcopy": 1, "rt": 16, "ed": 1, "e": 1, "g": 1, "gT_ps": 1, "gT": 1,
                       "bias_ps": 1, "acc0": 1, "unit_ps": 7, "acc": 16, "h_hi": 1, "h_lo": 1},
            "L2_ffn": {"logit_ps": 1, "lcopy": 1, "rt": 16, "ed": 1, "e": 1, "g": 1, "gT_ps": 1, "gT": 1,
                       "wx_ps": 1, "wx": 1, "ax": 1, "y_ps": 1},
            "L1_attn": {"q_ps": 1, "k_ps": 1, "q": 1, "k": 1, "v": 1, "split": 2, "parts": 1, "max_ps": 24, "max": 24,
                        "msplit": 6, "mparts": 2, "mT_ps": 2, "mT": 2, "score": 24, "prob": 24, "pv": 8, "oT": 8,
                        "otok_ps": 4, "rl": 4, "u": 4, "att": 1, "sq": 1, "ms": 1, "rn_raw": 1, "rn": 1, "og": 1,
                        "ogT_ps": 1, "ogT": 1, "y_ps": 1},
            "L3_attn": {"q_ps": 1, "k_ps": 1, "q": 1, "k": 1, "eq": 1, "ek": 1, "v": 1, "scan": 1, "sumk": 1,
                        "num": 1, "qs": 1, "den_ps": 1, "clip": 1, "rden": 1, "o": 1, "y_ps": 1},
            "L3_ffn": {"p_ps": 1, "htok_ps": 1, "hsq": 1, "sq": 1, "mx": 1, "ht": 1, "n_ps": 1, "zr": 3, "z": 1, "zT_ps": 1,
                       "tk": 7, "ed": 1, "e": 1, "g": 1, "oms": 1, "gT_ps": 1, "gT": 1, "se_ps": 1, "zz": 1, "y_ps": 1, "y1": 2},
            "L2_attn": {"state_ps": 1, "state": 1},
        }
        names = common + sorted({n for d in per_phase.values() for n in d})
        sems = {n: sem(n) for n in names}
        ga_in = [sem("ga_in0"), sem("ga_in1")]
        base = {n: 0 for n in names}
        sigs = []
        for p in range(first, last):
            per = {n: 1 for n in common} | per_phase.get(PHASES[p], {})
            sigs.append(Signals(lambda n: Sig(sems[n], base[n], per.get(n, 0))))
            for n, k in per.items():
                base[n] += B * k

        def ga_loaded(pl, b):
            v = 16 * (B // 2) * pl + 16 * (b.off // 2 + 1)
            return ga_in[b.par], v if b.reg is None else b.reg * 8 + v

        x_in = [sem("x_in_first"), sem("x_in_rest")]
        const_in = sem("const_in")
        idx_in = sem("idx_in")
        wmod_in = [sem("wmod_in0"), sem("wmod_in1")]
        ga_scr = sem("ga_scratch")
        w_in = [sem(f"w_in_{p}") for p in range(8)]
        out_done = sem("out_done")
        mod_sems = {n: sem("mod_" + n) for n in ("silu", "rows_ps", "rows", "col_ps", "col", "sign", "clip", "both", "ga")}

        X = sb("X", [P, B, TT, D])
        ident = sb("ident", [P, P])
        cT = sb("cT", [P, LAYERS, KH, B])
        scT = sb("scT", [P, LAYERS, KH, B])
        modT = sb("modT", [P, 2 * LAYERS, 2, KH, B])
        hT = [sb(f"hT{i}", [P, KH, T]) for i in range(2)]
        xn = [sb(f"xn{i}", [P, TT, D]) for i in range(2)]
        st6 = [sb(f"st6_{i}", [P, TT, 6]) for i in range(2)]
        mv = [sb(f"mv{i}", [P, TT, 2]) for i in range(2)]
        rs = [sb(f"rs{i}", [P, TT]) for i in range(2)]
        half = sb("half", [P, 32])
        eps = sb("eps", [P, TT])
        zero = sb("zero", [P, 1])
        eps_sum = sb("eps_sum", [P, 32])
        eps_sum1 = sb("eps_sum1", [P, 32])
        spare = sb("spare", [P, 1])
        rank = sb("rank", [P, TT, E])
        rt_l, rt_eq = sb("rt_l", [P, TT, E]), sb("rt_eq", [P, TT, E])
        rt_o = sb("rt_o", [P, 2, TT, E])
        rt_m, rt_w = sb("rt_m", [P, 2, TT]), sb("rt_w", [P, 2, TT])
        rt_r, rt_d, rt_e = sb("rt_r", [P, TT]), sb("rt_d", [P, TT]), sb("rt_e", [P, TT])
        rt_g = [sb(f"rt_g{i}", [P, TT, E]) for i in range(2)]
        rt_gT = sb("rt_gT", [E, T])
        ga_sb = [sb(f"ga_sb{i}", [P, D]) for i in range(2)]
        y_sb = [sb(f"y_sb{i}", [P, TT, D]) for i in range(2)]
        ga_dram = nc.dram_tensor("ga_dram", (2 * LAYERS, B, D), F32, kind="Internal").ap()
        PS = ctx.enter_context(nc.psum_tensor("PS", [P, 8, 512], F32))
        half_set = sem("half_set")

        kmask_in = [sem("kmask_in0"), sem("kmask_in1")]
        setup = {n: sem("set_" + n) for n in ("exp", "wo", "zero", "decay", "pads", "dexp", "dsum", "ddec",
                                                    "we_hi", "we_lo", "lut_hi", "lut_lo", "f_ps", "f_step", "f_set", "a_zero", "a_wo", "a_dot", "a_exp", "a_lam",
                                                    "a_pad", "a_one")}

        wbuf = lambda n, shape, k=2, dt=F32: [sb(f"{n}{i}", shape, dt, work) for i in range(k)]
        work = ExitStack()
        lut_lo = sb("lut_lo", [P, 2 * KH * INTER + FT * D], F32, work)
        work.close()
        work = ExitStack()
        we_lo = sb("we_lo", [P, KH, E, D], F32, work)
        work.close()
        work = ExitStack()
        l1_we = sb("l1_we", [P, KH, E, D], F32, work)
        l1_gw = sb("l1_gw", [P, KH, E], F32, work)
        l1_eb = sb("l1_eb", [E, D], F32, work)
        l1_acc = wbuf("l1_acc", [P, TT, D])
        work.close()
        work = ExitStack()
        l2_la, l2_w = sb("l2_la", [P, KH, P], F32, work), sb("l2_w", [P, KH, D], F32, work)
        l2_rw, l2_lb = sb("l2_rw", [P, KH, E], F32, work), sb("l2_lb", [P, D], F32, work)
        l2_sel = sb("l2_sel", [E, P], F32, work)
        l2_ax = wbuf("l2_ax", [P, T])
        l2_wx = sb("l2_wx", [P, T], F32, work)
        work.close()
        work = ExitStack()
        l3_sw, l3_up = sb("l3_sw", [P, KH, NS], F32, work), sb("l3_up", [P, KH, NS + E], F32, work)
        l3_md, l3_db, l3_m2 = (sb("l3_" + n, [P, KH, E], F32, work) for n in ("md", "db", "m2"))
        l3_mdr, l3_mdsq = sb("l3_mdr", [E, D], F32, work), sb("l3_mdsq", [E, D], F32, work)
        l3_cs, l3_md2 = sb("l3_cs", [E, 2], F32, work), sb("l3_md2", [E, 1], F32, work)
        l3_dg = sb("l3_dg", [NS + E, D], F32, work)
        l3_e72 = sb("l3_e72", [E, NS + E], F32, work)
        l3_blk, l3_own = sb("l3_blk", [P, E], F32, work), sb("l3_own", [NS + E, E], F32, work)
        l3_tail, l3_one = sb("l3_tail", [NS + E, 1], F32, work), sb("l3_one", [P, E], F32, work)
        l3_g1, l3_g0 = sb("l3_g1", [NS, E], F32, work), sb("l3_g0", [NS + E, E], F32, work)
        l3_c1, l3_c0 = sb("l3_c1", [NS, 1], F32, work), sb("l3_c0", [NS + E, 1], F32, work)
        l3_hsq, l3_sq = sb("l3_hsq", [P, KH, T], F32, work), sb("l3_sq", [P, T], F32, work)
        l3_mx, l3_ht, l3_oms = wbuf("l3_mx", [NS + E, T]), wbuf("l3_ht", [P, TT, D]), wbuf("l3_oms", [P, TT])
        l3_n, l3_z, l3_zz = sb("l3_n", [E, T], F32, work), sb("l3_z", [E, T], F32, work), sb("l3_zz", [NS + E, T], F32, work)
        l3_ez, l3_ee, l3_y1 = sb("l3_ez", [P, TT, E], F32, work), sb("l3_ee", [P, TT, E], F32, work), sb("l3_y1", [P, TT, D], F32, work)
        work.close()

        lut_w = sb("lut_w", [P, 2 * KH * INTER + FT * D])
        l2_dd_set = sem("l2_dd_set")
        ffn_size = max(taken[w] for w in taken if w is not ctx)
        beyond = ffn_size - 4 * (2 * KH * INTER + FT * D)

        work = ExitStack()
        wmod = [sb(f"wmod{i}", [P, KH, SECTIONS * D], F32, work) for i in range(2)]
        mrow = sb("mrow", [B, SECTIONS, D], F32, work)
        g_out = sb("g_out", [B, 2, D], F32, work)
        work.close()
        work = ExitStack()
        sb(f"beyond{len(taken)}", [P, beyond // 4], F32, work)
        l2_b = sb("l2_b", [P, KH, P], F32, work)
        l2_c = sb("l2_c", [P, D], F32, work)
        l2_d = sb("l2_d", [P, KH], F32, work)
        l2_dd = sb("l2_dd", [P, KH, P], F32, work)
        l2_st = [sb(f"l2_st{i}", [P, T], F32, work) for i in range(2)]
        work.close()
        work = ExitStack()
        l0_pick = sb("l0_pick", [P, 2 * KH * INTER + FT * D], F32, work)
        l0_idx = sb("l0_idx", [P, 2 * KH * INTER + FT * D], I32, work)
        kmask = wbuf("l0_kmask", [P, 8, KH, T])
        l0_w = {n: sb("l0_w" + n, [P, KH, D], F32, work) for n in "qkvo"}
        l0_wo_n = l0_w["o"]
        l0_wg1 = sb("l0_wg1", [P, KH, HD], F32, work)
        l0_wg2 = sb("l0_wg2", [HD, D], F32, work)
        l0_ld = sb("l0_ld", [P, HEADS], F32, work)
        l0_ld_col = sb("l0_ld_col", [P, KH], F32, work)
        l0_ld_row = sb("l0_ld_row", [P, D], F32, work)
        l0_nw = sb("l0_nw", [P, KH], F32, work)
        l0_age = sb("l0_age", [P, P], F32, work)
        causal = sb("causal", [P, P], F32, work)
        count = sb("count", [P, P], F32, work)
        left = sb("left", [P, 1], F32, work)
        l0_own = sb("l0_own", [P, KH * D], F32, work)
        l0_decay = sb("l0_decay", [P, HEADS, P], F32, work)
        l0_qdec = sb("l0_qdec", [P, KH, P], F32, work)
        l0_kdec = l0_ld_row
        l0_lut = sb("l0_lut", [P, LUT], F32, work)
        iota = sb("iota", [P, LUT], F32, work)
        qT, kT = wbuf("l0_qT", [P, KH, T]), wbuf("l0_kT", [P, KH, T], 1)
        vpad = wbuf("l0_vpad", [P, TT, HEADS, 32])
        kraw, kdec, g1T, qdec = wbuf("l0_kraw", [P, D], 1), wbuf("l0_kdec_", [P, D]), wbuf("l0_g1T", [HD, T]), wbuf("l0_qdec_", [P, KH, P])
        gate = wbuf("l0_gate", [P, TT, D])
        state = wbuf("l0_state", [P, KH * D])
        prob = wbuf("l0_prob", [P, 4, P], 4)
        oT = sb("l0_oT", [P, 4, TT, P], F32, work)
        u_sb, sq_sb, og_sb, ogT_sb = (sb("l0_" + n, [P, TT, D], F32, work) for n in ("u", "sq", "og", "ogT"))
        ms_sb = sb("l0_ms", [P, TT * HEADS], F32, work)
        work.close()

        work = ExitStack()
        sb(f"beyond{len(taken)}", [P, beyond // 4], F32, work)
        l1_w = {n: sb("l1_w" + n, [P, KH, D], F32, work) for n in "qkvo"}
        lam_v, lam_p, lam = sb("lam_v", [P, 2, 2, 8], F32, work), sb("lam_p", [P, 2, 8], F32, work), sb("lam", [P, 3], F32, work)
        ident_b = sb("ident_b", [P, P], BF16, work)
        later4 = sb("later4", [P, 4, P], BF16, work)
        earlier4 = sb("earlier4", [P, 4, P], BF16, work)
        QS, KS = wbuf("QS", [P, 16, 2, T], 2, BF16), wbuf("KS", [P, 16, T], 2, BF16)
        l1_vpad, mparts = wbuf("l1_vpad", [P, TT, HEADS, 32]), wbuf("mparts", [P, TT, P], 2, BF16)
        qk32, qk_rest = sb("qk32", [P, 2, KH * T], F32, work), sb("qk_rest", [P, 2, KH * T], F32, work)
        qk_parts = wbuf("qk_parts", [P, 3, 2, KH * T], 2, BF16)
        negmax = wbuf("negmax", [P, TT, 32])
        m_rest = sb("m_rest", [P, TT, 16], F32, work)
        maxT = wbuf("maxT", [48, T], 2, BF16)
        pw = [wbuf(f"pw{i}_", [P, 2, T]) for i in range(2)]
        pz = wbuf("pz", [P, 4, P])
        l1_oT = sb("l1_oT", [P, 8, T], F32, work)
        l1_rl, l1_t = sb("l1_rl", [P, TT, 32], F32, work), sb("l1_t", [P, TT, 32, HD], F32, work)
        l1_att, l1_sq = sb("l1_att", [P, TT * HEADS, HD], F32, work), sb("l1_sq", [P, TT * HEADS, HD], F32, work)
        l1_ms = sb("l1_ms", [P, TT * HEADS], F32, work)
        l1_og, l1_ogT = sb("l1_og", [P, TT, D], F32, work), sb("l1_ogT", [P, KH, T], F32, work)
        work.close()
        lut_size = 4 * (2 * KH * INTER + FT * D)
        here = 4 * (6 * T + 4 * FT * T + 4 * KH * T) + lut_size
        before = taken[work] + 9 * 1024 - here
        work = ExitStack()
        sb("before", [P, before // 4], F32, work)
        act_sb, hid = wbuf("l0f_act", [P, T], 3), wbuf("l0f_hid", [P, T], 3)
        hid_parts = wbuf("l0f_hid_parts", [P, 2, FT, T])
        l0_h_parts = wbuf("l0_h_parts", [P, 2, KH, T])
        lut_hi = sb("lut_hi", [P, 2 * KH * INTER + FT * D], F32, work)
        work.close()
        work = ExitStack()
        sb("beside", [P, 8 * 1024 // 4 + beyond // 4], F32, work)
        we_hi = sb("we_hi", [P, KH, E, D], F32, work)
        h_parts = wbuf("h_parts", [P, 2, KH, T])
        work.close()
        work = ExitStack()
        sb(f"beyond{len(taken)}", [P, beyond // 4], F32, work)
        l3_wqkv = sb("l3_wqkv", [P, KH, 3 * D], F32, work)
        l3_wo = sb("l3_wo", [P, KH, D], F32, work)
        l3_same = sb("l3_same", [P, P], F32, work)
        l3_dec = sb("l3_dec", [P, KH], F32, work)
        l3_r, l3_e = wbuf("l3_r", [P, KH * T]), wbuf("l3_e", [P, KH * T])
        l3_qk = wbuf("l3_qk", [P, KH, T])
        l3_sk, l3_kv, l3_skv, l3_qs = (sb("l3_" + n, [P, KH, T], F32, work) for n in ("sk", "kv", "skv", "qs"))
        l3_num = wbuf("l3_num", [P, KH, T])
        l3_den = sb("l3_den", [P, KH * T], F32, work)
        work.close()

        qk_dram = nc.dram_tensor("qk_dram", (2, 3, 2, KH, P, T), BF16, kind="Internal").ap()
        stack_in, max_in = [sem("stack_in0"), sem("stack_in1")], [sem("max_in0"), sem("max_in1")]
        scratch_in = [sem("scratch_in0"), sem("scratch_in1")]

        block = ctx.enter_context(nc.Block())

        def xb(b):
            return X[:, bass.ds(b.n, 1), :, :].rearrange("p a t d -> p (a t) d")

        def has(pl, b):
            return pl > 0 or b.ok

        def ln_stats(dve, pl, s, b):
            if pl == 0:
                if b.reg is None and b.off < 4:
                    dve.wait_ge(x_in[0], 16)
                else:
                    dve.wait_ge(x_in[1], 16)
            else:
                dve.wait_ge(*sigs[pl - 1].x(b))
            for t in range(TT):
                last_ = dve.bn_stats(st6[b.par][:, t, :], xb(b)[:, t, :])
            last_.then_inc(s.stat_raw.sem, 1)
            dve.wait_ge(*s.stat_raw(b))
            dve.memset(spare[:, :], 0.0)
            for t in range(TT):
                last_ = dve.bn_aggr(mv[b.par][:, t, :], st6[b.par][:, t, :])
            last_.then_inc(s.stat.sem, 1)

        def ln_rstd(pool, pl, s, b):
            pool.wait_ge(*s.stat(b))
            if has(pl, b - 2):
                pool.wait_ge(*s.xn(b - 2))
            pool.tensor_tensor(rs[b.par][:, :], mv[b.par][:, :, 1], eps[:, 0:TT], ALU.add).then_inc(s.rstd_raw.sem, 1)
            pool.wait_ge(*s.rstd_raw(b))
            pool.tensor_tensor(rs[b.par][:, :], rs[b.par][:, :], half[:, 0:TT], ALU.pow).then_inc(s.rstd.sem, 1)

        def ln_apply(dve, pl, s, b):
            dve.wait_ge(*s.rstd(b))
            if has(pl, b - 2):
                dve.wait_ge(*s.xT(b - 2))
            for t in range(TT):
                last_ = dve.tensor_scalar(xn[b.par][:, t, :], xb(b)[:, t, :], mv[b.par][:, t, 0:1],
                                          rs[b.par][:, t:t + 1], ALU.subtract, ALU.mult)
            last_.then_inc(s.xn.sem, 1)

        def ln_transpose(pe, pl, s, b):
            pe.wait_ge(*s.xn(b))
            if has(pl, b - 1):
                pe.wait_ge(*s.h(b - 1))
            for kh in range(KH):
                for t in range(TT):
                    last_ = pe.transpose(PS[:, 0, kh * T + t * P:kh * T + (t + 1) * P],
                                         xn[b.par][:, t, kh * P:(kh + 1) * P], ident[:, :])
            last_.then_inc(s.xT.sem, 1)

        def modulate(act, pl, s, b):
            sub = first + pl
            act.wait_ge(*s.xT(b))
            if has(pl, b - 2):
                act.wait_ge(*s.hfree(b - 2))
            for kh in range(KH):
                last_ = act.activation(hT[b.par][:, kh, :], PS[:, 0, kh * T:(kh + 1) * T], ACT.Identity,
                                       bias=modT[:, sub, 0, kh, bass.ds(b.n, 1)],
                                       scale=modT[:, sub, 1, kh, bass.ds(b.n, 1)])
            last_.then_inc(s.h.sem, 1)

        def gate_load(sp, pl, s, b):
            if has(pl, b - 2):
                sp.wait_ge(*s.y(b - 2))
            sp.dma_start(ga_sb[b.par][:, :], ga_dram[first + pl, bass.ds(b.n, 1), :].rearrange("a d -> (a d)")
                         .partition_broadcast(P)).then_inc(ga_in[b.par], 16)

        def gated(dve, pl, s, b, out_ps):
            dve.wait_ge(*ga_loaded(pl, b))
            if has(pl, b - 2):
                dve.wait_ge(*s.x(b - 2))
            dve.tensor_tensor(y_sb[b.par][:, :, :], out_ps, ga_sb[b.par][:, :].unsqueeze(1).broadcast_to([P, TT, D]),
                              ALU.mult).then_inc(s.y.sem, 1)

        def add_to_x(pool, pl, s, b):
            pool.wait_ge(*s.y(b))
            pool.tensor_tensor(xb(b), xb(b), y_sb[b.par][:, :, :], ALU.add).then_inc(s.x.sem, 1)

        def psum_free(pe, pl):
            if pl > 0:
                pe.wait_ge(*sigs[pl - 1].y(Idx(None, B - 1)))
            elif first > 0:
                mod_done(pe)

        def memory_free(eng, pl):
            if pl > 0:
                if first + pl == 1:
                    eng.wait_ge(*sigs[pl - 1].x(Idx(None, B - 1)))
            elif first > 0:
                mod_done(eng)

        def mod_done(eng):
            eng.wait_ge(ga_scr, 16 * LAYERS)
            eng.wait_ge(mod_sems["col"], LAYERS)

        begun = {}
        depth = lambda step, pl: (2 if step in (ln_stats, ln_rstd) else 1) + (1 if first + pl == 2 else 0)

        def ahead(step, eng, pl, i, k):
            b = i + k
            if b.reg is not None or b.off < B:
                if b.ok and (b.reg is not None or b.off >= begun.get((step, pl), 0)):
                    step(eng, pl, sigs[pl], b)
            elif i.off < B and pl + 1 < len(sigs) and b.off - B < depth(step, pl + 1):
                step(eng, pl + 1, sigs[pl + 1], Idx(None, b.off - B))
                begun[step, pl + 1] = b.off - B + 1

        M = mod_sems

        def mod_tensor(pe):
            pe.wait_ge(const_in, 16 * n_const)
            pe.wait_ge(M["silu"], 1)
            for i in range(LAYERS):
                pe.wait_ge(wmod_in[i % 2], 16 * (i // 2 + 1))
                if i:
                    pe.wait_ge(M["rows"], i)
                for n in range(3):
                    for kh in range(KH):
                        last_ = pe.matmul(PS[0:B, 1 + n, :], scT[:, i, kh, :], wmod[i % 2][:, kh, n * 512:(n + 1) * 512],
                                          start=kh == 0, stop=kh == KH - 1)
                last_.then_inc(M["rows_ps"], 1)
                pe.wait_ge(M["rows"], i + 1)
                if i:
                    pe.wait_ge(M["col"], i)
                for sub in range(2):
                    for c in range(2):
                        for kh in range(KH):
                            at = ((sub * 2 + c) * KH + kh) * B
                            last_ = pe.transpose(PS[:, 4, at:at + B],
                                                 mrow[:, 3 * sub + c, kh * P:(kh + 1) * P], ident[0:B, 0:B])
                last_.then_inc(M["col_ps"], 1)

        def mod_scalar(act):
            act.wait_ge(const_in, 16 * n_const)
            act.activation(scT[:, :, :, :], cT[:, :, :, :], ACT.Silu).then_inc(M["silu"], 1)
            for i in range(LAYERS):
                act.wait_ge(M["rows_ps"], i + 1)
                if i:
                    act.wait_ge(M["col_ps"], i)
                    act.wait_ge(M["both"], i)
                act.activation(mrow[:, :, :].rearrange("p s d -> p (s d)"), PS[0:B, 1:4, :].rearrange("p a n -> p (a n)"),
                               ACT.Copy).then_inc(M["rows"], 1)
                if i == 2 and first == 0:
                    l0a_tables(act)

        def mod_vector(dve):
            for i in range(LAYERS):
                dve.wait_ge(M["col_ps"], i + 1)
                cols = PS[:, 4, 0:8 * B].rearrange("p (s c k) -> p s c k", s=2, c=2)
                to = modT[:, 2 * i:2 * i + 2, :, :, :].rearrange("p s c k b -> p s c (k b)")
                dve.tensor_copy(to[:, :, 0, :], cols[:, :, 0, :])
                dve.tensor_scalar(to[:, :, 1, :], cols[:, :, 1, :], 1.0, None, ALU.add).then_inc(M["col"], 1)
                g = mrow[:, 2:SECTIONS:3, :]
                size, twice = y_sb[0][0:B], y_sb[1][0:B]
                if i:
                    dve.wait_ge(M["ga"], i)
                dve.scalar_tensor_tensor(size, g, -1.0, g, ALU.mult, ALU.max).then_inc(M["sign"], 1)
                dve.tensor_scalar(twice, g, 0.0, 2.0, ALU.is_ge, ALU.mult).then_inc(M["both"], 1)
                dve.wait_ge(M["sign"], i + 1)
                dve.tensor_scalar(size, size, 0.25, None, ALU.max).then_inc(M["clip"], 1)
                dve.wait_ge(M["clip"], i + 1)
                dve.wait_ge(M["both"], i + 1)
                if i:
                    dve.wait_ge(ga_scr, 16 * i)
                dve.scalar_tensor_tensor(g_out[:, :, :], twice, -1.0, size, ALU.add, ALU.mult).then_inc(M["ga"], 1)

        def mod_sync(sp):
            for i in range(LAYERS):
                if i + 2 < LAYERS:
                    sp.wait_ge(M["rows_ps"], i + 1)
                    sp.dma_start(wmod[i % 2][:, :, :], ins["wmod"][i + 2].rearrange("(k p) n -> p k n", p=P)).then_inc(wmod_in[i % 2], 16)
                sp.wait_ge(M["ga"], i + 1)
                sp.dma_start(ga_dram[2 * i:2 * i + 2].rearrange("s b d -> b s d"), g_out[:, :, :]).then_inc(ga_scr, 16)
            sp.wait_ge(ga_scr, 16 * LAYERS)

        LOOP0 = (4, 14)

        def bank(i, rows=P):
            return PS[0:rows, i, :]

        def kmask_ready(b):
            v = 16 * 8 * (b.off // 2 + 1)
            return kmask_in[b.par], v if b.reg is None else b.reg * 64 + v

        def l0a_tensor(pe, pl, s):
            psum_free(pe, pl)
            pe.wait_ge(w_in[0], 16 * len(weights[0]))
            pe.wait_ge(setup["wo"], 1)
            pe.wait_ge(setup["pads"], 1)

            def project(b):
                h = hT[b.par]
                pe.wait_ge(*s.h(b))
                if b.reg is not None or b.off >= 1:
                    pe.wait_ge(*s.gate(b - 1))
                    pe.wait_ge(*s.state(b - 1))
                for n, bk, done in (("q", 1, s.q_ps), ("k", 2, s.k_ps)):
                    for m in range(KH):
                        for kh in range(KH):
                            last_ = pe.matmul(bank(bk)[:, m * T:(m + 1) * T], l0_w[n][:, kh, m * P:(m + 1) * P],
                                              h[:, kh, :], start=kh == 0, stop=kh == 1)
                    last_.then_inc(done.sem, 1)
                pe.wait_ge(*s.q(b))
                for t in range(TT):
                    for kh in range(KH):
                        last_ = pe.matmul(bank(1)[:, t * D:(t + 1) * D], h[:, kh, t * P:(t + 1) * P],
                                          l0_w["v"][:, kh, :], start=kh == 0, stop=kh == 1)
                last_.then_inc(s.v_ps.sem, 1)
                pe.wait_ge(*s.k(b))
                for kh in range(KH):
                    pe.matmul(bank(2)[:, 0:D], h[:, kh, 0:P], l0_w["k"][:, kh, :], start=kh == 0, stop=kh == 1)
                for kh in range(KH):
                    last_ = pe.matmul(PS[0:HD, 2, D:D + T], l0_wg1[:, kh, :], h[:, kh, :], start=kh == 0, stop=kh == 1)
                last_.then_inc(s.hfree.sem, 1)

            def gate_state(b):
                pe.wait_ge(*s.kg(b))
                pe.wait_ge(*s.v(b))
                for t in range(TT):
                    last_ = pe.matmul(bank(1)[:, t * D:(t + 1) * D], g1T[b.par][:, t * P:(t + 1) * P], l0_wg2[:, :],
                                      start=True, stop=True)
                last_.then_inc(s.gate_ps.sem, 1)
                pe.wait_ge(*s.kdec(b))
                for m in range(KH):
                    last_ = pe.matmul(bank(2)[:, m * D:(m + 1) * D], kdec[b.par][:, m * P:(m + 1) * P],
                                      vpad[b.par][:, 0, 8 * m:8 * m + 8, :], start=True, stop=True)
                last_.then_inc(s.state_ps.sem, 1)

            def values(b, u):
                t, g = u // 4, u % 4
                pe.wait_ge(*s.prob(b, u + 1))
                if u == 0 and (b - 1).ok:
                    pe.wait_ge(*s.oT(b - 1))
                o = PS[:, 6 + g // 2, (g % 2 * 2 + t) * P:(g % 2 * 2 + t + 1) * P]
                if t == 1:
                    pe.wait_ge(*s.state(b))
                    pe.wait_ge(*s.qdec(b))
                    pe.matmul(o, state[b.par][:, g * P:(g + 1) * P], qdec[b.par][:, g // 2, :], start=True, stop=False)
                for j in range(4):
                    last_ = pe.matmul(o[32 * j:32 * j + 32], vpad[b.par][:, t, 4 * g + j, :], prob[u % 4][:, j, :],
                                      start=t == 0, stop=True)
                last_.then_inc(s.pv.sem, 1)

            def by_token(b):
                pe.wait_ge(*s.oT(b))
                for t in range(TT):
                    for g in range(4):
                        last_ = pe.transpose(bank(3 + t)[:, g * P:(g + 1) * P], oT[:, g, t, :], ident[:, :])
                    last_.then_inc(s.otok_ps.sem, 1)

            def normed_T(b):
                pe.wait_ge(*s.og(b))
                for kh in range(KH):
                    for t in range(TT):
                        last_ = pe.transpose(bank(3)[:, kh * T + t * P:kh * T + (t + 1) * P],
                                             og_sb[:, t, kh * P:(kh + 1) * P], ident[:, :])
                last_.then_inc(s.ogT_ps.sem, 1)

            def out(b):
                pe.wait_ge(*s.ogT(b))
                for t in range(TT):
                    for kh in range(KH):
                        last_ = pe.matmul(bank(4)[:, t * D:(t + 1) * D], ogT_sb[:, kh, t * P:(t + 1) * P],
                                          l0_wo_n[:, kh, :], start=kh == 0, stop=kh == 1)
                last_.then_inc(s.y_ps.sem, 1)

            def slot(i):
                if i.ok:
                    project(i)
                if (i - 2).ok:
                    pe.wait_ge(*s.prob(i - 2))
                    if (i - 3).ok:
                        pe.wait_ge(*s.y(i - 3))
                    by_token(i - 2)
                if (i - 1).ok:
                    c = i - 1
                    for u in range(8):
                        if u == 0 and (i - 2).ok:
                            pe.wait_ge(*s.u(i - 2))
                        t_scores(c, u)
                        if u >= 2:
                            values(c, u - 2)
                    values(c, 6)
                    values(c, 7)
                if (i - 2).ok:
                    if (i - 1).ok:
                        pe.wait_ge(*s.prob(i - 1))
                    normed_T(i - 2)
                if i.ok:
                    gate_state(i)
                ahead(ln_transpose, pe, pl, i, 1)
                if (i - 2).ok:
                    out(i - 2)

            def t_scores(b, u):
                t, g = u // 4, u % 4
                if u == 0:
                    pe.wait_ge(*kmask_ready(b))
                    pe.wait_ge(*s.q(b))
                if u < 3:
                    if (b - 1).ok:
                        pe.wait_ge(*s.prob(b - 1))
                else:
                    pe.wait_ge(*s.prob(b, u - 2))
                for j in range(4):
                    h = 4 * g + j
                    last_ = pe.matmul(bank(3 + u % 3)[:, j * P:(j + 1) * P], kmask[b.par][:, h % 8, h // 8, t * P:(t + 1) * P],
                                      qT[b.par][:, h // 8, t * P:(t + 1) * P], start=True, stop=True)
                last_.then_inc(s.score.sem, 1)

            slots(pe, slot, -1, LOOP0, B + 1)

        def l0a_tables(act):
            act.wait_ge(w_in[0], 16 * len(weights[0]))
            for h in range(HEADS):
                act.activation(l0_decay[:, h, :], l0_age[:, :], ACT.Exp, scale=l0_ld[:, h:h + 1])
            for m in range(KH):
                act.activation(l0_qdec[:, m, :], count[:, :], ACT.Exp, scale=l0_ld_col[:, m:m + 1])
            act.activation(l0_kdec[:, :], l0_ld_row[:, :], ACT.Exp, scale=left[:, 0:1]).then_inc(setup["exp"], 1)

        def l0a_scalar(act, pl, s):
            memory_free(act, pl)
            def slot(i):
                b = i
                if b.ok:
                    act.wait_ge(*s.q_ps(b))
                    if (b - 2).ok:
                        act.wait_ge(*s.score(b - 2))
                        act.wait_ge(*s.qdec(b - 2))
                    act.activation(qT[b.par][:, :, :].rearrange("p k t -> p (k t)"), bank(1), ACT.Silu).then_inc(s.q.sem, 1)
                    act.wait_ge(*s.k_ps(b))
                    if (b - 1).ok:
                        act.wait_ge(*kmask_ready(b - 1))
                    act.activation(kT[0][:, :, :].rearrange("p k t -> p (k t)"), bank(2), ACT.Silu).then_inc(s.k.sem, 1)
                    act.wait_ge(*s.v_ps(b))
                    if (b - 2).ok:
                        act.wait_ge(*s.pv(b - 2))
                    act.activation(vpad[b.par][:, :, :, 0:HD].rearrange("p t h e -> p (t h) e"),
                                   bank(1).rearrange("p (t e) -> p t e", e=HD), ACT.Silu).then_inc(s.v.sem, 1)
                    act.wait_ge(*s.hfree(b))
                    if (b - 1).ok:
                        act.wait_ge(*s.kdec(b - 1))
                    if (b - 2).ok:
                        act.wait_ge(*s.gate_ps(b - 2))
                    act.activation(kraw[0][:, :], bank(2)[:, 0:D], ACT.Silu)
                    act.activation(g1T[b.par][:, :], PS[0:HD, 2, D:D + T], ACT.Copy).then_inc(s.kg.sem, 1)
                if (i - 1).ok:
                    act.wait_ge(*s.pv(i - 1))
                    if (i - 2).ok:
                        act.wait_ge(*s.otok_ps(i - 2))
                    act.activation(oT[:, :, :, :].rearrange("p g t c -> p (g t c)"), PS[:, 6:8, :].rearrange("p a n -> p (a n)"),
                                   ACT.Copy).then_inc(s.oT.sem, 1)
                if (i - 2).ok:
                    act.wait_ge(*s.ogT_ps(i - 2))
                    if (i - 3).ok:
                        act.wait_ge(*s.y_ps(i - 3))
                    act.activation(ogT_sb[:, :, :].rearrange("p k t -> p (k t)"), bank(3), ACT.Copy).then_inc(s.ogT.sem, 1)
                if b.ok:
                    act.wait_ge(*s.gate_ps(b))
                    act.activation(gate[b.par][:, :, :].rearrange("p t d -> p (t d)"), bank(1), ACT.Tanh, scale=0.5)\
                       .then_inc(s.gate.sem, 1)
                ahead(modulate, act, pl, i, 1)

            slots(act, slot, -1, LOOP0, B + 1)

        def l0a_pads(pool):
            for i in range(2):
                pool.memset(kmask[i][:, :, :, :], 0.0)
                last_ = pool.memset(vpad[i][:, :, :, :], 0.0)
            last_.then_inc(setup["pads"], 1)
            pool.memset(lut_w[:, :], 0.0).then_inc(setup["zero"], 1)

        def l0a_vector(dve, pl, s):
            memory_free(dve, pl)
            dve.wait_ge(w_in[0], 16 * len(weights[0]))
            for m in range(KH):
                last_ = dve.tensor_scalar(l0_wo_n[:, m, :], l0_w["o"][:, m, :], l0_nw[:, m:m + 1], HD ** 0.5, ALU.mult, ALU.mult)
            last_.then_inc(setup["wo"], 1)
            def pick(i):
                if (i - 1).ok:
                    dve.wait_ge(*s.picked(i - 1))
                else:
                    dve.wait_ge(idx_in, 16)
                dve.tensor_scalar(l0_pick[:, :], l0_idx[:, :], iota[:, bass.ds(i.n, 1)], l0_lut[:, bass.ds(i.n, 1)],
                                  ALU.is_equal, ALU.mult).then_inc(s.pick.sem, 1)

            def slot(i):
                ahead(ln_stats, dve, pl, i, 2)
                if i.ok and (i.reg is not None or i.off > 1):
                    pick(i)
                if (i - 2).ok:
                    b = i - 2
                    for t in range(TT):
                        dve.wait_ge(*s.otok_ps(b, t + 1))
                        if t == 0:
                            dve.wait_ge(*s.gate(b))
                            if (b - 1).ok:
                                dve.wait_ge(*s.sq(b - 1))
                        dve.scalar_tensor_tensor(u_sb[:, t, :].rearrange("p (h e) -> p h e", e=HD),
                                                 gate[b.par][:, t, :].rearrange("p (h e) -> p h e", e=HD), 1.0,
                                                 bank(3 + t).rearrange("p (h e) -> p h e", e=32)[:, :, 0:HD],
                                                 ALU.add, ALU.mult).then_inc(s.u.sem, 1)
                if (i - 1).ok:
                    b = i - 1
                    for u in range(8):
                        dve.wait_ge(*s.score(b, u + 1))
                        if u == 0:
                            dve.wait_ge(setup["decay"], 1)
                        if u < 4:
                            if (b - 1).ok:
                                dve.wait_ge(*s.pv(b - 1, u + 5))
                        else:
                            dve.wait_ge(*s.pv(b, u - 3))
                        g = u % 4
                        dve.tensor_tensor(prob[u % 4][:, :, :], bank(3 + u % 3).rearrange("p (j c) -> p j c", j=4),
                                          l0_decay[:, 4 * g:4 * g + 4, :], ALU.mult).then_inc(s.prob.sem, 1)
                        if u == 2 and (i - 2).ok:
                            mean_square(i - 2)
                        if u == 6 and (i - 2).ok:
                            norm(i - 2)
                if not (i - 1).ok and (i - 2).ok:
                    mean_square(i - 2)
                    norm(i - 2)
                ahead(ln_apply, dve, pl, i, 1)
                if i.ok:
                    dve.wait_ge(*s.state_ps(i))
                    if (i - 2).ok:
                        dve.wait_ge(*s.pv(i - 2))
                    dve.tensor_tensor(state[i.par][:, :], bank(2), l0_own[:, :], ALU.mult).then_inc(s.state.sem, 1)
                if i.reg is None and i.off == 0:
                    dve.wait_ge(setup["exp"], 1)
                    dve.tensor_tensor(l0_decay[:, :, :], l0_decay[:, :, :], causal[:, :].unsqueeze(1).broadcast_to([P, HEADS, P]),
                                      ALU.mult).then_inc(setup["decay"], 1)
                if i.reg is None and i.off in (0, 1):
                    pick(i)
                if (i - 2).ok:
                    dve.wait_ge(*s.y_ps(i - 2))
                    gated(dve, pl, s, i - 2, bank(4).rearrange("p (t d) -> p t d", t=TT))

            def mean_square(b):
                dve.wait_ge(*s.sq(b))
                if (b - 1).ok:
                    dve.wait_ge(*s.rn(b - 1))
                dve.tensor_reduce(ms_sb[:, :], sq_sb[:, :, :].rearrange("p t (h e) -> p (t h) e", e=HD), AX.X, ALU.add)\
                   .then_inc(s.ms.sem, 1)

            def norm(b):
                dve.wait_ge(*s.rn(b))
                if (b - 1).ok:
                    dve.wait_ge(*s.ogT_ps(b - 1))
                dve.tensor_tensor(og_sb[:, :, :].rearrange("p t (h e) -> p (t h) e", e=HD),
                                  u_sb[:, :, :].rearrange("p t (h e) -> p (t h) e", e=HD),
                                  ms_sb[:, :].unsqueeze(2).broadcast_to([P, TT * HEADS, HD]), ALU.mult).then_inc(s.og.sem, 1)

            slots(dve, slot, -2, LOOP0, B + 1)

        def l0a_pool(pool, pl, s):
            memory_free(pool, pl)
            pool.wait_ge(setup["zero"], 1)
            pool.wait_ge(setup["exp"], 1)

            def slot(i):
                ahead(ln_rstd, pool, pl, i, 2)
                if (i - 2).ok:
                    b = i - 2
                    pool.wait_ge(*s.u(b))
                    pool.tensor_tensor(sq_sb[:, :, :], u_sb[:, :, :], u_sb[:, :, :], ALU.mult).then_inc(s.sq.sem, 1)
                    pool.wait_ge(*s.ms(b))
                    pool.tensor_tensor(ms_sb[:, :], ms_sb[:, :], eps_sum[:, 0:TT * HEADS], ALU.add).then_inc(s.rn_raw.sem, 1)
                    pool.wait_ge(*s.rn_raw(b))
                    pool.tensor_tensor(ms_sb[:, :], ms_sb[:, :], half[:, 0:TT * HEADS], ALU.pow).then_inc(s.rn.sem, 1)
                if i.ok:
                    pool.wait_ge(*s.q(i))
                    if (i - 2).ok:
                        pool.wait_ge(*s.pv(i - 2))
                    pool.tensor_tensor(qdec[i.par][:, :, :], qT[i.par][:, :, P:T], l0_qdec[:, :, :], ALU.mult)\
                        .then_inc(s.qdec.sem, 1)
                    pool.wait_ge(*s.kg(i))
                    pool.tensor_tensor(kdec[i.par][:, :], kraw[0][:, :], l0_kdec[:, :], ALU.mult).then_inc(s.kdec.sem, 1)
                if i.ok:
                    pool.wait_ge(*s.pick(i))
                    pool.tensor_tensor(lut_w[:, :], lut_w[:, :], l0_pick[:, :], ALU.add).then_inc(s.picked.sem, 1)
                if (i - 2).ok:
                    add_to_x(pool, pl, s, i - 2)

            slots(pool, slot, -2, LOOP0, B + 1)

        def l0a_sync(sp, pl, s, i):
            if i.ok:
                sp.wait_ge(*s.k(i))
                for r in range(8):
                    sp.dma_start(kmask[i.par][16 * r:16 * r + 16, r, :, :], kT[0][16 * r:16 * r + 16, :, :])\
                      .then_inc(kmask_in[i.par], 16)

        def split_hi(dve, out, x):
            return dve.tensor_copy(out.bitcast(F32R), x)

        def matmul3(pe, out, a, b_, start, stop):
            terms = ((a[0], b_[0]), (a[0], b_[1]), (a[1], b_[0]))
            for n, (x, y) in enumerate(terms):
                last_ = pe.matmul(out, x.bitcast(F32R), y.bitcast(F32R), start=start and n == 0, stop=stop and n == 2)
            return last_

        gate_w = [w[:, 0:KH * INTER].rearrange("p (k n) -> p k n", k=KH) for w in (lut_hi, lut_lo)]
        up_w = [w[:, KH * INTER:2 * KH * INTER].rearrange("p (k n) -> p k n", k=KH) for w in (lut_hi, lut_lo)]
        down_w = [w[:, 2 * KH * INTER:].rearrange("p (m d) -> p m d", m=FT) for w in (lut_hi, lut_lo)]
        rows_of = lambda m: min(P, INTER - m * P)

        def l0f_tensor(pe, pl, s):
            psum_free(pe, pl)
            pe.wait_ge(setup["lut_lo"], 1)

            def slot(i):
                if i.ok:
                    pe.wait_ge(*s.h_lo(i))
                    for m in range(FT):
                        r = rows_of(m)
                        if m >= 3:
                            pe.wait_ge(*s.hid(i, m - 2))
                        elif (i - 1).ok:
                            pe.wait_ge(*s.hid(i - 1, m + 4))
                        for n, w in enumerate((gate_w, up_w)):
                            for kh in range(KH):
                                last_ = matmul3(pe, PS[0:r, 1 + m % 3, n * T:(n + 1) * T], [x[:, kh, m * P:m * P + r] for x in w],
                                                [l0_h_parts[i.par][:, c, kh, :] for c in range(2)], kh == 0, kh == 1)
                        if m == FT - 1:
                            last_.then_inc(s.hfree.sem, 1)
                        else:
                            last_.then_inc(s.gate_ps.sem, 1)
                        if m == 2:
                            ahead(ln_transpose, pe, pl, i, 1)
                else:
                    ahead(ln_transpose, pe, pl, i, 1)
                if (i - 1).ok:
                    b = i - 1
                    if not (b - 1).ok:
                        pe.wait_ge(setup["lut_lo"], 2)
                    pe.wait_ge(*s.hid_lo(b))
                    if (b - 1).ok:
                        pe.wait_ge(*s.y(b - 1))
                    for t in range(TT):
                        for m in range(FT):
                            r = rows_of(m)
                            last_ = matmul3(pe, bank(4)[:, t * D:(t + 1) * D],
                                            [hid_parts[b.par][0:r, c, m, t * P:(t + 1) * P] for c in range(2)],
                                            [x[0:r, m, :] for x in down_w], m == 0, m == FT - 1)
                    last_.then_inc(s.y_ps.sem, 1)

            slots(pe, slot, -1, (4, 14), B)

        def l0f_wait_gu(eng, s, b, m):
            if m == FT - 1:
                eng.wait_ge(*s.hfree(b))
            else:
                eng.wait_ge(*s.gate_ps(b, m + 1))

        def l0f_scalar(act, pl, s):
            memory_free(act, pl)

            def slot(i):
                if i.ok:
                    for m in range(FT):
                        r = rows_of(m)
                        l0f_wait_gu(act, s, i, m)
                        if m >= 3:
                            act.wait_ge(*s.hid(i, m - 2))
                        elif (i - 1).ok:
                            act.wait_ge(*s.hid(i - 1, m + 4))
                        act.activation(act_sb[m % 3][0:r, :], PS[0:r, 1 + m % 3, 0:T], ACT.Silu).then_inc(s.gate.sem, 1)
                        if m == 2:
                            ahead(modulate, act, pl, i, 1)
                else:
                    ahead(modulate, act, pl, i, 1)

            slots(act, slot, -1, (4, 14), B - 1)

        def l0f_vector(dve, pl, s):
            memory_free(dve, pl)

            def high_bits(b):
                dve.wait_ge(*s.h(b))
                if (b - 2).ok:
                    dve.wait_ge(*s.hfree(b - 2))
                split_hi(dve, l0_h_parts[b.par][:, 0], hT[b.par][:, :, :]).then_inc(s.h_hi.sem, 1)

            cut = 2 * KH * INTER
            for n, part in enumerate((slice(0, cut), slice(cut, cut + FT * D))):
                split_hi(dve, lut_hi[:, part], lut_w[:, part]).then_inc(setup["lut_hi"], 1)
                dve.wait_ge(setup["lut_hi"], n + 1)
                dve.tensor_tensor(lut_lo[:, part].bitcast(F32R), lut_w[:, part], lut_hi[:, part], ALU.subtract).then_inc(setup["lut_lo"], 1)
                if n == 0:
                    high_bits(Idx(None, 0))

            def slot(i):
                ahead(ln_stats, dve, pl, i, 2)
                if not i.ok:
                    ahead(ln_apply, dve, pl, i, 1)
                if i.ok:
                    for m in range(FT):
                        r = rows_of(m)
                        dve.wait_ge(*s.gate(i, m + 1))
                        if m >= 3:
                            dve.wait_ge(*s.hid_lo(i, m - 2))
                        elif (i - 1).ok:
                            dve.wait_ge(*s.hid_lo(i - 1, m + 4))
                        dve.tensor_tensor(hid[m % 3][0:r, :], act_sb[m % 3][0:r, :], PS[0:r, 1 + m % 3, T:2 * T],
                                          ALU.mult).then_inc(s.hid.sem, 1)
                        if m == 0 and (i - 2).ok:
                            dve.wait_ge(*s.y_ps(i - 2))
                        if m == 0:
                            ahead(ln_apply, dve, pl, i, 1)
                        dve.wait_ge(*s.hid(i, m + 1))
                        split_hi(dve, hid_parts[i.par][0:r, 0, m, :], hid[m % 3][0:r, :]).then_inc(s.hid_hi.sem, 1)
                        if m == 4 and (i + 1).ok:
                            high_bits(i + 1)
                if (i - 1).ok:
                    dve.wait_ge(*s.y_ps(i - 1))
                    gated(dve, pl, s, i - 1, bank(4).rearrange("p (t d) -> p t d", t=TT))

            slots(dve, slot, -2, (4, 14), B)

        def l0f_pool(pool, pl, s):
            memory_free(pool, pl)

            def low_bits(b):
                pool.wait_ge(*s.h_hi(b))
                pool.tensor_tensor(l0_h_parts[b.par][:, 1].bitcast(F32R), hT[b.par][:, :, :], l0_h_parts[b.par][:, 0], ALU.subtract)\
                    .then_inc(s.h_lo.sem, 1)

            def slot(i):
                ahead(ln_rstd, pool, pl, i, 2)
                if i.ok:
                    for m in range(FT):
                        r = rows_of(m)
                        pool.wait_ge(*s.hid_hi(i, m + 1))
                        pool.tensor_tensor(hid_parts[i.par][0:r, 1, m, :].bitcast(F32R), hid[m % 3][0:r, :], hid_parts[i.par][0:r, 0, m, :],
                                           ALU.subtract).then_inc(s.hid_lo.sem, 1)
                        if m == 4 and (i + 1).ok:
                            low_bits(i + 1)
                elif (i + 1).ok:
                    low_bits(i + 1)
                if (i - 1).ok:
                    add_to_x(pool, pl, s, i - 1)
                if i.reg is None and 0 <= i.off < 4 and pl + 1 < len(sigs):
                    l1a_pads(pool, i.off)

            slots(pool, slot, -2, (4, 14), B)

        def l3a_tensor(pe, pl, s):
            psum_free(pe, pl)
            pe.wait_ge(w_in[6], 16 * len(weights[6]))

            def slot(i):
                if i.ok:
                    pe.wait_ge(*s.h(i))
                    for n, done, free in ((0, s.q_ps, s.q), (1, s.k_ps, s.k), (2, s.hfree, s.v)):
                        if (i - 1).ok:
                            pe.wait_ge(*free(i - 1))
                        for m in range(KH):
                            for kh in range(KH):
                                last_ = pe.matmul(bank(1 + n)[:, m * T:(m + 1) * T],
                                                  l3_wqkv[:, kh, n * D + m * P:n * D + (m + 1) * P],
                                                  hT[i.par][:, kh, :], start=kh == 0, stop=kh == 1)
                        last_.then_inc(done.sem, 1)
                ahead(ln_transpose, pe, pl, i, 1)
                if (i - 1).ok:
                    b = i - 1
                    pe.wait_ge(*s.qs(b))
                    if (b - 1).ok:
                        pe.wait_ge(*s.clip(b - 1))
                    for m in range(KH):
                        last_ = pe.matmul(bank(4)[:, m * T:(m + 1) * T], l3_same[:, :], l3_qs[:, m, :], start=True, stop=True)
                    last_.then_inc(s.den_ps.sem, 1)
                if (i - 2).ok:
                    b = i - 2
                    pe.wait_ge(*s.o(b))
                    if (b - 1).ok:
                        pe.wait_ge(*s.y(b - 1))
                    for t in range(TT):
                        for kh in range(KH):
                            last_ = pe.matmul(bank(5)[:, t * D:(t + 1) * D], l3_num[b.par][:, kh, t * P:(t + 1) * P],
                                              l3_wo[:, kh, :], start=kh == 0, stop=kh == 1)
                    last_.then_inc(s.y_ps.sem, 1)

            slots(pe, slot, -1, (6, 14), B + 1)

        def l3a_scalar(act, pl, s):
            memory_free(act, pl)
            act.wait_ge(w_in[6], 16 * len(weights[6]))
            act.activation(l3_dec[:, :], l3_dec[:, :], ACT.Exp, scale=-1.0).then_inc(setup["dexp"], 1)

            def slot(i):
                if i.ok:
                    for n, ps, done, r, e in ((0, s.q_ps, s.eq, l3_r[0], l3_e[0]), (1, s.k_ps, s.ek, l3_r[1], l3_e[1])):
                        act.wait_ge(*ps(i))
                        if (i - 1).ok:
                            act.wait_ge(*(s.q, s.k)[n](i - 1))
                        act.activation(r[:, :], bank(1 + n), ACT.Relu)
                        act.activation(e[:, :], bank(1 + n), ACT.Exp).then_inc(done.sem, 1)
                ahead(modulate, act, pl, i, 1)

            slots(act, slot, -1, (6, 14), B - 1)

        def l3a_vector(dve, pl, s):
            memory_free(dve, pl)

            def slot(i):
                ahead(ln_stats, dve, pl, i, 2)
                ahead(ln_apply, dve, pl, i, 1)
                if i.ok:
                    for n, done, ready in ((0, s.q, s.eq), (1, s.k, s.ek)):
                        dve.wait_ge(*ready(i))
                        if n == 0 and (i - 1).ok:
                            dve.wait_ge(*s.num(i - 1))
                            dve.wait_ge(*s.qs(i - 1))
                        dve.scalar_tensor_tensor(l3_qk[n][:, :, :].rearrange("p k t -> p (k t)"), l3_e[n][:, :], 1.0, l3_r[n][:, :],
                                                 ALU.min, ALU.add).then_inc(done.sem, 1)
                    dve.wait_ge(*s.k(i))
                    for m in range(KH):
                        last_ = dve.tensor_tensor_scan(l3_sk[:, m, :], l3_dec[:, m:m + 1].broadcast_to([P, T]), l3_qk[1][:, m, :],
                                                       0.0, ALU.mult, ALU.add)
                    last_.then_inc(s.sumk.sem, 1)
                    dve.wait_ge(*s.hfree(i))
                    dve.tensor_tensor(l3_kv[:, :, :].rearrange("p k t -> p (k t)"), l3_qk[1][:, :, :].rearrange("p k t -> p (k t)"),
                                      bank(3), ALU.mult).then_inc(s.v.sem, 1)
                    dve.wait_ge(*s.v(i))
                    for m in range(KH):
                        last_ = dve.tensor_tensor_scan(l3_skv[:, m, :], l3_dec[:, m:m + 1].broadcast_to([P, T]), l3_kv[:, m, :],
                                                       0.0, ALU.mult, ALU.add)
                    last_.then_inc(s.scan.sem, 1)
                if (i - 1).ok:
                    b = i - 1
                    dve.wait_ge(*s.den_ps(b))
                    if (b - 1).ok:
                        dve.wait_ge(*s.o(b - 1))
                    dve.tensor_scalar(l3_den[:, :], bank(4), EPS_DEN, None, ALU.max).then_inc(s.clip.sem, 1)
                    dve.wait_ge(*s.clip(b))
                    dve.reciprocal(l3_den[:, :], l3_den[:, :]).then_inc(s.rden.sem, 1)
                if (i - 2).ok:
                    dve.wait_ge(*s.y_ps(i - 2))
                    gated(dve, pl, s, i - 2, bank(5).rearrange("p (t d) -> p t d", t=TT))

            dve.wait_ge(w_in[6], 16 * len(weights[6]))
            dve.wait_ge(setup["dexp"], 1)
            dve.tensor_scalar(l3_dec[:, :], l3_dec[:, :], 1.0, None, ALU.add).then_inc(setup["dsum"], 1)
            dve.wait_ge(setup["dsum"], 1)
            dve.reciprocal(l3_dec[:, :], l3_dec[:, :]).then_inc(setup["ddec"], 1)
            dve.wait_ge(setup["ddec"], 1)
            slots(dve, slot, -2, (6, 14), B + 1)

        def l3a_pool(pool, pl, s):
            memory_free(pool, pl)

            def slot(i):
                ahead(ln_rstd, pool, pl, i, 2)
                if i.ok:
                    b = i
                    pool.wait_ge(*s.sumk(b))
                    if (b - 1).ok:
                        pool.wait_ge(*s.den_ps(b - 1))
                    pool.tensor_tensor(l3_qs[:, :, :], l3_qk[0][:, :, :], l3_sk[:, :, :], ALU.mult).then_inc(s.qs.sem, 1)
                    pool.wait_ge(*s.scan(b))
                    if (b - 2).ok:
                        pool.wait_ge(*s.y_ps(b - 2))
                    pool.tensor_tensor(l3_num[b.par][:, :, :], l3_qk[0][:, :, :], l3_skv[:, :, :], ALU.mult).then_inc(s.num.sem, 1)
                if (i - 1).ok:
                    b = i - 1
                    pool.wait_ge(*s.rden(b))
                    pool.wait_ge(*s.num(b))
                    o = l3_num[b.par][:, :, :].rearrange("p k t -> p (k t)")
                    pool.tensor_tensor(o, o, l3_den[:, :], ALU.mult).then_inc(s.o.sem, 1)
                if (i - 2).ok:
                    add_to_x(pool, pl, s, i - 2)

            slots(pool, slot, -2, (6, 14), B + 1)

        BIG = 3e38

        def logit_bank(pl):
            return bank(7 if PHASES[first + pl] == "L2_ffn" else 5)

        def logits(pe, pl, s, b, w):
            pe.wait_ge(*s.h(b))
            if (b - 1).ok:
                pe.wait_ge(*s.lcopy(b - 1))
            for t in range(TT):
                for kh in range(KH):
                    last_ = pe.matmul(logit_bank(pl)[:, t * E:(t + 1) * E], hT[b.par][:, kh, t * P:(t + 1) * P], w[:, kh, :],
                                      start=kh == 0, stop=kh == 1)
            last_.then_inc(s.logit_ps.sem, 1)

        def first_of(dve, link, vals, top, one):
            link(dve.tensor_reduce(top, vals, AX.X, ALU.max))
            link(dve.tensor_tensor(rt_eq[:, :, :], vals, top.unsqueeze(2).broadcast_to([P, TT, E]), ALU.is_equal))
            link(dve.tensor_tensor(rt_eq[:, :, :], rt_eq[:, :, :], rank[:, :, :], ALU.mult))
            link(dve.tensor_reduce(rt_r[:, :], rt_eq[:, :, :], AX.X, ALU.max))
            link(dve.tensor_tensor(one, rank[:, :, :], rt_r[:, :].unsqueeze(2).broadcast_to([P, TT, E]), ALU.is_equal))

        def route(dve, pl, s, b):
            n = [0]

            def link(ins):
                n[0] += 1
                ins.then_inc(s.rt.sem, 1)
                dve.wait_ge(*s.rt(b, n[0]))

            dve.wait_ge(*s.logit_ps(b))
            dve.tensor_copy(rt_l[:, :, :], logit_bank(pl)[:, 0:TT * E].rearrange("p (t e) -> p t e", t=TT)).then_inc(s.lcopy.sem, 1)
            dve.wait_ge(*s.lcopy(b))
            first_of(dve, link, rt_l[:, :, :], rt_m[:, 0, :], rt_o[:, 0])
            link(dve.scalar_tensor_tensor(rt_l[:, :, :], rt_o[:, 0], -BIG, rt_l[:, :, :], ALU.mult, ALU.add))
            first_of(dve, link, rt_l[:, :, :], rt_m[:, 1, :], rt_o[:, 1])
            if (b - 1).ok:
                dve.wait_ge(*s.e(b - 1))
            dve.tensor_tensor(rt_d[:, :], rt_m[:, 1, :], rt_m[:, 0, :], ALU.subtract).then_inc(s.ed.sem, 1)
            dve.wait_ge(*s.e(b))
            link(dve.tensor_scalar(rt_w[:, 0, :], rt_e[:, :], 1.0, None, ALU.add))
            link(dve.reciprocal(rt_w[:, 0, :], rt_w[:, 0, :]))
            link(dve.tensor_tensor(rt_w[:, 1, :], rt_e[:, :], rt_w[:, 0, :], ALU.mult))
            for m in range(2):
                link(dve.tensor_tensor(rt_o[:, m], rt_o[:, m], rt_w[:, m, :].unsqueeze(2).broadcast_to([P, TT, E]), ALU.mult))
            dve.tensor_tensor(rt_g[b.par][:, :, :], rt_o[:, 0], rt_o[:, 1], ALU.add).then_inc(s.g.sem, 1)

        def route_exp(act, pl, s, b):
            act.wait_ge(*s.ed(b))
            if PHASES[first + pl] == "L3_ffn":
                act.activation(l3_ee[:, :, :], l3_ez[:, :, :], ACT.Exp).then_inc(s.e.sem, 1)
            else:
                act.activation(rt_e[:, :], rt_d[:, :], ACT.Exp).then_inc(s.e.sem, 1)

        def gates_T(pe, pl, s, b, bk):
            pe.wait_ge(*s.g(b))
            if (b - 1).ok:
                pe.wait_ge(*s.gT(b - 1))
            for t in range(TT):
                last_ = pe.transpose(PS[0:E, bk, t * P:(t + 1) * P], rt_g[b.par][:, t, :], ident[:, :])
            last_.then_inc(s.gT_ps.sem, 1)

        def gates_T_copy(act, pl, s, b, bk):
            act.wait_ge(*s.gT_ps(b))
            act.activation(rt_gT[:, :], PS[0:E, bk, 0:T], ACT.Copy).then_inc(s.gT.sem, 1)

        def l1f_tensor(pe, pl, s):
            psum_free(pe, pl)
            pe.wait_ge(w_in[3], 16 * len(weights[3]))
            pe.wait_ge(setup["we_lo"], 1)

            def slot(i):
                b = i
                if b.ok:
                    for u in range(8):
                        t, e2 = u % 2, u // 2
                        if u >= 4:
                            pe.wait_ge(*s.acc(b, 4 * (e2 - 2) + 3 + t))
                        elif (b - 1).ok:
                            pe.wait_ge(*s.acc(b - 1, 4 * (e2 + 2) + 3 + t))
                        if u == 0:
                            pe.wait_ge(*s.h_lo(b))
                        for kh in range(KH):
                            last_ = matmul3(pe, bank(1 + u % 4), [h_parts[b.par][:, c, kh, t * P:(t + 1) * P] for c in range(2)],
                                            [w[:, kh, 2 * e2:2 * e2 + 2, :] for w in (we_hi, we_lo)], kh == 0, kh == 1)
                        last_.then_inc((s.hfree if u == 7 else s.unit_ps).sem, 1)
                        if u == 0:
                            gates_T(pe, pl, s, b, 6)
                        if u == 1:
                            pe.wait_ge(*s.gT(b))
                            if (b - 1).ok:
                                pe.wait_ge(*s.acc0(b - 1))
                            for tt in range(TT):
                                last_ = pe.matmul(bank(7)[:, tt * D:(tt + 1) * D], rt_gT[:, tt * P:(tt + 1) * P], l1_eb[:, :],
                                                  start=True, stop=True)
                            last_.then_inc(s.bias_ps.sem, 1)
                        if u == 3:
                            ahead(ln_transpose, pe, pl, i, 1)
                        if u == 5 and (i + 1).ok:
                            logits(pe, pl, s, i + 1, l1_gw)
                else:
                    ahead(ln_transpose, pe, pl, i, 1)
                    if (i + 1).ok:
                        logits(pe, pl, s, i + 1, l1_gw)

            slots(pe, slot, -1, (4, 14), B - 1)

        def l1f_scalar(act, pl, s):
            memory_free(act, pl)

            def slot(i):
                b = i
                if b.ok:
                    gates_T_copy(act, pl, s, b, 6)
                    act.wait_ge(*s.bias_ps(b))
                    if (b - 2).ok:
                        act.wait_ge(*s.y(b - 2))
                    act.activation(l1_acc[b.par][:, :, :].rearrange("p t d -> p (t d)"), bank(7), ACT.Copy).then_inc(s.acc0.sem, 1)
                ahead(modulate, act, pl, i, 1)
                if (i + 1).ok:
                    route_exp(act, pl, s, i + 1)

            slots(act, slot, -1, (4, 14), B - 1)

        def l1f_vector(dve, pl, s):
            memory_free(dve, pl)
            dve.wait_ge(w_in[3], 16 * len(weights[3]))
            if pl:
                dve.wait_ge(*sigs[pl - 1].x(Idx(None, B - 1)))
            split_hi(dve, we_hi[:, :, :, :], l1_we[:, :, :, :]).then_inc(setup["we_hi"], 1)
            dve.wait_ge(setup["we_hi"], 1)
            dve.tensor_tensor(we_lo[:, :, :, :].bitcast(F32R), l1_we[:, :, :, :], we_hi[:, :, :, :], ALU.subtract).then_inc(setup["we_lo"], 1)

            def high_bits(b):
                dve.wait_ge(*s.h(b))
                if (b - 2).ok:
                    dve.wait_ge(*s.hfree(b - 2))
                split_hi(dve, h_parts[b.par][:, 0], hT[b.par][:, :, :]).then_inc(s.h_hi.sem, 1)

            def slot(i):
                b = i
                ahead(ln_apply, dve, pl, i, 1)
                ahead(ln_stats, dve, pl, i, 2)
                if b.ok:
                    n = 0
                    for q in range(4):
                        for e in range(2):
                            for t in range(TT):
                                if n == 0:
                                    dve.wait_ge(*s.acc0(b))
                                if e == 0:
                                    u = 2 * q + t
                                    if u == 7:
                                        dve.wait_ge(*s.hfree(b))
                                    else:
                                        dve.wait_ge(*s.unit_ps(b, u + 1))
                                if n >= 2:
                                    dve.wait_ge(*s.acc(b, n - 1))
                                x_ = 2 * q + e
                                dve.scalar_tensor_tensor(l1_acc[b.par][:, t, :], bank(1 + (2 * q + t) % 4)[:, e * D:(e + 1) * D],
                                                         rt_g[b.par][:, t, x_:x_ + 1], l1_acc[b.par][:, t, :],
                                                         ALU.mult, ALU.add).then_inc(s.acc.sem, 1)
                                n += 1
                        if q == 2 and (i + 1).ok:
                            high_bits(i + 1)
                            route(dve, pl, s, i + 1)
                elif (i + 1).ok:
                    high_bits(i + 1)
                    route(dve, pl, s, i + 1)

            slots(dve, slot, -2, (4, 14), B - 1)

        def gate_on_pool(pool, pl, s, b, src, done):
            pool.wait_ge(*done)
            pool.wait_ge(*ga_loaded(pl, b))
            if has(pl, b - 1):
                pool.wait_ge(*s.x(b - 1))
            pool.tensor_tensor(y_sb[b.par][:, :, :], src, ga_sb[b.par][:, :].unsqueeze(1).broadcast_to([P, TT, D]),
                               ALU.mult).then_inc(s.y.sem, 1)
            add_to_x(pool, pl, s, b)

        def l1f_pool(pool, pl, s):
            memory_free(pool, pl)

            def slot(i):
                ahead(ln_rstd, pool, pl, i, 2)
                if (i + 1).ok:
                    b = i + 1
                    pool.wait_ge(*s.h_hi(b))
                    pool.tensor_tensor(h_parts[b.par][:, 1].bitcast(F32R), hT[b.par][:, :, :], h_parts[b.par][:, 0], ALU.subtract)\
                        .then_inc(s.h_lo.sem, 1)
                if i.ok:
                    gate_on_pool(pool, pl, s, i, l1_acc[i.par][:, :, :], s.acc(i))

            slots(pool, slot, -2, (4, 14), B - 1)

        def l2f_tensor(pe, pl, s):
            psum_free(pe, pl)
            pe.wait_ge(w_in[5], 16 * len(weights[5]))

            def slot(i):
                b = i - 1
                h = hT[i.par]
                if i.ok:
                    logits(pe, pl, s, i, l2_rw)
                if b.ok:
                    if (b - 1).ok:
                        pe.wait_ge(*s.wx(b - 1))
                    gates_T(pe, pl, s, b, 2)
                if i.ok:
                    if (i - 2).ok:
                        pe.wait_ge(*s.y(i - 2))
                    for t in range(TT):
                        for kh in range(KH):
                            pe.matmul(bank(3 + 2 * i.par + t)[:, 0:D], h[:, kh, t * P:(t + 1) * P], l2_w[:, kh, :],
                                      start=kh == 0, stop=False)
                if b.ok:
                    pe.wait_ge(*s.gT(b))
                    pe.matmul(bank(2)[:, 0:T], l2_sel[:, :], rt_gT[:, :], start=True, stop=True).then_inc(s.wx_ps.sem, 1)
                ahead(ln_transpose, pe, pl, i, 1)
                if b.ok:
                    pe.wait_ge(*s.ax(b))
                    for t in range(TT):
                        last_ = pe.matmul(bank(3 + 2 * b.par + t)[:, 0:D], l2_ax[b.par][:, t * P:(t + 1) * P], l2_lb[:, :],
                                          start=False, stop=True)
                    last_.then_inc(s.y_ps.sem, 1)
                if i.ok:
                    for kh in range(KH):
                        last_ = pe.matmul(bank(1)[:, 0:T], l2_la[:, kh, :], h[:, kh, :], start=kh == 0, stop=kh == 1)
                    last_.then_inc(s.hfree.sem, 1)

            slots(pe, slot, -1, (4, 14), B)

        def l2f_scalar(act, pl, s):
            memory_free(act, pl)

            def slot(i):
                b = i - 1
                if b.ok:
                    gates_T_copy(act, pl, s, b, 2)
                if i.ok:
                    route_exp(act, pl, s, i)
                if b.ok:
                    act.wait_ge(*s.wx_ps(b))
                    if (b - 1).ok:
                        act.wait_ge(*s.ax(b - 1))
                    act.activation(l2_wx[:, :], bank(2)[:, 0:T], ACT.Copy, scale=LORA_SCALE).then_inc(s.wx.sem, 1)
                ahead(modulate, act, pl, i, 1)

            slots(act, slot, -1, (4, 14), B)

        def l2f_vector(dve, pl, s):
            memory_free(dve, pl)

            def slot(i):
                b = i - 1
                ahead(ln_apply, dve, pl, i, 1)
                if i.ok:
                    route(dve, pl, s, i)
                if b.ok:
                    dve.wait_ge(*s.wx(b))
                    dve.wait_ge(*s.hfree(b))
                    if (b - 2).ok:
                        dve.wait_ge(*s.y_ps(b - 2))
                    dve.tensor_tensor(l2_ax[b.par][:, :], bank(1)[:, 0:T], l2_wx[:, :], ALU.mult).then_inc(s.ax.sem, 1)
                ahead(ln_stats, dve, pl, i, 2)
                if b.ok:
                    dve.wait_ge(*s.y_ps(b))
                    gated(dve, pl, s, b, PS[:, 3 + 2 * b.par:5 + 2 * b.par, 0:D])

            slots(dve, slot, -2, (4, 14), B)

        def l3f_tensor(pe, pl, s):
            psum_free(pe, pl)
            pe.wait_ge(w_in[7], 16 * len(weights[7]))
            for kh in range(KH):
                pe.matmul(PS[0:NS, 7, 0:E], l3_sw[:, kh, :], l3_md[:, kh, :], start=kh == 0, stop=kh == 1)
            for kh in range(KH):
                last_ = pe.matmul(PS[0:NS + E, 7, 8:8 + E], l3_up[:, kh, :], l3_db[:, kh, :], start=kh == 0, stop=kh == 1)
            last_.then_inc(setup["f_ps"], 1)
            pe.wait_ge(setup["f_set"], 1)

            def slot(i):
                h = hT[i.par]
                if i.ok:
                    pe.wait_ge(*s.h(i))
                    if (i - 1).ok:
                        pe.wait_ge(*s.mx(i - 1))
                    for kh in range(KH):
                        pe.matmul(PS[0:NS, 1, 0:T], l3_sw[:, kh, :], h[:, kh, :], start=kh == 0, stop=kh == 1)
                    for kh in range(KH):
                        last_ = pe.matmul(PS[0:NS + E, 1, T:2 * T], l3_up[:, kh, :], h[:, kh, :], start=kh == 0, stop=kh == 1)
                    last_.then_inc(s.p_ps.sem, 1)
                if (i - 2).ok:
                    gates_T(pe, pl, s, i - 2, 6)
                if i.ok:
                    if (i - 1).ok:
                        pe.wait_ge(*s.ht(i - 1))
                    for t in range(TT):
                        for kh in range(KH):
                            last_ = pe.transpose(bank(2)[:, t * D + kh * P:t * D + (kh + 1) * P], h[:, kh, t * P:(t + 1) * P], ident[:, :])
                    last_.then_inc(s.htok_ps.sem, 1)
                ahead(ln_transpose, pe, pl, i, 1)
                if (i - 2).ok:
                    b = i - 2
                    pe.wait_ge(*s.gT(b))
                    if (b - 1).ok:
                        pe.wait_ge(*s.zz(b - 1))
                    pe.matmul(PS[0:NS + E, 7, 0:T], l3_e72[:, :], rt_gT[:, :], start=True, stop=True).then_inc(s.se_ps.sem, 1)
                if (i - 1).ok:
                    b = i - 1
                    pe.wait_ge(*s.z(b))
                    if (b - 1).ok:
                        pe.wait_ge(*s.ed(b - 1))
                    for t in range(TT):
                        last_ = pe.matmul(bank(5)[:, t * E:(t + 1) * E], l3_z[:, t * P:(t + 1) * P], ident[0:E, 0:E],
                                          start=True, stop=True)
                    last_.then_inc(s.zT_ps.sem, 1)
                if (i - 2).ok:
                    b = i - 2
                    pe.wait_ge(*s.zz(b))
                    if (b - 1).ok:
                        pe.wait_ge(*s.y1(b - 1))
                    for t in range(TT):
                        last_ = pe.matmul(bank(4)[:, t * D:(t + 1) * D], l3_zz[:, t * P:(t + 1) * P], l3_dg[:, :],
                                          start=True, stop=True)
                    last_.then_inc(s.y_ps.sem, 1)
                if i.ok:
                    pe.wait_ge(*s.sq(i))
                    if (i - 1).ok:
                        pe.wait_ge(*s.z(i - 1))
                    pe.matmul(PS[0:E, 3, 0:T], l3_blk[:, :], l3_sq[:, :], start=True, stop=True)
                    for kh in range(KH):
                        pe.matmul(PS[0:E, 3, T:2 * T], l3_one[:, :], l3_hsq[:, kh, :], start=kh == 0, stop=False)
                    for kh in range(KH):
                        last_ = pe.matmul(PS[0:E, 3, T:2 * T], l3_m2[:, kh, :], h[:, kh, :], start=False, stop=kh == 1)
                    last_.then_inc(s.hfree.sem, 1)

            slots(pe, slot, -1, (4, 14), B + 1)

        def l3f_scalar(act, pl, s):
            memory_free(act, pl)
            act.wait_ge(setup["f_set"], 1)

            def slot(i):
                if i.ok:
                    act.wait_ge(*s.h(i))
                    if (i - 1).ok:
                        act.wait_ge(*s.hfree(i - 1))
                    act.activation(l3_hsq[:, :, :], hT[i.par][:, :, :], ACT.Square)
                    act.wait_ge(*s.p_ps(i))
                    act.activation(l3_sq[0:NS, :], PS[0:NS, 1, 0:T], ACT.Square, bias=l3_c1[:, 0:1]).then_inc(s.sq.sem, 1)
                if (i - 2).ok:
                    gates_T_copy(act, pl, s, i - 2, 6)
                if (i - 1).ok:
                    route_exp(act, pl, s, i - 1)
                if i.ok:
                    if (i - 2).ok:
                        act.wait_ge(*s.zz(i - 2))
                    act.activation(l3_mx[i.par][:, :], PS[0:NS + E, 1, T:2 * T], ACT.Identity, bias=l3_c0[:, 0:1])\
                       .then_inc(s.mx.sem, 1)
                ahead(modulate, act, pl, i, 1)
                if i.ok:
                    act.wait_ge(*s.htok_ps(i))
                    if (i - 2).ok:
                        act.wait_ge(*s.y1(i - 2))
                    act.activation(l3_ht[i.par][:, :, :].rearrange("p t d -> p (t d)"), bank(2), ACT.Copy).then_inc(s.ht.sem, 1)

            slots(act, slot, -1, (4, 14), B + 1)

        def l3f_vector(dve, pl, s):
            memory_free(dve, pl)
            dve.wait_ge(w_in[7], 16 * len(weights[7]))
            dve.wait_ge(setup["f_ps"], 1)
            f = setup["f_step"]
            dve.memset(l3_sq[NS:P, :], 0.0)
            dve.tensor_tensor(l3_g1[:, :], PS[0:NS, 7, 0:E], l3_blk[0:NS, :], ALU.mult)
            dve.tensor_tensor(l3_g0[:, :], PS[0:NS + E, 7, 8:8 + E], l3_own[:, :], ALU.mult)
            dve.tensor_tensor(l3_mdsq[:, :], l3_mdr[:, :], l3_mdr[:, :], ALU.mult)
            dve.tensor_scalar(l3_m2[:, :, :], l3_md[:, :, :], -2.0, None, ALU.mult).then_inc(f, 1)
            dve.wait_ge(f, 1)
            dve.tensor_reduce(l3_c1[:, :], l3_g1[:, :], AX.X, ALU.add, negate=True)
            dve.tensor_reduce(l3_c0[:, :], l3_g0[:, :], AX.X, ALU.add, negate=True)
            dve.tensor_reduce(l3_md2[:, :], l3_mdsq[:, :], AX.X, ALU.add).then_inc(f, 1)
            dve.wait_ge(f, 2)
            dve.tensor_tensor(l3_c0[:, :], l3_c0[:, :], l3_tail[:, :], ALU.add).then_inc(setup["f_set"], 1)
            dve.wait_ge(setup["f_set"], 1)

            def slot(i):
                ahead(ln_apply, dve, pl, i, 1)
                if (i - 1).ok:
                    b = i - 1
                    dve.wait_ge(*s.hfree(b))
                    dve.tensor_scalar(l3_n[:, :], PS[0:E, 3, T:2 * T], l3_md2[:, 0:1], None, ALU.add).then_inc(s.zr.sem, 1)
                    dve.wait_ge(*s.zr(b, 1))
                    dve.reciprocal(l3_n[:, :], l3_n[:, :]).then_inc(s.zr.sem, 1)
                    dve.wait_ge(*s.zr(b, 2))
                    dve.tensor_tensor(l3_n[:, :], l3_n[:, :], PS[0:E, 3, 0:T], ALU.mult).then_inc(s.zr.sem, 1)
                    dve.wait_ge(*s.zr(b, 3))
                    if (b - 1).ok:
                        dve.wait_ge(*s.zT_ps(b - 1))
                    dve.tensor_scalar(l3_z[:, :], l3_n[:, :], l3_cs[:, 0:1], l3_cs[:, 1:2], ALU.subtract, ALU.mult).then_inc(s.z.sem, 1)
                if (i - 1).ok:
                    b = i - 1
                    dve.wait_ge(*s.zT_ps(b))
                    if (b - 1).ok:
                        dve.wait_ge(*s.e(b - 1))
                    dve.tensor_scalar(l3_ez[:, :, :].rearrange("p t e -> p (t e)"), bank(5)[:, 0:TT * E], -1.0, 88.0,
                                      ALU.mult, ALU.min).then_inc(s.ed.sem, 1)
                if (i - 2).ok:
                    b = i - 2
                    dve.wait_ge(*s.se_ps(b))
                    if (b - 1).ok:
                        dve.wait_ge(*s.y_ps(b - 1))
                    dve.tensor_tensor(l3_zz[:, :], PS[0:NS + E, 7, 0:T], l3_mx[b.par][:, :], ALU.mult).then_inc(s.zz.sem, 1)
                if (i - 1).ok:
                    b = i - 1
                    n = [0]

                    def link(ins):
                        n[0] += 1
                        ins.then_inc(s.tk.sem, 1)
                        dve.wait_ge(*s.tk(b, n[0]))

                    dve.wait_ge(*s.e(b))
                    link(dve.tensor_scalar(l3_ee[:, :, :], l3_ee[:, :, :], 1.0, None, ALU.add))
                    link(dve.reciprocal(rt_l[:, :, :], l3_ee[:, :, :]))
                    first_of(dve, link, rt_l[:, :, :], rt_m[:, 0, :], rt_o[:, 0])
                    dve.tensor_scalar(l3_oms[b.par][:, :], rt_m[:, 0, :], -1.0, 1.0, ALU.mult, ALU.add).then_inc(s.oms.sem, 1)
                    dve.tensor_tensor(rt_g[b.par][:, :, :], rt_o[:, 0], rt_m[:, 0, :].unsqueeze(2).broadcast_to([P, TT, E]),
                                      ALU.mult).then_inc(s.g.sem, 1)
                if (i - 2).ok:
                    b = i - 2
                    dve.wait_ge(*s.y_ps(b))
                    if (b - 1).ok:
                        dve.wait_ge(*s.y(b - 1))
                    for t in range(TT):
                        dve.scalar_tensor_tensor(l3_y1[:, t, :], l3_ht[b.par][:, t, :], l3_oms[b.par][:, t:t + 1],
                                                 bank(4)[:, t * D:(t + 1) * D], ALU.mult, ALU.add).then_inc(s.y1.sem, 1)
                ahead(ln_stats, dve, pl, i, 2)

            slots(dve, slot, -2, (4, 14), B + 1)

        def l3f_pool(pool, pl, s):
            memory_free(pool, pl)

            def slot(i):
                ahead(ln_rstd, pool, pl, i, 2)
                if (i - 2).ok:
                    gate_on_pool(pool, pl, s, i - 2, l3_y1[:, :, :], s.y1(i - 2))

            slots(pool, slot, -2, (4, 14), B + 1)

        LOOP2 = (4, 12)

        def stack_ready(b):
            v = 16 * N_STACK * (b.off // 2 + 1)
            return stack_in[b.par], v if b.reg is None else b.reg * (8 * N_STACK) + v

        def max_ready(b, half_):
            v = 16 * 6 * (2 * (b.off // 2) + half_ + 1)
            return max_in[b.par], v if b.reg is None else b.reg * (16 * 6) + v

        def scratch_ready(b):
            v = 16 * (b.off // 2 + 1)
            return scratch_in[b.par], v if b.reg is None else b.reg * 8 + v

        def l1a_tensor(pe, pl, s):
            psum_free(pe, pl)
            pe.wait_ge(w_in[2], 16 * len(weights[2]))
            pe.wait_ge(setup["a_wo"], 1)
            pe.wait_ge(setup["a_zero"], 4)

            def project(b, n, bk, done):
                if n == "k":
                    pe.wait_ge(*s.h(b))
                    if (b - 2).ok:
                        pe.wait_ge(*s.max(b - 2))
                    elif (b - 1).ok:
                        pe.wait_ge(*s.v(b - 1))
                for m in range(KH):
                    for kh in range(KH):
                        last_ = pe.matmul(bank(bk)[:, m * T:(m + 1) * T], l1_w[n][:, kh, m * P:(m + 1) * P],
                                          hT[b.par][:, kh, :], start=kh == 0, stop=kh == 1)
                last_.then_inc(done.sem, 1)

            def project_v(b, t):
                if t == 0:
                    pe.wait_ge(*(s.max(b - 1, 11) if (b - 1).ok else s.k(b)))
                for kh in range(KH):
                    last_ = pe.matmul(bank(2)[:, t * D:(t + 1) * D], hT[b.par][:, kh, t * P:(t + 1) * P],
                                      l1_w["v"][:, kh, :], start=kh == 0, stop=kh == 1)
                if t == TT - 1:
                    last_.then_inc(s.hfree.sem, 1)

            def q_of(b, h, q0, q1):
                return QS[b.par][:, h // 2, h % 2, q0:q1]

            def k_of(b, h, k0, k1):
                return KS[b.par][:, h // 2, k0:k1]

            def max_scores(b, gg):
                if gg == 0:
                    pe.wait_ge(*stack_ready(b))
                for n in range(3):
                    if gg:
                        pe.wait_ge(*s.max(b, 3 * gg + n - 2))
                    elif n and (b + 1).ok:
                        pe.wait_ge(*(s.k, s.q)[n - 1](b + 1))
                    elif (b - 1).ok:
                        pe.wait_ge(*s.max(b - 1, 22 + n))
                    if gg == 4 and n == 1 and (b + 1).ok:
                        pe.wait_ge(*s.v(b + 1))
                    if n == 0 and gg == 4:
                        pe.wait_ge(*s.mT(b, 1))
                    if n == 0 and gg == 0 and (b - 1).ok:
                        pe.wait_ge(*s.mT(b - 1, 2))
                    if n == 0:
                        pe.matmul(bank(1), ident_b[:, :], later4[:, :, :], start=True, stop=False)
                        for j in range(4):
                            h = 4 * gg + j
                            last_ = pe.matmul(bank(1)[:, j * P:(j + 1) * P], q_of(b, h, 0, P), k_of(b, h, 0, P), start=False, stop=j == 3)
                    else:
                        for j in range(2):
                            h = 4 * gg + 2 * (n - 1) + j
                            o = bank(1 + n)[:, j * T:(j + 1) * T]
                            pe.matmul(o, q_of(b, h, P, T), k_of(b, h, 0, T), start=True, stop=False)
                            last_ = pe.matmul(o[:, P:T], ident_b[:, :], later4[:, 0, :], start=False, stop=True)
                    last_.then_inc(s.max_ps.sem, 1)

            def max_T(b, half_):
                pe.wait_ge(*s.mparts(b, half_ + 1))
                pe.wait_ge(*s.max(b, 12 * half_ + 10))
                to = PS[:, 1, :].bitcast(BF16)
                for qt in range(TT):
                    last_ = pe.transpose(to[:, qt * P:(qt + 1) * P], mparts[half_][:, qt, :], ident_b[:, :])
                last_.then_inc(s.mT_ps.sem, 1)

            def exp_scores(b, gg):
                half_ = gg // 4
                for n in range(3):
                    if gg:
                        pe.wait_ge(*s.prob(b, 3 * gg + n - 2))
                    elif (b - 1).ok:
                        pe.wait_ge(*s.prob(b - 1, 22 + n))
                    if gg == 0 and (b - 1).ok:
                        pe.wait_ge(*s.u(b - 1, (4, 2, 3)[n]))
                    if n == 0 and gg == 4 and (b - 1).ok:
                        pe.wait_ge(*s.ogT(b - 1))
                        pe.wait_ge(*s.y(b - 1))
                    if n == 0 and gg % 4 == 0:
                        pe.wait_ge(*max_ready(b, half_))
                    if n < 2:
                        for j in range(2):
                            h = 4 * gg + 2 * n + j
                            o = bank(4 + n)[:, j * T:(j + 1) * T]
                            pe.matmul(o, k_of(b, h, 0, P), q_of(b, h, 0, T), start=True, stop=False)
                            last_ = pe.matmul(o[:, 0:P], ident_b[:, :], earlier4[:, 0, :], start=False, stop=True)
                    else:
                        pe.matmul(bank(6), ident_b[:, :], earlier4[:, :, :], start=True, stop=False)
                        for j in range(4):
                            h = 4 * gg + j
                            o = bank(6)[:, j * P:(j + 1) * P]
                            last_ = pe.matmul(o, k_of(b, h, P, T), q_of(b, h, P, T), start=False, stop=j == 3)
                    last_.then_inc(s.score.sem, 1)

            def values(b, gg):
                pe.wait_ge(*s.prob(b, 3 * gg + 3))
                if gg:
                    pe.wait_ge(*s.oT(b, gg))
                elif (b - 1).ok:
                    pe.wait_ge(*s.oT(b - 1))
                at = gg % 2 * T
                for kt in range(TT):
                    for j in range(4):
                        v = l1_vpad[b.par][:, kt, 2 * gg + j // 2, :]
                        o = PS[32 * j:32 * j + 32, 7, at:at + T]
                        if kt == 0:
                            pe.matmul(o, v, pw[gg % 2][j // 2][:, j % 2, :], start=True, stop=False)
                        else:
                            last_ = pe.matmul(o[:, P:T], v, pz[gg % 2][:, j, :], start=False, stop=True)
                last_.then_inc(s.pv.sem, 1)

            def by_token(b):
                pe.wait_ge(*s.oT(b))
                for n in range(4):
                    if n == 3:
                        pe.wait_ge(*s.u(b, 1))
                    qt, gh = n // 2, n % 2
                    for g in range(4):
                        last_ = pe.transpose(bank(4 + n % 3)[:, g * P:(g + 1) * P], l1_oT[:, 4 * gh + g, qt * P:(qt + 1) * P], ident[:, :])
                    last_.then_inc(s.otok_ps.sem, 1)

            def normed_T(b):
                pe.wait_ge(*s.og(b))
                if (b + 1).ok:
                    pe.wait_ge(*s.prob(b + 1, 12))
                for kh in range(KH):
                    for t in range(TT):
                        last_ = pe.transpose(bank(4)[:, kh * T + t * P:kh * T + (t + 1) * P],
                                             l1_og[:, t, kh * P:(kh + 1) * P], ident[:, :])
                last_.then_inc(s.ogT_ps.sem, 1)

            def out(b):
                pe.wait_ge(*s.ogT(b))
                for t in range(TT):
                    for kh in range(KH):
                        last_ = pe.matmul(bank(5)[:, t * D:(t + 1) * D], l1_ogT[:, kh, t * P:(t + 1) * P],
                                          l1_w["o"][:, kh, :], start=kh == 0, stop=kh == 1)
                last_.then_inc(s.y_ps.sem, 1)

            def slot(i):
                if (i + 1).ok:
                    project(i + 1, "k", 2, s.k_ps)
                    project(i + 1, "q", 3, s.q_ps)
                for k in range(4):
                    if k and i.ok:
                        max_scores(i, k)
                    if (i - 1).ok:
                        exp_scores(i - 1, 4 + k)
                    if k == 0 and i.ok:
                        max_scores(i, k)
                    if k and (i - 1).ok:
                        values(i - 1, 3 + k)
                if (i + 1).ok:
                    project_v(i + 1, 0)
                if i.ok:
                    max_T(i, 0)
                if (i - 1).ok:
                    values(i - 1, 7)
                if (i + 1).ok:
                    project_v(i + 1, 1)
                if (i - 1).ok:
                    by_token(i - 1)
                for k in range(4):
                    if i.ok:
                        max_scores(i, 4 + k)
                        exp_scores(i, k)
                        if k:
                            values(i, k - 1)
                if i.ok:
                    values(i, 3)
                if (i - 1).ok:
                    normed_T(i - 1)
                ahead(ln_transpose, pe, pl, i, 2)
                if i.ok:
                    max_T(i, 1)
                if (i - 1).ok:
                    out(i - 1)

            slots(pe, slot, -2, LOOP2, B)

        def l1a_scalar(act, pl, s):
            memory_free(act, pl)
            act.wait_ge(setup["a_dot"], 1)
            act.activation(lam[:, 0:2], lam[:, 0:2], ACT.Exp).then_inc(setup["a_exp"], 1)

            def copy_maxT(b, half_):
                act.wait_ge(*s.mT_ps(b, half_ + 1))
                if (b - 1).ok:
                    act.wait_ge(*max_ready(b - 1, half_))
                act.activation(maxT[half_][:, :], PS[0:48, 1, :].bitcast(BF16)[:, 0:T], ACT.Copy).then_inc(s.mT.sem, 1)

            def exps(b, gg):
                for n in range(3):
                    act.wait_ge(*s.score(b, 3 * gg + n + 1))
                    if n == 0:
                        if gg >= 2:
                            act.wait_ge(*s.pv(b, gg - 1))
                        elif (b - 1).ok:
                            act.wait_ge(*s.pv(b - 1, gg + 7))
                    to = pw[gg % 2][n][:, :, :] if n < 2 else pz[gg % 2][:, :, :]
                    act.activation(to.rearrange("p a n -> p (a n)"), bank(4 + n), ACT.Exp).then_inc(s.prob.sem, 1)

            def copy_oT(b, gg):
                act.wait_ge(*s.pv(b, gg + 1))
                if (b - 1).ok and gg == 0:
                    act.wait_ge(*s.otok_ps(b - 1))
                act.activation(l1_oT[:, gg, :], bank(7)[:, gg % 2 * T:(gg % 2 + 1) * T], ACT.Copy).then_inc(s.oT.sem, 1)

            def slot(i):
                if (i + 1).ok:
                    for n, ps, done, scale in ((1, s.k_ps, s.k, 1.0), (0, s.q_ps, s.q, QK_SCALE)):
                        act.wait_ge(*ps(i + 1))
                        if n == 1 and i.ok:
                            act.wait_ge(*s.split(i, 1))
                        if n == 1 and (i - 1).ok:
                            act.wait_ge(*scratch_ready(i - 1))
                        act.activation(qk32[:, n, :], bank(3 - n), ACT.Copy, scale=scale)
                        act.activation(qk_parts[(i + 1).par][:, 0, n, :], bank(3 - n), ACT.Copy, scale=scale).then_inc(done.sem, 1)
                for k in range(4):
                    if (i - 1).ok:
                        exps(i - 1, 4 + k)
                        if k:
                            copy_oT(i - 1, 3 + k)
                if i.ok:
                    copy_maxT(i, 0)
                if (i - 1).ok:
                    copy_oT(i - 1, 7)
                if (i + 1).ok:
                    act.wait_ge(*s.hfree(i + 1))
                    act.activation(l1_vpad[(i + 1).par][:, :, :, 0:HD].rearrange("p t h e -> p (t h) e"),
                                   bank(2).rearrange("p (t e) -> p t e", e=HD), ACT.Copy).then_inc(s.v.sem, 1)
                if i.ok:
                    for k in range(4):
                        exps(i, k)
                        if k:
                            copy_oT(i, k - 1)
                    copy_oT(i, 3)
                if (i - 1).ok:
                    act.wait_ge(*s.ogT_ps(i - 1))
                    act.activation(l1_ogT[:, :, :].rearrange("p k t -> p (k t)"), bank(4), ACT.Copy).then_inc(s.ogT.sem, 1)
                if i.ok:
                    copy_maxT(i, 1)
                ahead(modulate, act, pl, i, 2)

            slots(act, slot, -2, LOOP2, B)

        def l1a_vector(dve, pl, s):
            memory_free(dve, pl)
            dve.wait_ge(w_in[2], 16 * len(weights[2]))
            dve.tensor_tensor(lam_p[:, :, :], lam_v[:, :, 0, :], lam_v[:, :, 1, :], ALU.mult)
            dve.tensor_scalar(l1_w["o"][:, :, :], l1_w["o"][:, :, :], (1 - LAMBDA_INIT) * HD ** 0.5, None, ALU.mult)\
               .then_inc(setup["a_wo"], 1)
            dve.wait_ge(setup["a_wo"], 1)
            dve.tensor_reduce(lam[:, 0:2], lam_p[:, :, :], AX.X, ALU.add).then_inc(setup["a_dot"], 1)
            dve.wait_ge(setup["a_exp"], 1)
            dve.scalar_tensor_tensor(lam[:, 2:3], lam[:, 1:2], LAMBDA_INIT, lam[:, 0:1], ALU.subtract, ALU.subtract)\
               .then_inc(setup["a_lam"], 1)
            dve.wait_ge(setup["a_lam"], 1)

            def maxima(b, gg):
                for n in range(3):
                    dve.wait_ge(*s.max_ps(b, 3 * gg + n + 1))
                    if n == 0:
                        to, src = negmax[b.par][:, 0, 4 * gg:4 * gg + 4], bank(1).rearrange("p (j k) -> p j k", j=4)
                    else:
                        h = 4 * gg + 2 * (n - 1)
                        to, src = negmax[b.par][:, 1, h:h + 2], bank(1 + n).rearrange("p (j k) -> p j k", j=2)
                    dve.tensor_reduce(to, src, AX.X, ALU.max, negate=True).then_inc(s.max.sem, 1)

            def by_token(b):
                for n in range(4):
                    qt, gh = n // 2, n % 2
                    dve.wait_ge(*s.otok_ps(b, n + 1))
                    o = bank(4 + n % 3).rearrange("p (h e) -> p h e", e=32)
                    rl_ = l1_rl[:, qt, 16 * gh:16 * gh + 16]
                    dve.reciprocal(rl_, o[:, :, HD]).then_inc(s.rl.sem, 1)
                    dve.wait_ge(*s.rl(b, n + 1))
                    dve.tensor_tensor(l1_t[:, qt, 16 * gh:16 * gh + 16, :], o[:, :, 0:HD],
                                      rl_.unsqueeze(2).broadcast_to([P, 16, HD]), ALU.mult).then_inc(s.u.sem, 1)

            def subtract(b):
                dve.wait_ge(*s.u(b))
                pair = l1_t[:, :, :, :].rearrange("p q (h two) e -> p (q h) two e", two=2)
                dve.scalar_tensor_tensor(l1_att[:, :, :], pair[:, :, 1, :], lam[:, 2:3], pair[:, :, 0, :], ALU.mult, ALU.add)\
                   .then_inc(s.att.sem, 1)

            def slot(i):
                ahead(ln_stats, dve, pl, i, 3)
                for k in range(8):
                    if k == 4 and (i - 1).ok:
                        by_token(i - 1)
                    if i.ok:
                        maxima(i, k)
                    if k == 3:
                        ahead(ln_apply, dve, pl, i, 2)
                    if (i - 1).ok:
                        b = i - 1
                        if k == 4:
                            subtract(b)
                        if k == 5:
                            dve.wait_ge(*s.sq(b))
                            dve.tensor_reduce(l1_ms[:, :], l1_sq[:, :, :], AX.X, ALU.add).then_inc(s.ms.sem, 1)
                        if k == 7:
                            dve.wait_ge(*s.rn(b))
                            dve.tensor_tensor(l1_og[:, :, :].rearrange("p t (h e) -> p (t h) e", e=HD), l1_att[:, :, :],
                                              l1_ms[:, :].unsqueeze(2).broadcast_to([P, TT * HEADS, HD]), ALU.mult)\
                               .then_inc(s.og.sem, 1)
                if (i - 1).ok:
                    dve.wait_ge(*s.y_ps(i - 1))
                    gated(dve, pl, s, i - 1, bank(5).rearrange("p (t d) -> p t d", t=TT))

            slots(dve, slot, -3, LOOP2, B)

        def l1a_pads(pool, n):
            if n < 2:
                pool.memset(QS[n][:, :, :, :].bitcast(F32), 0.0).then_inc(setup["a_zero"], 1)
            elif n == 2:
                for i in range(2):
                    pool.memset(KS[i][:, :, :], 1.0)
                    last_ = pool.memset(mparts[i][:, :, :].bitcast(F32), 0.0)
                last_.then_inc(setup["a_zero"], 1)
            else:
                for i in range(2):
                    last_ = pool.memset(l1_vpad[i][:, :, :, :], 0.0)
                last_.then_inc(setup["a_zero"], 1)
                pool.wait_ge(setup["a_zero"], 4)
                for i in range(2):
                    last_ = pool.memset(l1_vpad[i][:, :, :, HD:HD + 1], 1.0)
                last_.then_inc(setup["a_one"], 1)

        def l1a_pool(pool, pl, s):
            memory_free(pool, pl)
            if pl == 0:
                for n in range(4):
                    l1a_pads(pool, n)

            def split_qk(b):
                pool.wait_ge(*s.q(b))
                pool.wait_ge(*s.k(b))
                pool.tensor_tensor(qk_rest[:, :, :], qk32[:, :, :], qk_parts[b.par][:, 0, :, :], ALU.subtract).then_inc(s.split.sem, 1)
                pool.wait_ge(*s.split(b, 1))
                pool.tensor_tensor(qk_parts[b.par][:, 1, :, :], qk_rest[:, :, :], zero[:, :].unsqueeze(1).broadcast_to([P, 2, KH * T]), ALU.add).then_inc(s.split.sem, 1)
                pool.wait_ge(*s.split(b, 2))
                pool.tensor_tensor(qk_parts[b.par][:, 2, :, :], qk_rest[:, :, :], qk_parts[b.par][:, 1, :, :], ALU.subtract)\
                    .then_inc(s.parts.sem, 1)

            def split_max(b, half_):
                m = negmax[b.par][:, :, 16 * half_:16 * half_ + 16].rearrange("p t (j r) -> p t r j", r=2)
                part = lambda n: mparts[half_][:, :, 0:48].rearrange("p t (r a j) -> p t a r j", r=2, a=3)[:, :, n]
                rest = m_rest[:, :, :].rearrange("p t (r j) -> p t r j", r=2)
                nil = zero[:, :].unsqueeze(1).unsqueeze(1).broadcast_to([P, TT, 2, 8])
                pool.wait_ge(*s.max(b, 12 * half_ + 12))
                if not (b - 1).ok and half_ == 0:
                    pool.wait_ge(setup["a_zero"], 4)
                if (b - 1).ok:
                    pool.wait_ge(*s.mT_ps(b - 1, half_ + 1))
                pool.tensor_tensor(part(0), m, nil, ALU.add).then_inc(s.msplit.sem, 1)
                pool.wait_ge(*s.msplit(b, 3 * half_ + 1))
                pool.tensor_tensor(rest, m, part(0), ALU.subtract).then_inc(s.msplit.sem, 1)
                pool.wait_ge(*s.msplit(b, 3 * half_ + 2))
                pool.tensor_tensor(part(1), rest, nil, ALU.add).then_inc(s.msplit.sem, 1)
                pool.wait_ge(*s.msplit(b, 3 * half_ + 3))
                pool.tensor_tensor(part(2), rest, part(1), ALU.subtract).then_inc(s.mparts.sem, 1)

            def slot(i):
                ahead(ln_rstd, pool, pl, i, 3)
                if (i + 1).ok:
                    split_qk(i + 1)
                if i.ok:
                    split_max(i, 0)
                if (i - 1).ok:
                    b = i - 1
                    pool.wait_ge(*s.att(b))
                    pool.tensor_tensor(l1_sq[:, :, :], l1_att[:, :, :], l1_att[:, :, :], ALU.mult).then_inc(s.sq.sem, 1)
                    pool.wait_ge(*s.ms(b))
                    pool.tensor_tensor(l1_ms[:, :], l1_ms[:, :], eps_sum1[:, 0:TT * HEADS], ALU.add).then_inc(s.rn_raw.sem, 1)
                    pool.wait_ge(*s.rn_raw(b))
                    pool.tensor_tensor(l1_ms[:, :], l1_ms[:, :], half[:, 0:TT * HEADS], ALU.pow).then_inc(s.rn.sem, 1)
                if i.ok:
                    split_max(i, 1)
                if (i - 1).ok:
                    add_to_x(pool, pl, s, i - 1)

            slots(pool, slot, -3, LOOP2, B)

        Q_TERMS, K_TERMS = (0, 0, 0, 1, 1, 2), (0, 1, 2, 0, 1, 0)
        N_STACK = 2 * (2 * len(Q_TERMS) + 1)
        M_ROW = 8 * len(Q_TERMS)

        def l1a_sync(sp, pl, s, i):
            sp.wait_ge(*s.parts(i))
            sp.dma_start(qk_dram[i.par].rearrange("a c m p t -> p a c m t"),
                         qk_parts[i.par][:, :, :, :].rearrange("p a c (m t) -> p a c m t", m=KH)).then_inc(scratch_in[i.par], 16)

        def l1a_stack_sync(sp, pl, s, i):
            if i.reg is None and i.off == 0:
                sp.wait_ge(setup["a_zero"], 4)
            if (i - 2).ok:
                sp.wait_ge(*s.score(i - 2))
            if not (i - 1).ok:
                sp.wait_ge(*scratch_ready(i))
            for pr in range(2):
                for c, terms in ((0, Q_TERMS), (1, K_TERMS)):
                    for n, part in enumerate(terms):
                        src = qk_dram[i.par, part, c].rearrange("m (g r d) t -> r d (m g) t", g=8, r=2)[pr]
                        r0 = 64 * pr + 8 * n
                        to = QS[i.par][r0:r0 + 8, :, pr, :] if c == 0 else KS[i.par][r0:r0 + 8, :, :]
                        sp.dma_start(to, src).then_inc(stack_in[i.par], 16)
                r0 = 64 * pr + M_ROW
                sp.dma_start(QS[i.par][r0:r0 + 3, :, pr, :], ins["no_max"]).then_inc(stack_in[i.par], 16)

        def l1a_max_sync(sp, pl, s, b, half_):
            if not b.ok:
                return
            sp.wait_ge(*s.mT(b, half_ + 1))
            for pr in range(2):
                if pr == 1 and half_ == 0 and (b + 1).ok:
                    sp.wait_ge(*scratch_ready(b + 1))
                for part in range(3):
                    r0, r1 = 64 * pr + M_ROW + part, 24 * pr + 8 * part
                    sp.dma_start(QS[b.par][r0:r0 + 1, 8 * half_:8 * half_ + 8, pr, :], maxT[half_][r1:r1 + 8, :])\
                      .then_inc(max_in[b.par], 16)

        def l2a_tensor(pe, pl, s):
            psum_free(pe, pl)
            pe.wait_ge(w_in[4], 48)
            pe.wait_ge(l2_dd_set, 1)

            def slot(i):
                b = i
                if b.ok:
                    pe.wait_ge(*s.h(b))
                    if has(0, b - 1):
                        pe.wait_ge(*s.state(b - 1))
                    for kh in range(KH):
                        last_ = pe.matmul(PS[:, 1, 0:T], l2_b[:, kh, :], hT[b.par][:, kh, :], start=kh == 0, stop=kh == 1)
                    last_.then_inc(s.state_ps.sem, 1)
                ahead(ln_transpose, pe, pl, i, 1)
                if b.ok:
                    pe.wait_ge(*s.state(b))
                    if has(0, b - 2):
                        pe.wait_ge(*s.y(b - 2))
                    for t in range(TT):
                        o = PS[:, 2 + b.par, t * D:(t + 1) * D]
                        pe.matmul(o, l2_st[b.par][:, t * P:(t + 1) * P], l2_c[:, :], start=True, stop=False)
                        for kh in range(KH):
                            last_ = pe.matmul(o[:, kh * P:(kh + 1) * P], hT[b.par][:, kh, t * P:(t + 1) * P],
                                              l2_dd[:, kh, :], start=False, stop=kh == 1)
                    last_.then_inc(s.hfree.sem, 1)

            slots(pe, slot, -1, (2, 14), B - 1)

        def l2a_scalar(act, pl, s):
            memory_free(act, pl)

            def slot(i):
                if i.ok:
                    act.wait_ge(*s.state_ps(i))
                    if has(0, i - 2):
                        act.wait_ge(*s.hfree(i - 2))
                    act.activation(l2_st[i.par][:, :], PS[:, 1, 0:T], ACT.Tanh).then_inc(s.state.sem, 1)
                ahead(modulate, act, pl, i, 1)

            slots(act, slot, -1, (2, 14), B - 1)

        def l2a_vector(dve, pl, s):
            memory_free(dve, pl)
            dve.wait_ge(w_in[4], 48)
            for kh in range(KH):
                last_ = dve.tensor_scalar(l2_dd[:, kh, :], ident[:, :], l2_d[:, kh:kh + 1], None, ALU.mult)
            last_.then_inc(l2_dd_set, 1)

            def slot(i):
                ahead(ln_stats, dve, pl, i, 2)
                ahead(ln_apply, dve, pl, i, 1)
                if i.ok:
                    dve.wait_ge(*s.hfree(i))
                    gated(dve, pl, s, i, PS[:, 2 + i.par, :].rearrange("p (t d) -> p t d", t=TT))

            slots(dve, slot, -2, (2, 14), B - 1)

        def plain_pool(pool, pl, s):
            memory_free(pool, pl)

            def slot(i):
                ahead(ln_rstd, pool, pl, i, 2)
                if (i - 1).ok:
                    add_to_x(pool, pl, s, i - 1)

            slots(pool, slot, -2, (4, 14), B)

        tensor_of = {0: l0a_tensor, 1: l0f_tensor, 2: l1a_tensor, 3: l1f_tensor, 5: l2f_tensor, 7: l3f_tensor, 6: l3a_tensor, 4: l2a_tensor}
        scalar_of = {0: l0a_scalar, 1: l0f_scalar, 2: l1a_scalar, 3: l1f_scalar, 5: l2f_scalar, 7: l3f_scalar, 6: l3a_scalar, 4: l2a_scalar}
        vector_of = {0: l0a_vector, 1: l0f_vector, 2: l1a_vector, 3: l1f_vector, 5: l2f_vector, 7: l3f_vector, 6: l3a_vector, 4: l2a_vector}
        pool_of = {0: l0a_pool, 1: l0f_pool, 2: l1a_pool, 3: l1f_pool, 7: l3f_pool, 6: l3a_pool}
        consts = [(ident[:, :], ins["ident"]), (rank[:, :, :], ins["rank"]), (cT[:, :, :, :], ins["c"])]
        n_const = len(consts)
        rows = lambda x: x.partition_broadcast(P)
        weights = {0: [(l0_w[n][:, :, :], ins["l0_w" + n]) for n in "qkvo"] + [
            (l0_wg1[:, :, :], ins["l0_wg1"]), (l0_wg2[:, :], ins["l0_wg2"]), (l0_ld[:, :], rows(ins["l0_ld"])),
            (l0_ld_col[:, :], ins["l0_ld_col"]), (l0_ld_row[:, :], rows(ins["l0_ld_row"])), (l0_nw[:, :], ins["l0_nw"]),
            (l0_age[:, :], ins["l0_age"]), (causal[:, :], ins["causal"]), (count[:, :], ins["count"]), (left[:, :], ins["left"]),
            (l0_own[:, :], ins["l0_own"].rearrange("p k d -> p (k d)")),
            (l0_lut[:, :], rows(ins["l0_lut"])), (iota[:, :], rows(ins["iota"]))],
            1: [],
            2: [(l1_w[n][:, :, :], ins["l1_w" + n]) for n in "qkvo"] + [
                (lam_v[:, :, :, :], rows(ins["lam_v"])), (ident_b[:, :], ins["ident_b"]), (later4[:, :, :], ins["later4"]),
                (earlier4[:, :, :], ins["earlier4"])],
            3: [(l1_we[:, :, :, :], ins["l1_we"]), (l1_gw[:, :, :], ins["l1_gw"]), (l1_eb[:, :], ins["l1_eb"])],
            5: [(l2_la[:, :, :], ins["l2_la"]), (l2_w[:, :, :], ins["l2_w"]), (l2_rw[:, :, :], ins["l2_rw"]),
                (l2_lb[:, :], ins["l2_lb"]), (l2_sel[:, :], ins["l2_sel"])],
            7: [(l3_sw[:, :, :], ins["l3_sw"]), (l3_up[:, :, :], ins["l3_up"]), (l3_md[:, :, :], ins["l3_md"]),
                (l3_db[:, :, :], ins["l3_db"]), (l3_mdr[:, :], ins["l3_mdr"]), (l3_cs[:, :], ins["l3_cs"]), (l3_dg[:, :], ins["l3_dg"]),
                (l3_blk[:, :], ins["l3_blk"]), (l3_own[:, :], ins["l3_own"]), (l3_e72[:, :], ins["l3_e72"]),
                (l3_tail[:, :], ins["l3_tail"]), (l3_one[:, :], ins["l3_one"])],
            6: [(l3_wqkv[:, :, :], ins["l3_wqkv"]), (l3_wo[:, :, :], ins["l3_wo"]), (l3_same[:, :], ins["l3_same"]),
                (l3_dec[:, :], ins["l3_dec"])],
            4: [(l2_b[:, :, :], ins["l2_b"]), (l2_c[:, :], ins["l2_c"]), (l2_d[:, :], ins["l2_d"])]}

        @block.sync
        def _(sp):
            for to, src in consts:
                sp.dma_start(to, src).then_inc(const_in, 16)
            for i in range(2):
                sp.dma_start(wmod[i][:, :, :], ins["wmod"][i].rearrange("(k p) n -> p k n", p=P)).then_inc(wmod_in[i], 16)
            sp.dma_start(X[:, 0:4], ins["x"][0:4].rearrange("b t p d -> p b t d")).then_inc(x_in[0], 16)
            if first == 0:
                for to, src in weights[first]:
                    sp.dma_start(to, src).then_inc(w_in[first], 16)
            mod_sync(sp)
            if first:
                for to, src in weights[first]:
                    sp.dma_start(to, src).then_inc(w_in[first], 16)
            if first == 0:
                sp.dma_start(l0_idx[:, :], ins["l0_idx"]).then_inc(idx_in, 16)
            sp.dma_start(X[:, 4:B], ins["x"][4:B].rearrange("b t p d -> p b t d")).then_inc(x_in[1], 16)
            for p in range(first, last):
                pl = p - first
                if p == 0:
                    sp.wait_ge(setup["pads"], 1)

                def slot(i):
                    if p == 0:
                        l0a_sync(sp, pl, sigs[pl], i)
                    if i.ok:
                        gate_load(sp, pl, sigs[pl], i)
                    if i.reg is None and i.off == 1 and pl + 1 < len(sigs):
                        if pl:
                            sp.wait_ge(*sigs[pl - 1].x(Idx(None, B - 1)))
                        for to, src in weights[p + 1]:
                            sp.dma_start(to, src).then_inc(w_in[p + 1], 16)
                    if p == 2:
                        if (i + 1).ok:
                            l1a_sync(sp, pl, sigs[pl], i + 1)
                        l1a_max_sync(sp, pl, sigs[pl], i, 0)
                        if (i + 1).ok:
                            l1a_stack_sync(sp, pl, sigs[pl], i + 1)
                        l1a_max_sync(sp, pl, sigs[pl], i, 1)
                    if p == last - 1 and (i - 2).ok:
                        o = i - 2
                        sp.wait_ge(*sigs[pl].x(o))
                        sp.dma_start(y_out[bass.ds(o.n, 1)].rearrange("a (t p) d -> p (a t) d", p=P), xb(o)).then_inc(out_done, 16)

                slots(sp, slot, -1 if p == 2 else 0, (4, 14), B - 1)
            for o in (Idx(None, B - 2), Idx(None, B - 1)):
                sp.wait_ge(*sigs[-1].x(o))
                sp.dma_start(y_out[bass.ds(o.n, 1)].rearrange("a (t p) d -> p (a t) d", p=P), xb(o)).then_inc(out_done, 16)
            sp.wait_ge(out_done, 16 * B)

        @block.gpsimd
        def _(pool):
            pool.memset(eps[:, :], LN_EPS)
            pool.memset(zero[:, :], 0.0)
            pool.memset(eps_sum[:, :], 4 * HD * LN_EPS)
            pool.memset(eps_sum1[:, :], HD * LN_EPS)
            pool.memset(half[:, :], -0.5).then_inc(half_set, 1)
            if first == 0:
                l0a_pads(pool)
            pool.wait_ge(half_set, 1)
            for p in range(first, last):
                pool_of.get(p, plain_pool)(pool, p - first, sigs[p - first])

        @block.scalar
        def _(act):
            mod_scalar(act)
            act.wait_ge(M["col"], LAYERS)
            for p in range(first, last):
                scalar_of[p](act, p - first, sigs[p - first])

        @block.vector
        def _(dve):
            mod_vector(dve)
            for p in range(first, last):
                vector_of[p](dve, p - first, sigs[p - first])

        @block.tensor
        def _(pe):
            mod_tensor(pe)
            for p in range(first, last):
                tensor_of[p](pe, p - first, sigs[p - first])


def declare_and_build(nc, arrays, first=0, last=8):
    ins = {k[3:]: nc.dram_tensor(k, v.shape, mybir.dt.from_np(v.dtype), kind="ExternalInput").ap() for k, v in arrays.items()}
    out = nc.dram_tensor("y_out", (B, T, D), F32, kind="ExternalOutput").ap()
    build(nc, ins, out, first, last)


def kernel(**inputs):
    import concourse.bacc as _bacc
    from concourse.bass_utils import run_bass_kernel_spmd as _run

    arrays = layout(**inputs)
    nc = _bacc.Bacc("TRN2", target_bir_lowering=False, num_devices=1)
    declare_and_build(nc, arrays)
    r = _run(nc, [arrays], core_ids=[0])
    return r.results[0]["y_out"]
```
